# Optimizing a Trainium2 kernel written in Bass

```python
import numpy as np
import jax
import jax.numpy as jnp

def _softmax(x, axis=-1):
    return jax.nn.softmax(x, axis=axis)

def _gelu(x):
    return jax.nn.gelu(x, approximate=True)

def _silu(x):
    return jax.nn.silu(x)

def _sigmoid(x):
    return jax.nn.sigmoid(x)

def _layernorm(x, axis=-1, eps=1e-05):
    m = jnp.mean(x, axis=axis, keepdims=True)
    v = jnp.var(x, axis=axis, keepdims=True)
    return (x - m) / jnp.sqrt(v + eps)

def _scatter_add(tgt, idx, src, axis=0):
    return tgt.at[idx].add(src)

def _segment_sum(src, seg, n):
    return jax.ops.segment_sum(src, seg, n)
kernel_name = 'mk_xattn_ffn_d2_seqx_r2_b4495b'

def setup_inputs(seed: int=0):
    np.random.seed(seed)
    _w = jnp.asarray

    def _rec_inputs():
        import jax
        import jax.numpy as jnp
        _rk = jax.random.key(seed)
        x = -0.0002928 + 1 * jax.random.normal(jax.random.fold_in(_rk, 1), (8, 224, 512), jnp.float32)
        _lenS = 224 - jax.random.randint(jax.random.fold_in(_rk, 7), (8,), 0, max(1, 224 // 4) + 1, jnp.int32)
        _lenS2 = 750 - jax.random.randint(jax.random.fold_in(_rk, 8), (8,), 0, max(1, 750 // 4) + 1, jnp.int32)
        _ctx_1024P = jax.random.normal(jax.random.fold_in(_rk, 11), (8, 16, 512), jnp.float32)
        _ctx_1024c = jax.random.dirichlet(jax.random.fold_in(_rk, 511), 0.3 * jnp.ones((16,), jnp.float32), (8, 750))
        _ctx_1024t = jnp.einsum('bsk,bkd->bsd', _ctx_1024c, _ctx_1024P)
        _ctx_1024t = _ctx_1024t * jax.lax.rsqrt(jnp.mean(jnp.square(_ctx_1024t)) + 1e-12) * 0.953939
        ctx_1024 = -1.39393e-06 + 0.999914 * (_ctx_1024t + 0.3 * jax.random.normal(jax.random.fold_in(_rk, 611), (8, 750, 512), jnp.float32))
        _validS = jnp.arange(224)[None, :] < _lenS[:, None]
        _validS2 = jnp.arange(750)[None, :] < _lenS2[:, None]
        _causal = jnp.tril(jnp.ones((224, 224), dtype=bool))
        mask_BxSxS2_bf0 = jnp.logical_not(jnp.ones((8, 224, 750), dtype=bool))
        mask_BxS2_bf0 = jnp.logical_not(jnp.ones((8, 750), dtype=bool))
        return (x, ctx_1024, mask_BxSxS2_bf0, mask_BxS2_bf0)
    x, ctx_1024, mask_BxSxS2_bf0, mask_BxS2_bf0 = _rec_inputs()

    def _L0_xattn_setup():
        import jax, jax.numpy as jnp
        import numpy as np
        D_MODEL, NHEAD = (512, 16)
        D_K = D_MODEL // NHEAD
        key = jax.random.key(seed)
        ks = jax.random.split(key, 11)
        B, S = (2, 1024)
        xav = lambda k, shp: jax.random.uniform(k, shp, jnp.float32, -np.sqrt(6.0 / (shp[0] + shp[1])), np.sqrt(6.0 / (shp[0] + shp[1])))
        return {'query': jax.random.normal(ks[0], (B, S, D_MODEL), jnp.float32), 'key': jax.random.normal(ks[1], (B, S, D_MODEL), jnp.float32), 'value': jax.random.normal(ks[2], (B, S, D_MODEL), jnp.float32), 'attn_mask': jnp.zeros((B, S, S), dtype=bool), 'key_padding_mask': jnp.zeros((B, S), dtype=bool), 'Wq': xav(ks[3], (D_MODEL, D_MODEL)), 'bq': jnp.zeros((D_MODEL,), jnp.float32), 'Wk': xav(ks[4], (D_MODEL, D_MODEL)), 'bk': jnp.zeros((D_MODEL,), jnp.float32), 'Wv': xav(ks[5], (D_MODEL, D_MODEL)), 'bv': jnp.zeros((D_MODEL,), jnp.float32), 'Wo': xav(ks[6], (D_MODEL, D_MODEL)), 'bo': jnp.zeros((D_MODEL,), jnp.float32)}
    _L0_xattn_all = _L0_xattn_setup()
    _L0_xattn_in = {k: v for k, v in _L0_xattn_all.items() if k in ('Wq', 'bq', 'Wk', 'bk', 'Wv', 'bv', 'Wo', 'bo')}
    del _L0_xattn_all

    def _L0_ffn_setup():
        import jax, jax.numpy as jnp
        import numpy as np
        B, T, D, E, H = (8, 1024, 512, 8, 128)
        LN_EPS = 1e-05
        key = jax.random.key(seed)
        ks = jax.random.split(key, 4)
        return {'x': jax.random.normal(ks[0], (B, T, D), dtype=jnp.float32), 'Wg': jax.random.normal(ks[1], (E, D), dtype=jnp.float32) * 0.02, 'ln_scale': jnp.ones((E, D), dtype=jnp.float32), 'ln_bias': jnp.zeros((E, D), dtype=jnp.float32), 'W1': jax.random.normal(ks[2], (E, D, H), dtype=jnp.float32) * 0.02, 'b1': jnp.zeros((E, H), dtype=jnp.float32), 'W2': jax.random.normal(ks[3], (E, H, D), dtype=jnp.float32) * 0.02, 'b2': jnp.zeros((E, D), dtype=jnp.float32)}
    _L0_ffn_all = _L0_ffn_setup()
    _L0_ffn_in = {k: v for k, v in _L0_ffn_all.items() if k in ('Wg', 'ln_scale', 'ln_bias', 'W1', 'b1', 'W2', 'b2')}
    del _L0_ffn_all

    def _L1_xattn_setup():
        import jax, jax.numpy as jnp
        import numpy as np
        D, H = (512, 16)
        DH = D // H

        def _split_heads(z):
            b, t, _ = z.shape
            return z.reshape(b, t, H, DH).transpose(0, 2, 1, 3)
        key = jax.random.key(seed)
        ks = jax.random.split(key, 11)
        b, t, ta = (2, 1024, 750)
        s = 1.0 / np.sqrt(D)
        return {'x': jax.random.normal(ks[0], (b, t, D), dtype=jnp.float32), 'xa': jax.random.normal(ks[1], (b, ta, D), dtype=jnp.float32), 'Wqkv': jax.random.normal(ks[2], (D, 3 * D), dtype=jnp.float32) * s, 'bqkv': jax.random.normal(ks[3], (3 * D,), dtype=jnp.float32) * 0.01, 'Wqkv_aux': jax.random.normal(ks[4], (D, 3 * D), dtype=jnp.float32) * s, 'bqkv_aux': jax.random.normal(ks[5], (3 * D,), dtype=jnp.float32) * 0.01, 'Wo': jax.random.normal(ks[6], (D, D), dtype=jnp.float32) * s, 'bo': jax.random.normal(ks[7], (D,), dtype=jnp.float32) * 0.01, 'g': jnp.zeros((H,), dtype=jnp.float32)}
    _L1_xattn_all = _L1_xattn_setup()
    _L1_xattn_in = {k: v for k, v in _L1_xattn_all.items() if k in ('Wqkv', 'bqkv', 'Wqkv_aux', 'bqkv_aux', 'Wo', 'bo', 'g')}
    del _L1_xattn_all

    def _L1_ffn_setup():
        import jax, jax.numpy as jnp
        import numpy as np
        BLOCK = 32
        W_BITS = 4
        ACT_BITS = 16

        def act_qdq(x):
            qmax = 2.0 ** (ACT_BITS - 1) - 1.0
            scale = jnp.maximum(jnp.max(jnp.abs(x)) / qmax, 1e-12)
            return jnp.clip(jnp.round(x / scale), -qmax - 1.0, qmax) * scale

        def fixed_qdq_u16(x):
            scale = 1.0 / 65536.0
            return jnp.clip(jnp.round(x / scale), 0.0, 65535.0) * scale

        def lpbq_dequant(w):
            O, I = w.shape
            qmax = 2.0 ** (W_BITS - 1) - 1.0
            wb = w.reshape(O, I // BLOCK, BLOCK)
            s = jnp.maximum(jnp.max(jnp.abs(wb), axis=-1, keepdims=True) / qmax, 1e-12)
            wq = jnp.clip(jnp.round(wb / s), -qmax - 1.0, qmax) * s
            return wq.reshape(O, I)
        key = jax.random.key(seed)
        k1, k2, k3, k4 = jax.random.split(key, 4)
        B, S, H, I = (2, 2048, 512, 1536)
        x = jax.random.normal(k1, (B, S, H), jnp.float32)
        w_gate = jax.random.normal(k2, (I, H), jnp.float32) * 0.02
        w_up = jax.random.normal(k3, (I, H), jnp.float32) * 0.02
        w_down = jax.random.normal(k4, (H, I), jnp.float32) * 0.02
        return {'x': x, 'w_gate': w_gate, 'w_up': w_up, 'w_down': w_down}
    _L1_ffn_all = _L1_ffn_setup()
    _L1_ffn_in = {k: v for k, v in _L1_ffn_all.items() if k in ('w_gate', 'w_up', 'w_down')}
    del _L1_ffn_all
    return {'x': x, 'ctx_1024': ctx_1024, 'mask_BxSxS2_bf0': mask_BxSxS2_bf0, 'mask_BxS2_bf0': mask_BxS2_bf0, 'L0_xattn_Wq': _L0_xattn_in['Wq'], 'L0_xattn_bq': _L0_xattn_in['bq'], 'L0_xattn_Wk': _L0_xattn_in['Wk'], 'L0_xattn_bk': _L0_xattn_in['bk'], 'L0_xattn_Wv': _L0_xattn_in['Wv'], 'L0_xattn_bv': _L0_xattn_in['bv'], 'L0_xattn_Wo': _L0_xattn_in['Wo'], 'L0_xattn_bo': _L0_xattn_in['bo'], 'L0_ffn_Wg': _L0_ffn_in['Wg'], 'L0_ffn_ln_scale': _L0_ffn_in['ln_scale'], 'L0_ffn_ln_bias': _L0_ffn_in['ln_bias'], 'L0_ffn_W1': _L0_ffn_in['W1'], 'L0_ffn_b1': _L0_ffn_in['b1'], 'L0_ffn_W2': _L0_ffn_in['W2'], 'L0_ffn_b2': _L0_ffn_in['b2'], 'L1_xattn_Wqkv': _L1_xattn_in['Wqkv'], 'L1_xattn_bqkv': _L1_xattn_in['bqkv'], 'L1_xattn_Wqkv_aux': _L1_xattn_in['Wqkv_aux'], 'L1_xattn_bqkv_aux': _L1_xattn_in['bqkv_aux'], 'L1_xattn_Wo': _L1_xattn_in['Wo'], 'L1_xattn_bo': _L1_xattn_in['bo'], 'L1_xattn_g': _L1_xattn_in['g'], 'L1_ffn_w_gate': _L1_ffn_in['w_gate'], 'L1_ffn_w_up': _L1_ffn_in['w_up'], 'L1_ffn_w_down': _L1_ffn_in['w_down']}

def reference(x, ctx_1024, mask_BxSxS2_bf0, mask_BxS2_bf0, L0_xattn_Wq, L0_xattn_bq, L0_xattn_Wk, L0_xattn_bk, L0_xattn_Wv, L0_xattn_bv, L0_xattn_Wo, L0_xattn_bo, L0_ffn_Wg, L0_ffn_ln_scale, L0_ffn_ln_bias, L0_ffn_W1, L0_ffn_b1, L0_ffn_W2, L0_ffn_b2, L1_xattn_Wqkv, L1_xattn_bqkv, L1_xattn_Wqkv_aux, L1_xattn_bqkv_aux, L1_xattn_Wo, L1_xattn_bo, L1_xattn_g, L1_ffn_w_gate, L1_ffn_w_up, L1_ffn_w_down):
    import jax
    import jax.numpy as jnp

    def _L0_xattn_ref(query, key, value, attn_mask, key_padding_mask, Wq, bq, Wk, bk, Wv, bv, Wo, bo):
        import jax, jax.numpy as jnp
        import numpy as np
        D_MODEL, NHEAD = (512, 16)
        D_K = D_MODEL // NHEAD
        B = query.shape[0]

        def proj(x, W, b):
            y = x @ W.T + b
            return y.reshape(B, -1, NHEAD, D_K).transpose(0, 2, 1, 3)
        q = proj(query, Wq, bq)
        k = proj(key, Wk, bk)
        v = proj(value, Wv, bv)
        scores = jnp.einsum('bhqd,bhkd->bhqk', q, k) / jnp.sqrt(jnp.float32(D_K))
        neg_inf = jnp.float32(-jnp.inf)
        scores = jnp.where(attn_mask[:, None, :, :], neg_inf, scores)
        scores = jnp.where(key_padding_mask[:, None, None, :], neg_inf, scores)
        p = jax.nn.softmax(scores, axis=-1)
        p = jnp.where(jnp.isnan(p), jnp.zeros_like(p), p)
        x = jnp.einsum('bhqk,bhkd->bhqd', p, v)
        x = x.transpose(0, 2, 1, 3).reshape(B, -1, D_MODEL)
        return x @ Wo.T + bo

    def _L0_ffn_ref(x, Wg, ln_scale, ln_bias, W1, b1, W2, b2):
        import jax, jax.numpy as jnp
        import numpy as np
        B, T, D, E, H = (8, 1024, 512, 8, 128)
        LN_EPS = 1e-05
        Bs, Ts, Ds = x.shape
        xt = x.reshape(Bs * Ts, Ds)
        logits = xt @ Wg.T
        top1 = jnp.argmax(logits, axis=-1)
        mu = jnp.mean(xt, axis=-1, keepdims=True)
        var = jnp.mean(jnp.square(xt - mu), axis=-1, keepdims=True)
        xhat = (xt - mu) * jax.lax.rsqrt(var + LN_EPS)
        n_experts = Wg.shape[0]

        def body(y, p):
            s_e, b_e, w1, bb1, w2, bb2, eid = p
            h = jax.nn.gelu((xhat * s_e + b_e) @ w1 + bb1, approximate=False)
            out = h @ w2 + bb2
            mask = (top1 == eid)[:, None].astype(out.dtype)
            return (y + mask * out, None)
        y0 = jnp.zeros_like(xt)
        y, _ = jax.lax.scan(body, y0, (ln_scale, ln_bias, W1, b1, W2, b2, jnp.arange(n_experts)))
        return y.reshape(Bs, Ts, Ds)

    def _L1_xattn_ref(x, xa, Wqkv, bqkv, Wqkv_aux, bqkv_aux, Wo, bo, g):
        import jax, jax.numpy as jnp
        import numpy as np
        D, H = (512, 16)
        DH = D // H

        def _split_heads(z):
            b, t, _ = z.shape
            return z.reshape(b, t, H, DH).transpose(0, 2, 1, 3)
        qkv = x @ Wqkv + bqkv
        qkv_a = xa @ Wqkv_aux + bqkv_aux
        q, k, v = (_split_heads(c) for c in jnp.split(qkv, 3, axis=-1))
        qa, ka, va = (_split_heads(c) for c in jnp.split(qkv_a, 3, axis=-1))
        scale = 1.0 / jnp.sqrt(jnp.float32(DH))
        dots = jnp.einsum('bhqd,bhkd->bhqk', q, k) * scale
        dots_aux = jnp.einsum('bhqd,bhkd->bhqk', q, ka) * scale
        p = jax.nn.softmax(dots, axis=-1)
        pa = jax.nn.softmax(dots_aux, axis=-1)
        h_main = jnp.einsum('bhqk,bhkd->bhqd', p, v)
        h_aux = jnp.einsum('bhqk,bhkd->bhqd', pa, va)
        gate = jax.nn.sigmoid(g).reshape(1, H, 1, 1)
        out = h_main * (1.0 - gate) + h_aux * gate
        b, _, t, _ = out.shape
        out = out.transpose(0, 2, 1, 3).reshape(b, t, H * DH)
        return out @ Wo + bo

    def _L1_ffn_ref(x, w_gate, w_up, w_down):
        import jax, jax.numpy as jnp
        import numpy as np
        BLOCK = 32
        W_BITS = 4
        ACT_BITS = 16

        def act_qdq(x):
            qmax = 2.0 ** (ACT_BITS - 1) - 1.0
            scale = jnp.maximum(jnp.max(jnp.abs(x)) / qmax, 1e-12)
            return jnp.clip(jnp.round(x / scale), -qmax - 1.0, qmax) * scale

        def fixed_qdq_u16(x):
            scale = 1.0 / 65536.0
            return jnp.clip(jnp.round(x / scale), 0.0, 65535.0) * scale

        def lpbq_dequant(w):
            O, I = w.shape
            qmax = 2.0 ** (W_BITS - 1) - 1.0
            wb = w.reshape(O, I // BLOCK, BLOCK)
            s = jnp.maximum(jnp.max(jnp.abs(wb), axis=-1, keepdims=True) / qmax, 1e-12)
            wq = jnp.clip(jnp.round(wb / s), -qmax - 1.0, qmax) * s
            return wq.reshape(O, I)
        x = act_qdq(x)
        up = act_qdq(x @ lpbq_dequant(w_up).T)
        gate = act_qdq(x @ lpbq_dequant(w_gate).T)
        sig = fixed_qdq_u16(jax.nn.sigmoid(gate))
        gate = act_qdq(gate * sig)
        o = act_qdq(gate * up)
        return o @ lpbq_dequant(w_down).T
    x = x + _L0_xattn_ref(_layernorm(x, axis=-1), ctx_1024, ctx_1024, mask_BxSxS2_bf0, mask_BxS2_bf0, L0_xattn_Wq, L0_xattn_bq, L0_xattn_Wk, L0_xattn_bk, L0_xattn_Wv, L0_xattn_bv, L0_xattn_Wo, L0_xattn_bo)
    x = x + _L0_ffn_ref(_layernorm(x, axis=-1), L0_ffn_Wg, L0_ffn_ln_scale, L0_ffn_ln_bias, L0_ffn_W1, L0_ffn_b1, L0_ffn_W2, L0_ffn_b2)
    x = x + _L1_xattn_ref(_layernorm(x, axis=-1), ctx_1024, L1_xattn_Wqkv, L1_xattn_bqkv, L1_xattn_Wqkv_aux, L1_xattn_bqkv_aux, L1_xattn_Wo, L1_xattn_bo, L1_xattn_g)
    x = x + _L1_ffn_ref(_layernorm(x, axis=-1), L1_ffn_w_gate, L1_ffn_w_up, L1_ffn_w_down)
    return x

_drawn_inputs = setup_inputs


def setup_inputs(seed=0):
    import zlib

    import numpy as np

    out = dict(_drawn_inputs(seed))
    spreads = {'L0_xattn_bq': (0.0, 0.299),
     'L0_xattn_bk': (0.0, 0.8),
     'L0_xattn_bv': (0.0, 0.1),
     'L0_xattn_bo': (0.0, 0.1),
     'L0_ffn_ln_scale': (1.0, 0.6),
     'L0_ffn_ln_bias': (0.0, 0.8),
     'L0_ffn_b1': (0.0, 0.709),
     'L0_ffn_b2': (0.0, 0.1),
     'L1_xattn_g': (0.0, 0.457)}
    factors = {'L1_xattn_bqkv': 8.0, 'L1_xattn_bqkv_aux': 8.0, 'L1_xattn_bo': 6.847}
    for name, (base, spread) in spreads.items():
        noise = np.random.default_rng([zlib.crc32(name.encode()), seed]).standard_normal(out[name].shape)
        drawn = base * np.exp(spread * noise) if base else spread * noise
        out[name] = jnp.asarray(drawn.astype(out[name].dtype))
    for name, factor in factors.items():
        out[name] = (out[name] * factor).astype(out[name].dtype)
    return out
```

```python
from contextlib import ExitStack

import concourse.bass as bass
from concourse import mybir

F32 = mybir.dt.float32
F32R = mybir.dt.float32r
BF16 = mybir.dt.bfloat16
U8 = mybir.dt.uint8
ALU = mybir.AluOpType
ACT = mybir.ActivationFunctionType
AX = mybir.AxisListType
RMAX = bass.bass_isa.ReduceOp.max

P = 128
B, S, D, S2 = 8, 224, 512, 750
H, DH = 16, 32
HG = P // DH
G = H // HG
C = D // P
T = 112
TB = S // T
NT = B * TB
KC = (S2 + P - 1) // P
SP2 = KC * P
VW = DH + 1
E, HID = 8, 128
FF = 1536
FI = FF // P
EPS = 1e-5
MASKED = -float(2.0 ** 100)
SCALE = float(DH) ** -0.5


def f32(ap):
    return ap.bitcast(F32)


class Phase:

    def __init__(self, nc, name):
        self.nc, self.name, self.stack, self.semaphores = nc, name, ExitStack(), []

    def __enter__(self):
        self.stack.__enter__()
        return self

    def __exit__(self, *e):
        self.stack.__exit__(*e)
        if self.semaphores:
            self.nc.clear_and_free_semaphores(self.semaphores)
            self.nc.all_engine_barrier()

    def sb(self, name, shape, dt=F32):
        return self.stack.enter_context(self.nc.sbuf_tensor(f"{self.name}_{name}", shape, dt))

    def ps(self, name, shape, dt=F32):
        return self.stack.enter_context(self.nc.psum_tensor(f"{self.name}_{name}", shape, dt))

    def sem(self, name):
        self.semaphores.append(self.nc.alloc_semaphore(f"{self.name}_{name}"))
        return self.semaphores[-1]

    def sems(self, name, n):
        return [self.sem(f"{name}{i}") for i in range(n)]

    def block(self):
        return self.stack.enter_context(self.nc.Block())


class SplitWeights:

    def __init__(self, ph, weights, raw_cols=C * D):
        self.src = weights
        self.hi = [ph.sb(f"w{i}h", [P, w.shape[1], w.shape[2]], F32R) for i, w in enumerate(weights)]
        self.lo = [ph.sb(f"w{i}l", [P, w.shape[1], w.shape[2]], F32R) for i, w in enumerate(weights)]
        self.raw = ph.sb("wraw", [P, 2, raw_cols])
        self.loaded = ph.sems("w_loaded", 2)
        self.hi_done = ph.sem("w_hi_done")
        self.lo_done = ph.sem("w_lo_done")

    def raw_of(self, i):
        w = self.src[i]
        return self.raw[:, i % 2, 0:w.shape[1] * w.shape[2]].rearrange("p (c n) -> p c n", c=w.shape[1])

    def load(self, sp):
        for i, w in enumerate(self.src):
            if i >= 2:
                sp.wait_ge(self.lo_done, i - 1)
            sp.dma_start(self.raw_of(i), w).then_inc(self.loaded[i % 2], 16)

    def split_hi(self, act):
        for i in range(len(self.src)):
            act.wait_ge(self.loaded[i % 2], 16 * (i // 2 + 1))
            act.activation(self.hi[i][:, :, :], self.raw_of(i), ACT.Identity).then_inc(self.hi_done, 1)

    def split_lo(self, dve):
        for i in range(len(self.src)):
            dve.wait_ge(self.hi_done, i + 1)
            dve.tensor_tensor(self.lo[i][:, :, :], self.raw_of(i), f32(self.hi[i][:, :, :]),
                              ALU.subtract).then_inc(self.lo_done, 1)

    def wait(self, pe):
        pe.wait_ge(self.lo_done, len(self.src))


def three_passes(pe, out, lhs, rhs, start=True, stop=True):
    for c in range(C):
        for k, (a, b) in enumerate(((0, 0), (0, 1), (1, 0))):
            last = pe.matmul(out, lhs(a, c), rhs(b, c), start=start and c == 0 and k == 0,
                             stop=stop and c == C - 1 and k == 2)
    return last


def ctx_projections(nc, ctx_t, weights, bk, bv, k_scr, v_scr):
    HALF = (376, 374)
    PER = 2 * G * 2 + 2 * KC
    BANKS = 8
    with Phase(nc, "cp") as ph:
        w = SplitWeights(ph, weights)
        raw = ph.sb("raw", [P, C, S2])
        ctxs = [[ph.sb(f"ctx{p}{x}", [P, C, S2], F32R) for x in "hl"] for p in range(2)]
        kst = [ph.sb(f"kst{i}", [P, 2, S2], F32R) for i in range(G)]
        vst = ph.sb("vst", [P, 4, H, VW])
        bk_sb = ph.sb("bk", [P, 2, G])
        bv_sb = ph.sb("bv", [P, 2, D])
        ps = ph.ps("ps", [P, BANKS, 512])
        consts = ph.sem("consts")
        raw_loaded, ctx_split = ph.sem("raw_loaded"), ph.sem("ctx_split")
        tile_ready, bank_free = ph.sem("tile_ready"), ph.sem("bank_free")
        passed = ph.sem("passed")
        hi_done = ph.sem("hi_done")
        k_stored, v_stored = ph.sems("k_stored", G), ph.sems("v_stored", 4)
        split_hi = ph.sem("split_hi")
        credit = ph.sb("credit", [P, 2])
        ones = ph.sem("ones")
        block = ph.block()

        @block.sync
        def _(sp):
            sp.dma_start(bk_sb[:, :, :], bk).then_inc(consts, 16)
            sp.dma_start(bv_sb[:, :, :], bv).then_inc(consts, 16)
            w.load(sp)
            with sp.Fori(0, B // 2) as i:
                for p in range(2):
                    b = i * 2 + p
                    for l in range(2):
                        for g in range(G):
                            sp.wait_ge(bank_free, b * PER + (l * 2 * G + 2 * g + 2 + BANKS))
                            sp.dma_start(k_scr[l, :, bass.ds(b, 1), g * P:(g + 1) * P, :].rearrange(
                                "x b p k -> p (x b) k"), f32(kst[g][:, :, :])).then_inc(k_stored[g], 16)
                    for v in range(2 * KC):
                        m = min(P, S2 - v % KC * P)
                        sp.wait_ge(bank_free, b * PER + (4 * G + v + 1 + BANKS))
                        sp.dma_start(v_scr[v // KC, bass.ds(b, 1), v % KC * P:v % KC * P + m, :].rearrange(
                            "b k n -> (b k) n"), vst[0:m, v % 4, :, :].rearrange("p h w -> p (h w)")).then_inc(
                                v_stored[v % 4], 16)
            for g in range(G):
                sp.wait_ge(k_stored[g], 16 * 2 * B)
            for s in range(4):
                sp.wait_ge(v_stored[s], 16 * 2 * KC * B // 4)

        @block.gpsimd
        def _(pool):
            with pool.Fori(0, B // 2) as i:
                for p in range(2):
                    b = i * 2 + p
                    pool.wait_ge(ctx_split, b)
                    pool.dma_start(raw[:, :, :], ctx_t[bass.ds(b, 1)].rearrange(
                        "b p c k -> p (b c) k")).then_inc(raw_loaded, 16)
                    pool.wait_ge(raw_loaded, b * 16 + 16)
                    pool.wait_ge(tile_ready, b * PER)
                    pool.sem_inc(passed, 1)
                    pool.tensor_copy(ctxs[p][0][:, :, :], raw[:, :, :]).then_inc(split_hi, 1)
                    pool.wait_ge(split_hi, b + 1)
                    pool.tensor_tensor(ctxs[p][1][:, :, :], raw[:, :, :], f32(ctxs[p][0][:, :, :]),
                                       ALU.subtract).then_inc(ctx_split, 1)

        @block.tensor
        def _(pe):
            w.wait(pe)
            with pe.Fori(0, B // 2) as i:
                for p in range(2):
                    b = i * 2 + p
                    pe.wait_ge(ctx_split, b + 1)
                    n = 0
                    for l in range(2):
                        wk = (w.hi[2 * l], w.lo[2 * l])
                        for g in range(G):
                            for half in range(2):
                                pe.wait_ge(bank_free, b * PER + (n + 1))
                                lo = half * HALF[0]
                                three_passes(pe, ps[:, (p * PER + n) % BANKS, 0:HALF[half]],
                                             lambda a, c: wk[a][:, c, g * P:(g + 1) * P],
                                             lambda a, c: ctxs[p][a][:, c, lo:lo + HALF[half]]).then_inc(tile_ready, 1)
                                n += 1
                    for l in range(2):
                        wv = (w.hi[2 * l + 1], w.lo[2 * l + 1])
                        for k in range(KC):
                            m = min(P, S2 - k * P)
                            pe.wait_ge(bank_free, b * PER + (n + 1))
                            last = three_passes(pe, ps[0:m, (p * PER + n) % BANKS, :],
                                                lambda a, c: ctxs[p][a][:, c, k * P:k * P + m],
                                                lambda a, c: wv[a][:, c, :])
                            last.then_inc(tile_ready, 1)
                            n += 1

        @block.scalar
        def _(act):
            w.split_hi(act)
            act.wait_ge(consts, 32)
            with act.Fori(0, B // 2) as i:
                for p in range(2):
                    b = i * 2 + p
                    for l in range(2):
                        for g in range(G):
                            act.wait_ge(k_stored[g], b * 32 + 16 * l)
                            for half in range(2):
                                n = (l * G + g) * 2 + half
                                lo = half * HALF[0]
                                act.wait_ge(tile_ready, b * PER + (PER + n + 1))
                                act.activation(kst[g][:, 0, lo:lo + HALF[half]],
                                               ps[:, (p * PER + n) % BANKS, 0:HALF[half]], ACT.Identity,
                                               bias=bk_sb[:, l, g:g + 1]).then_inc(hi_done, 1)

        @block.vector
        def _(dve):
            dve.memset(vst[:, :, :, :], 1.0).then_inc(ones, 1)
            dve.memset(credit[:, 0:1], 0.0).then_inc(bank_free, BANKS)
            dve.memset(credit[:, 1:2], 0.0).then_inc(tile_ready, PER)
            w.split_lo(dve)
            dve.wait_ge(consts, 32)
            dve.wait_ge(ones, 1)
            with dve.Fori(0, B // 2) as i:
                for p in range(2):
                    b = i * 2 + p
                    for l in range(2):
                        for g in range(G):
                            for half in range(2):
                                n = (l * G + g) * 2 + half
                                lo = half * HALF[0]
                                dve.wait_ge(hi_done, b * 4 * G + (n + 1))
                                dve.scalar_tensor_tensor(
                                    kst[g][:, 1, lo:lo + HALF[half]], ps[:, (p * PER + n) % BANKS, 0:HALF[half]],
                                    bk_sb[:, l, g:g + 1], f32(kst[g][:, 0, lo:lo + HALF[half]]),
                                    ALU.add, ALU.subtract).then_inc(bank_free, 1)
                    for v in range(2 * KC):
                        m = min(P, S2 - v % KC * P)
                        n = 4 * G + v
                        dve.wait_ge(v_stored[v % 4], b * (16 * 2 * KC // 4) + 16 * (v // 4))
                        dve.wait_ge(tile_ready, b * PER + (PER + n + 1))
                        dve.tensor_tensor(
                            vst[0:m, v % 4, :, 0:DH],
                            ps[0:m, (p * PER + n) % BANKS, :].rearrange("p (h d) -> p h d", h=H),
                            bv_sb[0:m, v // KC, :].rearrange("p (h d) -> p h d", h=H),
                            ALU.add).then_inc(bank_free, 1)


class LayerNormStats:

    def __init__(self, ph, twice=False):
        self.twice = twice
        self.st = ph.sb("ln_st", [T, NT, 6])
        self.t = [ph.sb(f"ln_t{i}", [T, NT]) for i in range(10)]
        self.mean, self.rstd = ph.sb("ln_mean", [T, NT]), ph.sb("ln_rstd", [T, NT])
        self.power = ph.sb("ln_power", [T, NT])
        self.stat = ph.sem("ln_stat")
        self.pow_ready = ph.sem("ln_pow_ready")
        self.count = NT

    def chain(self, dve, ins):
        ins.then_inc(self.stat, 1)
        self.count += 1
        dve.wait_ge(self.stat, self.count)

    def on_vector(self, dve, x):
        m_even, m_odd, v_even, v_odd = (self.st[:, :, i] for i in (1, 4, 2, 5))
        t = [a[:, :] for a in self.t]
        with dve.Fori(0, NT) as n:
            dve.bn_stats(self.st[:, bass.ds(n, 1), :].rearrange("p a s -> p (a s)"),
                         x[:, bass.ds(n, 1), :].rearrange("p a d -> p (a d)")).then_inc(self.stat, 1)
        dve.wait_ge(self.stat, NT)
        self.chain(dve, dve.tensor_tensor(t[0], m_even, m_odd, ALU.add))
        self.chain(dve, dve.tensor_scalar(self.mean[:, :], t[0], 0.5, None, ALU.mult))
        self.chain(dve, dve.tensor_tensor(t[1], m_even, m_odd, ALU.subtract))
        self.chain(dve, dve.scalar_tensor_tensor(t[2], t[1], 0.25, t[1], ALU.mult, ALU.mult))
        self.chain(dve, dve.tensor_tensor(t[3], v_even, v_odd, ALU.add))
        self.chain(dve, dve.scalar_tensor_tensor(t[4], t[3], 1.0 / D, t[2], ALU.mult, ALU.add))
        self.chain(dve, dve.tensor_scalar(t[5], t[4], EPS, None, ALU.add))
        self.var_done = self.count
        if self.twice:
            dve.wait_ge(self.pow_ready, 2)
            self.chain(dve, dve.tensor_tensor(t[6], t[4], t[9], ALU.mult))
            self.chain(dve, dve.tensor_tensor(t[7], t[6], t[9], ALU.mult))
            self.chain(dve, dve.tensor_scalar(t[8], t[7], EPS, None, ALU.add))
            dve.wait_ge(self.pow_ready, 3)
            self.chain(dve, dve.tensor_tensor(self.rstd[:, :], t[9], self.t[6][:, :], ALU.mult))
        else:
            dve.wait_ge(self.pow_ready, 2)

    def on_pool(self, pool):
        t = [a[:, :] for a in self.t]
        pool.memset(self.power[:, :], -0.5).then_inc(self.pow_ready, 1)
        pool.wait_ge(self.pow_ready, 1)
        pool.wait_ge(self.stat, NT + 7)
        first = t[9] if self.twice else self.rstd[:, :]
        pool.tensor_tensor(first, t[5], self.power[:, :], ALU.pow).then_inc(self.pow_ready, 1)
        if self.twice:
            pool.wait_ge(self.stat, NT + 10)
            pool.tensor_tensor(t[6], t[8], self.power[:, :], ALU.pow).then_inc(self.pow_ready, 1)

    def normalise(self, dve, out, x, n):
        return dve.tensor_scalar(out, x[:, bass.ds(n, 1), :].rearrange("p a d -> p (a d)"),
                                 self.mean[:, bass.ds(n, 1)], self.rstd[:, bass.ds(n, 1)],
                                 ALU.subtract, ALU.mult)


def identity(pool, ident, done):
    pool.memset(ident[:, :], 0.0).then_inc(done, 1)
    pool.wait_ge(done, 1)
    pool.affine_select(out=ident[:, :], in_=ident[:, :], compare_op=ALU.not_equal, fill=1.0, base=0,
                       pattern=[[-1, P]], channel_multiplier=1).then_inc(done, 1)


def batch_pairs(engine, body):
    with engine.Fori(0, B // 2 - 1) as i:
        for p in range(2):
            body(i * 2 + p, p, False)
    for p in range(2):
        body(B - 2 + p, p, p == 1)


class TransposedTokens:

    def __init__(self, ph, ln):
        self.ln = ln
        self.xn = [ph.sb(f"xn{p}", [T, TB, D]) for p in range(2)]
        self.xt = [[ph.sb(f"xt{p}{x}", [P, C, S], F32R) for x in "hl"] for p in range(2)]
        self.ps = ph.ps("xt_ps", [P, 2, 512])
        self.ident = ph.sb("ident", [P, P])
        self.ident_done = ph.sem("ident_done")
        self.xn_ready, self.xt_ready = ph.sem("xn_ready"), ph.sem("xt_ready")
        self.hi, self.lo = ph.sem("xt_hi"), ph.sem("xt_lo")

    def ps_view(self):
        return self.ps[:, :, 0:2 * S]

    def xt_view(self, p, part):
        return self.xt[p][part][:, :, :].rearrange("p (a c) s -> p a (c s)", a=2)

    def dve_normalise(self, dve, x, b, p):
        for t in range(TB):
            self.ln.normalise(dve, self.xn[p][:, t, :], x, b * TB + t).then_inc(self.xn_ready, 1)

    def pe_transpose(self, pe, b, p):
        pe.wait_ge(self.xn_ready, b * TB + TB)
        pe.wait_ge(self.lo, b)
        for t in range(TB):
            for c in range(C):
                last = pe.transpose(self.ps[:, c // 2, c % 2 * S + t * T:c % 2 * S + (t + 1) * T],
                                    self.xn[p][:, t, c * P:(c + 1) * P], self.ident[0:T, 0:T])
        last.then_inc(self.xt_ready, 1)

    def act_hi(self, act, b, p):
        act.wait_ge(self.xt_ready, b + 1)
        act.activation(self.xt_view(p, 0), self.ps_view(), ACT.Identity).then_inc(self.hi, 1)

    def dve_lo(self, dve, b, p):
        dve.wait_ge(self.hi, b + 1)
        dve.tensor_tensor(self.xt_view(p, 1), self.ps_view(), f32(self.xt_view(p, 0)),
                          ALU.subtract).then_inc(self.lo, 1)


def token_projections(nc, name, x, x_src, weights, bq, bv, q_scr, v_scr):
    NP = 1 if len(weights) == 1 else 2
    with_v = len(weights) == 3
    PER = NP * G + (TB if with_v else 0)
    BANKS = 4
    with Phase(nc, name) as ph:
        w = SplitWeights(ph, weights)
        ln = LayerNormStats(ph)
        tt = TransposedTokens(ph, ln)
        stage = [ph.sb(f"stage{i}", [P, 2, S], F32R) for i in range(G)]
        vst = ph.sb("vst", [T, TB, H, VW])
        bq_sb = ph.sb("bq", [P, NP, G])
        bv_sb = ph.sb("bv", [P, D])
        ps = ph.ps("ps", [P, BANKS, 512])
        credit = ph.sb("credit", [P, 2])
        consts, x_loaded, ones = ph.sem("consts"), ph.sem("x_loaded"), ph.sem("ones")
        tile_ready, bank_free, hi_done = ph.sem("tile_ready"), ph.sem("bank_free"), ph.sem("hi_done")
        stored, v_stored = ph.sems("stored", G), ph.sems("v_stored", TB)
        block = ph.block()
        n_x = 0

        @block.sync
        def _(sp):
            if x_src is not None:
                sp.dma_start(x[:, :, :], x_src.rearrange("(n p) d -> p n d", p=T)).then_inc(x_loaded, 16)
            w.load(sp)
            sp.dma_start(bq_sb[:, :, :], bq).then_inc(consts, 16)
            if with_v:
                sp.dma_start(bv_sb[:, :], bv).then_inc(consts, 16)

            with sp.Fori(0, B) as b:
                for i in range(NP):
                    for g in range(G):
                        sp.wait_ge(bank_free, b * PER + (i * G + g + 1 + BANKS))
                        sp.dma_start(q_scr[i, :, g * P:(g + 1) * P, bass.ds(b * S, S)].rearrange(
                            "x p s -> p x s"), f32(stage[g][:, :, :])).then_inc(stored[g], 16)
                if with_v:
                    for t in range(TB):
                        sp.wait_ge(bank_free, b * PER + (NP * G + t + 1 + BANKS))
                        sp.dma_start(v_scr[bass.ds(b * S + t * T, T), :],
                                     vst[:, t, :, :].rearrange("p h w -> p (h w)")).then_inc(v_stored[t], 16)
            for g in range(G):
                sp.wait_ge(stored[g], 16 * B * NP)
            if with_v:
                for t in range(TB):
                    sp.wait_ge(v_stored[t], 16 * B)

        @block.gpsimd
        def _(pool):
            identity(pool, tt.ident, tt.ident_done)
            ln.on_pool(pool)

        @block.tensor
        def _(pe):
            pe.wait_ge(tt.ident_done, 2)
            tt.pe_transpose(pe, 0, 0)
            w.wait(pe)

            def body(b, p, last):
                if not last:
                    tt.pe_transpose(pe, b + 1, 1 - p)
                pe.wait_ge(tt.lo, b + 1)
                n = 0
                for i in range(NP):
                    for g in range(G):
                        pe.wait_ge(bank_free, b * PER + (n + 1))
                        three_passes(pe, ps[:, (p * PER + n) % BANKS, 0:S],
                                     lambda a, c: (w.hi[i], w.lo[i])[a][:, c, g * P:(g + 1) * P],
                                     lambda a, c: tt.xt[p][a][:, c, :]).then_inc(tile_ready, 1)
                        n += 1
                for t in range(TB if with_v else 0):
                    pe.wait_ge(bank_free, b * PER + (n + 1))
                    three_passes(pe, ps[0:T, (p * PER + n) % BANKS, :],
                                 lambda a, c: tt.xt[p][a][:, c, t * T:(t + 1) * T],
                                 lambda a, c: (w.hi[2], w.lo[2])[a][:, c, :]).then_inc(tile_ready, 1)
                    n += 1
            batch_pairs(pe, body)

        @block.scalar
        def _(act):
            w.split_hi(act)
            act.wait_ge(consts, 16 * (2 if with_v else 1))
            tt.act_hi(act, 0, 0)

            def body(b, p, last):
                if not last:
                    act.wait_ge(tile_ready, b * PER)
                    tt.act_hi(act, b + 1, 1 - p)
                for n in range(NP * G):
                    act.wait_ge(stored[n % G], b * 16 * NP + 16 * (n // G))
                    act.wait_ge(tile_ready, b * PER + (n + 1))
                    act.activation(stage[n % G][:, 0, :], ps[:, (p * PER + n) % BANKS, 0:S], ACT.Identity,
                                   bias=bq_sb[:, n // G, n % G:n % G + 1]).then_inc(hi_done, 1)
            batch_pairs(act, body)

        @block.vector
        def _(dve):
            dve.memset(vst[:, :, :, :], 1.0).then_inc(ones, 1)
            dve.memset(credit[:, 0:1], 0.0).then_inc(bank_free, BANKS)
            if x_src is not None:
                dve.wait_ge(x_loaded, 16)
            ln.on_vector(dve, x)
            tt.dve_normalise(dve, x, 0, 0)
            w.split_lo(dve)
            tt.dve_lo(dve, 0, 0)
            dve.wait_ge(ones, 1)
            dve.wait_ge(consts, 16 * (2 if with_v else 1))

            def body(b, p, last):
                if not last:
                    dve.wait_ge(tile_ready, b * PER)
                    tt.dve_normalise(dve, x, b + 1, 1 - p)
                    tt.dve_lo(dve, b + 1, 1 - p)
                for n in range(NP * G):
                    dve.wait_ge(hi_done, b * NP * G + (n + 1))
                    dve.scalar_tensor_tensor(stage[n % G][:, 1, :], ps[:, (p * PER + n) % BANKS, 0:S],
                                             bq_sb[:, n // G, n % G:n % G + 1], f32(stage[n % G][:, 0, :]),
                                             ALU.add, ALU.subtract).then_inc(bank_free, 1)
                for t in range(TB if with_v else 0):
                    n = NP * G + t
                    dve.wait_ge(v_stored[t], b * 16)
                    dve.wait_ge(tile_ready, b * PER + (n + 1))
                    dve.tensor_tensor(vst[:, t, :, 0:DH],
                                      ps[0:T, (p * PER + n) % BANKS, :].rearrange("p (h d) -> p h d", h=H),
                                      bv_sb[0:T, :].rearrange("p (h d) -> p h d", h=H),
                                      ALU.add).then_inc(bank_free, 1)
            batch_pairs(dve, body)


def attention(nc, name, x, q_scr, sources, wo, bo, masks=None, gates=None):
    NSRC = len(sources)
    units = [(src, g) for src in range(NSRC) for g in range(G)]
    NU = len(units)
    SLOTS = (2 * HG + 1) * NU + 2
    FIRST = 2 * HG + 1
    LOADS = 8
    NM = 2 + TB + KC
    with Phase(nc, name) as ph:
        w = SplitWeights(ph, [wo])
        kst = [ph.sb(f"kst{g}", [97, HG, SP2], F32R) for g in range(G)]
        qst = [ph.sb(f"qst{g}", [97, HG, S], F32R) for g in range(G)]
        vst = [ph.sb(f"vst{g}", [P, KC, HG * VW]) for g in range(G)]
        prob = [ph.sb(f"prob{i}", [P, KC, S]) for i in range(2)]
        osb = ph.sb("osb", [T, TB, D])
        part = ph.sb("part", [T, TB, HG, DH])
        ot = [ph.sb(f"ot{x}", [P, C, S], F32R) for x in "hl"]
        mx = [ph.sb(f"mx{i}", [T, 2 * HG]) for i in range(2)]
        mrow = [ph.sb(f"mrow{i}", [2 * HG, T], F32R) for i in range(2)]
        rden = [ph.sb(f"rden{i}", [T, TB, HG]) for i in range(3)]
        ident, ident_b = ph.sb("ident", [P, P]), ph.sb("ident_b", [P, P], BF16)
        bo_sb = ph.sb("bo", [T, D])
        credit = ph.sb("credit", [P, 4])
        slot = ph.ps("slot", [P, 2, 1024])
        st_ps = ph.ps("st_ps", [P, 3, 512])
        o_ps = ph.ps("o_ps", [P, 512])
        o_heads = o_ps[0:T, 0:TB * HG * VW].rearrange("p (t h w) -> p t h w", t=TB, h=HG)
        ident_done, consts, init = ph.sem("ident_done"), ph.sem("consts"), ph.sem("init")
        loaded = ph.sems("loaded", G)
        slot_ready, slot_free = ph.sem("slot_ready"), ph.sem("slot_free")
        passed = ph.sem("passed")
        m_stored = ph.sems("m_stored", 2)
        st_ready, exp_done, pv_done = ph.sem("st_ready"), ph.sem("exp_done"), ph.sem("pv_done")
        o_free, step = ph.sem("o_free"), ph.sem("step")
        ot_hi, x_biased = ph.sem("ot_hi"), ph.sem("x_biased")
        if masks:
            mb = [ph.sb(f"mb{i}", [T, TB, S2], BF16) for i in range(2)]
            mbt = [ph.sb(f"mbt{i}", [P, KC, S], BF16) for i in range(2)]
            m_raw, mt_raw = ph.sb("m_raw", [T, TB, S2], U8), ph.sb("mt_raw", [P, KC, S], U8)
            kp_raw, kpt_raw = ph.sb("kp_raw", [T, S2], U8), ph.sb("kpt_raw", [P, KC], U8)
            kpb, kptb = ph.sb("kpb", [T, S2], BF16), ph.sb("kptb", [P, KC])
            mask_loaded, mask_conv = ph.sem("mask_loaded"), ph.sem("mask_conv")
        if gates is not None:
            gate_raw, gate = ph.sb("gate_raw", [T, H]), [ph.sb(f"gate{i}", [T, H]) for i in range(3)]
            gate_done = ph.sem("gate_done")
        CREDIT = 4 * HG
        pads = [(keys, -(-keys // P) * P) for keys, _, _ in sources]
        INIT = G * len(pads) + (1 if masks else 0)
        block = ph.block()

        @block.sync
        def _(sp):
            w.load(sp)
            sp.dma_start(bo_sb[:, :], bo).then_inc(consts, 16)
            if gates is not None:
                sp.dma_start(gate_raw[:, :], gates).then_inc(consts, 16)
            sp.wait_ge(init, INIT)
            sp.wait_ge(ident_done, 3 + G)

            def body(b, p, last):
                if masks:
                    sp.wait_ge(mask_conv, b * NM)
                    sp.sem_inc(passed, 1)
                    attn_mask, attn_mask_t, key_mask, key_mask_t = masks
                    full = KC - 1
                    sp.dma_start(m_raw[:, :, :], attn_mask[bass.ds(b, 1)].rearrange(
                        "b (t p) k -> p (b t) k", p=T)).then_inc(mask_loaded, 16)
                    sp.dma_start(mt_raw[:, 0:full, :], attn_mask_t[bass.ds(b, 1), 0:full * P, :].rearrange(
                        "b (c p) s -> p (b c) s", p=P)).then_inc(mask_loaded, 16)
                    sp.dma_start(mt_raw[0:S2 - full * P, full, :], attn_mask_t[
                        bass.ds(b, 1), full * P:S2, :].rearrange("b p s -> p (b s)")).then_inc(mask_loaded, 16)
                    sp.dma_start(kp_raw[:, :], key_mask[bass.ds(b, 1), :].to_broadcast([T, S2])).then_inc(
                        mask_loaded, 16)
                    sp.dma_start(kpt_raw[:, :], key_mask_t[:, bass.ds(b, 1), :].rearrange(
                        "p b c -> p (b c)")).then_inc(mask_loaded, 16)
                for ui, (src, g) in enumerate(units):
                    keys, k_of, v_of = sources[src]
                    full = (keys - 1) // P
                    sp.wait_ge(pv_done, b * NU * HG + HG * (ui + 1))
                    kh = [k_of(b, part)[g * P:(g + 1) * P, :].rearrange("(h d) k -> d h k", h=HG) for part in (0, 1)]
                    qh = [q_scr[part, g * P:(g + 1) * P, bass.ds(b * S, S)].rearrange("(h d) s -> d h s", h=HG)
                          for part in (0, 1)]
                    for row, part in enumerate((0, 1, 0)):
                        sp.dma_start(f32(kst[g][row * DH:(row + 1) * DH, :, 0:keys]), kh[part]).then_inc(loaded[g], 16)
                    for row, part in enumerate((0, 0, 1)):
                        sp.dma_start(f32(qst[g][row * DH:(row + 1) * DH, :, :]), qh[part]).then_inc(loaded[g], 16)
                    v = v_of(b)[:, g * HG * VW:(g + 1) * HG * VW]
                    sp.dma_start(vst[g][:, 0:full, :], v[0:full * P, :].rearrange(
                        "(c p) w -> p c w", p=P)).then_inc(loaded[g], 16)
                    sp.dma_start(vst[g][0:keys - full * P, full, :], v[full * P:keys, :]).then_inc(loaded[g], 16)
            with sp.Fori(0, B) as b:
                body(b, 0, False)

        @block.gpsimd
        def _(pool):
            identity(pool, ident, ident_done)
            pool.wait_ge(ident_done, 2)
            pool.tensor_copy(ident_b[:, :], ident[:, :]).then_inc(ident_done, 1)
            for g in range(G):
                pool.wait_ge(ident_done, 3 + g)
                pool.memset(f32(kst[g][96:97, :, :]), 1.0).then_inc(ident_done, 1)

            def m_rows(b, ui):
                if isinstance(b, int) and b == 0 and ui == 0:
                    pool.wait_ge(slot_free, 2 + FIRST)
                    pool.sem_inc(passed, 1)
                elif ui == 0:
                    pool.wait_ge(slot_free, b * SLOTS + (2 + FIRST - 2))
                    pool.sem_inc(passed, 1)
                else:
                    pool.wait_ge(slot_free, b * SLOTS + (2 + FIRST + ui * (2 * HG + 1)))
                    pool.sem_inc(passed, 1)
                g = units[ui][1]
                pool.dma_start(f32(qst[g][96:97, :, :]).rearrange("a h (t s) -> a (h t) s", t=TB),
                               f32(mrow[ui % 2][:, :])).then_inc(m_stored[ui % 2], 16)
            m_rows(0, 0)

            def body(b, p, last):
                for ui in range(1, NU):
                    m_rows(b, ui)
                if not last:
                    m_rows(b + 1, 0)
            batch_pairs(pool, body)

        @block.tensor
        def _(pe):
            pe.wait_ge(ident_done, 3)

            def slot_number(b, ui, j):
                return b * SLOTS + (ui * (2 * HG + 1) + j)

            def parity(p, n):
                return (p * SLOTS + n) % 2

            def score_tile(b, p, ui, h, t, base, psb):
                src, g = units[ui]
                keys = sources[src][0]
                s = 2 * h + t
                pe.wait_ge(slot_free, base + (s + 1))
                par = (psb + s) % 2
                for lo in range(0, keys, 512):
                    n = min(512, keys - lo)
                    last = pe.matmul(slot[0:T, par, lo:lo + n], qst[g][0:96, h, t * T:(t + 1) * T],
                                     kst[g][0:96, h, lo:lo + n], start=True, stop=not masks)
                    if masks:
                        last = pe.matmul(slot[0:T, par, lo:lo + n], ident_b[0:T, 0:T],
                                         mb[p][:, t, lo:lo + n], start=False, stop=True)
                last.then_inc(slot_ready, 1)

            def max_transpose(ui, base, psb):
                pe.wait_ge(slot_free, base + (2 * HG + 2))
                par = (psb + 2 * HG) % 2
                pe.transpose(slot[0:2 * HG, par, 0:T], mx[ui % 2][:, :], ident[0:T, 0:T]).then_inc(slot_ready, 1)

            def phase1_ready(b, ui):
                src, g = units[ui]
                pe.wait_ge(loaded[g], b * (16 * LOADS * NSRC) + 16 * LOADS * (src + 1))
                if masks and ui == 0:
                    pe.wait_ge(mask_conv, b * NM + NM)

            phase1_ready(0, 0)
            for h in range(HG):
                for t in range(TB):
                    score_tile(0, 0, 0, h, t, 0, 0)
            max_transpose(0, 0, 0)

            def body(b, p, last):
                for ui, (src, g) in enumerate(units):
                    keys = sources[src][0]
                    nch = (keys + P - 1) // P
                    follows = not (last and ui == NU - 1)
                    nb, np_, nu = (b, p, ui + 1) if ui + 1 < NU else (b + 1, 1 - p, 0)
                    base = b * SLOTS + (FIRST + ui * FIRST)
                    psb = p * SLOTS + FIRST + ui * FIRST

                    def probabilities_times_v(h):
                        k = ui * HG + h
                        pe.wait_ge(exp_done, b * NU * HG + (k + 1))
                        if h == 0:
                            pe.wait_ge(o_free, b * NU + ui)
                        for t in range(TB):
                            for c in range(nch):
                                m = min(P, keys - c * P)
                                last_mm = pe.matmul(o_heads[:, t, h, :], prob[h % 2][0:m, c, t * T:(t + 1) * T],
                                                    vst[g][0:m, c, h * VW:(h + 1) * VW],
                                                    start=c == 0, stop=c == nch - 1)
                        last_mm.then_inc(pv_done, 1)

                    if follows:
                        phase1_ready(nb, nu)
                    pe.wait_ge(m_stored[ui % 2], b * (8 * NU) + 16 * (ui // 2 + 1))
                    for h in range(HG):
                        if h == HG - 1 and follows:
                            max_transpose(nu, base, psb)
                        pe.wait_ge(exp_done, b * NU * HG + (ui * HG + h))
                        for c in range(nch):
                            out = st_ps[:, c // 2, c % 2 * S:c % 2 * S + S]
                            last_mm = pe.matmul(out, kst[g][:, h, c * P:(c + 1) * P], qst[g][:, h, :],
                                                start=True, stop=not masks)
                            if masks:
                                last_mm = pe.matmul(out, ident_b[:, :], mbt[p][:, c, :], start=False, stop=True)
                        last_mm.then_inc(st_ready, 1)
                        if h >= 1:
                            probabilities_times_v(h - 1)
                        if follows:
                            for nh in ((0, 1), (2,), (3,), ())[h]:
                                for t in range(TB):
                                    score_tile(nb, np_, nu, nh, t, base, psb)
                    probabilities_times_v(HG - 1)
                base = b * SLOTS + (FIRST + NU * FIRST) - (FIRST if last else 0)
                psb = p * SLOTS + FIRST + NU * FIRST - (FIRST if last else 0)
                pe.wait_ge(o_free, b * NU + NU)
                pe.wait_ge(slot_free, base + 1)
                par = psb % 2
                for t in range(TB):
                    for c in range(C):
                        at = c // 2 * 512 + c % 2 * S + t * T
                        tr = pe.transpose(slot[:, par, at:at + T], osb[:, t, c * P:(c + 1) * P], ident[0:T, 0:T])
                tr.then_inc(slot_ready, 1)
                w.wait(pe)
                pe.wait_ge(slot_free, base + 3)
                par = (psb + 1) % 2
                for t in range(TB):
                    mm = three_passes(pe, slot[0:T, par, t * D:(t + 1) * D],
                                      lambda a, c: ot[a][:, c, t * T:(t + 1) * T],
                                      lambda a, c: (w.hi[0], w.lo[0])[a][:, c, :])
                mm.then_inc(slot_ready, 1)
            batch_pairs(pe, body)

        @block.scalar
        def _(act):
            if gates is not None:
                act.wait_ge(consts, 32)
                act.activation(gate[0][:, :], gate_raw[:, :], ACT.Exp, scale=-1.0).then_inc(gate_done, 1)
            w.split_hi(act)

            def body(b, p, last):
                for ui, (src, g) in enumerate(units):
                    nch = (sources[src][0] + P - 1) // P
                    for h in range(HG):
                        k = ui * HG + h
                        act.wait_ge(st_ready, b * NU * HG + (k + 1))
                        act.wait_ge(pv_done, b * NU * HG + (k + CREDIT - 1))
                        act.activation(prob[h % 2][:, 0:nch, :].rearrange("p (a c) s -> p a (c s)", c=2),
                                       st_ps[:, 0:nch // 2, 0:2 * S], ACT.Exp, scale=SCALE).then_inc(exp_done, 1)
                base = b * SLOTS + (FIRST + NU * FIRST) - (FIRST if last else 0)
                par = (p * SLOTS + FIRST + NU * FIRST - (FIRST if last else 0)) % 2
                act.wait_ge(slot_ready, base + 1)
                act.activation(ot[0][:, :, :].rearrange("p (a c) s -> p a (c s)", a=2),
                               slot[:, par, :].rearrange("p (a n) -> p a n", a=2)[:, :, 0:2 * S],
                               ACT.Identity).then_inc(ot_hi, 1)
            batch_pairs(act, body)

        @block.vector
        def _(dve):
            dve.memset(credit[:, 0:1], 0.0).then_inc(slot_free, 2)
            dve.memset(credit[:, 1:2], 0.0).then_inc(pv_done, CREDIT)
            for g in range(G):
                for lo, hi in pads:
                    dve.memset(f32(kst[g][0:96, :, lo:hi]), 0.0).then_inc(init, 1)
            if masks:
                dve.memset(mt_raw[:, :, :].rearrange("p c s -> p (c s)"), 1).then_inc(init, 1)
            if gates is not None:
                dve.wait_ge(gate_done, 1)
                dve.tensor_scalar(gate[1][:, :], gate[0][:, :], 1.0, None, ALU.add).then_inc(gate_done, 1)
                dve.wait_ge(gate_done, 2)
                dve.reciprocal(gate[0][:, :], gate[1][:, :]).then_inc(gate_done, 1)
                dve.wait_ge(gate_done, 3)
                dve.tensor_scalar(gate[2][:, :], gate[0][:, :], -1.0, 1.0, ALU.mult, ALU.add).then_inc(gate_done, 1)
                dve.wait_ge(gate_done, 4)
            w.split_lo(dve)
            dve.wait_ge(consts, 16 * (2 if gates is not None else 1))
            with dve.Fori(0, NT) as n:
                xt = x[:, bass.ds(n, 1), :].rearrange("p a d -> p (a d)")
                dve.tensor_tensor(xt, xt, bo_sb[:, :], ALU.add).then_inc(x_biased, 1)

            def convert_masks(b, p):
                dve.wait_ge(mask_loaded, b * 80 + 80)
                dve.tensor_scalar(kpb[:, :], kp_raw[:, :], MASKED, None, ALU.mult).then_inc(mask_conv, 1)
                dve.tensor_scalar(kptb[:, :], kpt_raw[:, :], MASKED, None, ALU.mult).then_inc(mask_conv, 1)
                dve.wait_ge(mask_conv, b * NM + 2)
                for t in range(TB):
                    dve.scalar_tensor_tensor(mb[p][:, t, :], m_raw[:, t, :], MASKED, kpb[:, :],
                                             ALU.mult, ALU.add).then_inc(mask_conv, 1)
                for c in range(KC):
                    dve.tensor_scalar(mbt[p][:, c, :], mt_raw[:, c, :], MASKED, kptb[:, c:c + 1],
                                      ALU.mult, ALU.add).then_inc(mask_conv, 1)

            def maxima(ui, base, psb, mb_):
                keys = sources[units[ui][0]][0]
                for s in range(2 * HG):
                    dve.wait_ge(slot_ready, base + (s + 1))
                    dve.tensor_reduce(mx[ui % 2][:, s:s + 1], slot[0:T, (psb + s) % 2, 0:keys], AX.X, ALU.max,
                                      negate=True).then_inc(slot_free, 1)
                dve.wait_ge(slot_ready, base + (2 * HG + 1))
                dve.wait_ge(m_stored[ui % 2], mb_ * (8 * NU) + 16 * (ui // 2))
                dve.tensor_copy(mrow[ui % 2][:, :], slot[0:2 * HG, (psb + 2 * HG) % 2, 0:T]).then_inc(slot_free, 1)

            if masks:
                convert_masks(0, 0)
            maxima(0, 0, 0, 0)

            def body(b, p, last):
                NSTEP = NU * (3 if masks else 2) + sum(1 for s, g in units if s > 0)
                done = 0
                for ui, (src, g) in enumerate(units):
                    if masks and ui == 1 and not last:
                        convert_masks(b + 1, 1 - p)
                    nu = (ui + 1) % NU
                    if not (last and ui == NU - 1):
                        maxima(nu, b * SLOTS + (FIRST + ui * FIRST), p * SLOTS + FIRST + ui * FIRST,
                               b if nu else b + 1)

                    def link(ins):
                        nonlocal done
                        ins.then_inc(step, 1)
                        done += 1
                        dve.wait_ge(step, b * NSTEP + done)
                    dve.wait_ge(pv_done, b * NU * HG + (CREDIT + HG * (ui + 1)))
                    link(dve.reciprocal(rden[0][:, :, :], o_heads[:, :, :, DH]))
                    scale = rden[0]
                    if masks:
                        link(dve.tensor_scalar(rden[1][:, :, :], mx[ui % 2][:, :].rearrange("p (h t) -> p t h", t=TB),
                                               -MASKED / 2, None, ALU.is_lt))
                        link(dve.tensor_tensor(rden[2][:, :, :], rden[0][:, :, :], rden[1][:, :, :], ALU.mult))
                        scale = rden[2]
                    if gates is not None:
                        gs = gate[2 if src == 0 else 0][:, g * HG:(g + 1) * HG].unsqueeze(1).to_broadcast([T, TB, HG])
                        link(dve.tensor_tensor(rden[2][:, :, :], rden[0][:, :, :], gs, ALU.mult))
                        scale = rden[2]
                    scale = scale[:, :, :].unsqueeze(3).to_broadcast([T, TB, HG, DH])
                    dst = osb[:, :, g * P:(g + 1) * P].rearrange("p t (h d) -> p t h d", h=HG)
                    if src == 0:
                        dve.tensor_tensor(dst, o_heads[:, :, :, 0:DH], scale, ALU.mult).then_inc(o_free, 1)
                    else:
                        dve.tensor_tensor(part[:, :, :, :], o_heads[:, :, :, 0:DH], scale, ALU.mult).then_inc(step, 1)
                        done += 1
                        dve.wait_ge(step, b * NSTEP + done)
                        dve.tensor_tensor(dst, dst, part[:, :, :, :], ALU.add).then_inc(o_free, 1)
                base = b * SLOTS + (FIRST + NU * FIRST) - (FIRST if last else 0)
                psb = p * SLOTS + FIRST + NU * FIRST - (FIRST if last else 0)
                dve.wait_ge(ot_hi, b + 1)
                dve.tensor_tensor(ot[1][:, :, :].rearrange("p (a c) s -> p a (c s)", a=2),
                                  slot[:, psb % 2, :].rearrange("p (a n) -> p a n", a=2)[:, :, 0:2 * S],
                                  f32(ot[0][:, :, :]).rearrange("p (a c) s -> p a (c s)", a=2),
                                  ALU.subtract).then_inc(slot_free, 1)
                dve.wait_ge(slot_ready, base + 2)
                xb = x[:, bass.ds(b * TB, TB), :]
                dve.tensor_tensor(xb, slot[0:T, (psb + 1) % 2, :].rearrange("p (t d) -> p t d", t=TB), xb,
                                  ALU.add).then_inc(slot_free, 1)
            batch_pairs(dve, body)


def experts(nc, x, wg, ln_scale, ln_bias, w1, b1, w2, b2):
    with Phase(nc, "ex") as ph:
        ln = LayerNormStats(ph, twice=True)
        tt = TransposedTokens(ph, ln)
        w1_raw = ph.sb("w1_raw", [P, 2, C, HID])
        w1_sc = ph.sb("w1_sc", [P, 2, C, HID])
        w1h, w1l = [ph.sb(f"w1{x_}", [P, E, C, HID], F32R) for x_ in "hl"]
        w2_raw = ph.sb("w2_raw", [P, 2, D])
        w2h, w2l = [ph.sb(f"w2{x_}", [P, E, D], F32R) for x_ in "hl"]
        wg_sb, sc_sb, bi_sb = ph.sb("wg", [P, C, E]), ph.sb("sc", [P, C, E]), ph.sb("bi", [P, C, E])
        wgh, wgl = [ph.sb(f"wg{x_}", [P, C, E], F32R) for x_ in "hl"]
        b1_sb, b1f = ph.sb("b1", [P, E]), ph.sb("b1f", [P, E])
        b2_sb = ph.sb("b2", [E, D])
        rank = ph.sb("rank", [T, TB, E])
        sel = ph.sb("sel", [E, E, P])
        logit = ph.sb("logit", [T, TB, E])
        top, pick, best = ph.sb("top", [T, TB]), ph.sb("pick", [T, TB, E]), ph.sb("best", [T, TB])
        is_top, hot = ph.sb("is_top", [T, TB, E]), ph.sb("hot", [T, TB, E])
        hot_t = ph.sb("hot_t", [E, S])
        hid = [ph.sb(f"hid{i}", [P, S]) for i in range(2)]
        hm = [ph.sb(f"hm{i}", [P, S]) for i in range(2)]
        hh = [[ph.sb(f"h{x_}{p}", [P, E, S], F32R) for x_ in "hl"] for p in range(2)]
        small = ph.ps("small", [P, 512])
        hid_ps = [ph.ps(f"hid_ps{i}", [P, 512]) for i in range(2)]
        y_ps = ph.ps("y_ps", [P, 2, 512])
        mask_ps = ph.ps("mask_ps", [P, 512])
        consts = ph.sem("consts")
        w1_loaded, w2_loaded = ph.sems("w1_loaded", 2), ph.sems("w2_loaded", 2)
        w1_scaled, w1_hi, w1_lo = ph.sem("w1_scaled"), ph.sem("w1_hi"), ph.sem("w1_lo")
        w2_hi, w2_lo = ph.sem("w2_hi"), ph.sem("w2_lo")
        bias_ready, bias_done, wg_hi, wg_lo = ph.sem("bias_ready"), ph.sem("bias_done"), ph.sem("wg_hi"), ph.sem("wg_lo")
        sel_done = ph.sem("sel_done")
        logit_ready, gate_step, hot_ready = ph.sem("logit_ready"), ph.sem("gate_step"), ph.sem("hot_ready")
        mask_ready, hid_ready, gelu_done = ph.sem("mask_ready"), ph.sem("hid_ready"), ph.sem("gelu_done")
        h_masked, h_hi, h_lo = ph.sem("h_masked"), ph.sem("h_hi"), ph.sem("h_lo")
        y_ready, y_added = ph.sem("y_ready"), ph.sem("y_added")
        block = ph.block()
        STEPS = 6

        @block.sync
        def _(sp):
            for dst, src in ((wg_sb[:, :, :], wg), (sc_sb[:, :, :], ln_scale), (bi_sb[:, :, :], ln_bias),
                             (b1_sb[:, :], b1), (b2_sb[:, :], b2)):
                sp.dma_start(dst, src).then_inc(consts, 16)
            for e in range(E):
                if e >= 2:
                    sp.wait_ge(w1_scaled, C * (e - 1))
                    sp.wait_ge(bias_ready, e - 1)
                    sp.wait_ge(w2_lo, e - 1)
                sp.dma_start(w1_raw[:, e % 2, :, :], w1[:, e, :, :]).then_inc(w1_loaded[e % 2], 16)
                sp.dma_start(w2_raw[:, e % 2, :], w2[:, e, :]).then_inc(w2_loaded[e % 2], 16)

        @block.gpsimd
        def _(pool):
            identity(pool, tt.ident, tt.ident_done)
            ln.on_pool(pool)
            pool.memset(sel[:, :, :], 0.0).then_inc(sel_done, 1)
            pool.wait_ge(sel_done, 1)
            pool.affine_select(out=sel[:, :, :], in_=sel[:, :, :], compare_op=ALU.not_equal, fill=1.0, base=0,
                               pattern=[[-1, E], [0, P]], channel_multiplier=1).then_inc(sel_done, 1)
            for e in range(E):
                pool.memset(rank[:, :, e:e + 1], float(E - e)).then_inc(sel_done, 1)
                pool.wait_ge(sel_done, 3 + e)

        @block.tensor
        def _(pe):
            pe.wait_ge(tt.ident_done, 2)
            pe.wait_ge(consts, 80)
            for e in range(E):
                pe.wait_ge(w1_loaded[e % 2], 16 * (e // 2 + 1))
                for c in range(C):
                    mm = pe.matmul(small[:, e:e + 1], w1_raw[:, e % 2, c, :], bi_sb[:, c, e:e + 1],
                                   start=c == 0, stop=c == C - 1)
                mm.then_inc(bias_ready, 1)
            tt.pe_transpose(pe, 0, 0)

            def body(b, p, last):
                if not last:
                    tt.pe_transpose(pe, b + 1, 1 - p)
                pe.wait_ge(tt.lo, b + 1)
                pe.wait_ge(hot_ready, b * 2 + 1)
                if isinstance(b, int) or True:
                    pe.wait_ge(wg_lo, 1)
                for t in range(TB):
                    mm = three_passes(pe, small[0:T, t * E:(t + 1) * E],
                                      lambda a, c: tt.xt[p][a][:, c, t * T:(t + 1) * T],
                                      lambda a, c: (wgh, wgl)[a][:, c, :])
                mm.then_inc(logit_ready, 1)

                def first_product(e):
                    k = e
                    pe.wait_ge(gelu_done, b * E + k - 1) if k >= 1 else pe.wait_ge(gelu_done, b * E)
                    three_passes(pe, hid_ps[e % 2][:, 0:S], lambda a, c: (w1h, w1l)[a][:, e, c, :],
                                 lambda a, c: tt.xt[p][a][:, c, :]).then_inc(hid_ready, 1)
                pe.wait_ge(w1_lo, E * C)
                first_product(0)
                first_product(1)
                pe.wait_ge(gate_step, b * STEPS + STEPS)
                for t in range(TB):
                    mm = pe.transpose(small[0:E, 64 + t * T:64 + (t + 1) * T], hot[:, t, :], tt.ident[0:T, 0:T])
                mm.then_inc(logit_ready, 1)
                for e in range(E):
                    if e >= 2:
                        first_product(e)
                    pe.wait_ge(hot_ready, b * 2 + 3)
                    pe.wait_ge(h_masked, b * E + e)
                    pe.matmul(mask_ps[:, 0:S], sel[:, e, :], hot_t[:, :], start=True, stop=True).then_inc(mask_ready, 1)
                pe.wait_ge(w2_lo, E)
                pe.wait_ge(y_added, b)
                for t in range(TB):
                    pe.matmul(y_ps[0:T, t, :], hot_t[:, t * T:(t + 1) * T], b2_sb[:, :], start=True, stop=False)
                for e in range(E):
                    pe.wait_ge(h_lo, b * E + (e + 1))
                    for t in range(TB):
                        for a, w in ((0, w2h), (0, w2l), (1, w2h)):
                            mm = pe.matmul(y_ps[0:T, t, :], hh[p][a][:, e, t * T:(t + 1) * T], w[:, e, :],
                                           start=False, stop=e == E - 1 and a == 1)
                mm.then_inc(y_ready, 1)
            batch_pairs(pe, body)

        @block.scalar
        def _(act):
            for e in range(E):
                for c in range(C):
                    act.wait_ge(w1_scaled, e * C + c + 1)
                act.activation(w1h[:, e, :, :], w1_sc[:, e % 2, :, :], ACT.Identity).then_inc(w1_hi, 1)
                act.wait_ge(w2_loaded[e % 2], 16 * (e // 2 + 1))
                act.activation(w2h[:, e, :], w2_raw[:, e % 2, :], ACT.Identity).then_inc(w2_hi, 1)
            act.wait_ge(consts, 80)
            act.activation(wgh[:, :, :], wg_sb[:, :, :], ACT.Identity).then_inc(wg_hi, 1)
            tt.act_hi(act, 0, 0)
            act.wait_ge(hot_ready, 1)

            def body(b, p, last):
                if not last:
                    act.wait_ge(y_ready, b)
                    tt.act_hi(act, b + 1, 1 - p)
                for e in range(E):
                    act.wait_ge(hid_ready, b * E + (e + 1))
                    if e >= 2:
                        act.wait_ge(h_masked, b * E + (e - 1))
                    else:
                        act.wait_ge(h_masked, b * E)
                    act.activation(hid[e % 2][:, :], hid_ps[e % 2][:, 0:S], ACT.Gelu,
                                   bias=b1f[:, e:e + 1]).then_inc(gelu_done, 1)
            batch_pairs(act, body)

        @block.vector
        def _(dve):
            ln.on_vector(dve, x)
            tt.dve_normalise(dve, x, 0, 0)
            dve.wait_ge(consts, 80)
            for e in range(E):
                dve.wait_ge(w1_loaded[e % 2], 16 * (e // 2 + 1))
                if e >= 2:
                    dve.wait_ge(w1_lo, C * (e - 1))
                for c in range(C):
                    dve.tensor_scalar(w1_sc[:, e % 2, c, :], w1_raw[:, e % 2, c, :], sc_sb[:, c, e:e + 1], None,
                                      ALU.mult).then_inc(w1_scaled, 1)
                dve.wait_ge(w1_hi, e + 1)
                dve.tensor_tensor(w1l[:, e, :, :], w1_sc[:, e % 2, :, :], f32(w1h[:, e, :, :]),
                                  ALU.subtract).then_inc(w1_lo, C)
                dve.wait_ge(w2_hi, e + 1)
                dve.tensor_tensor(w2l[:, e, :], w2_raw[:, e % 2, :], f32(w2h[:, e, :]), ALU.subtract).then_inc(w2_lo, 1)
            dve.wait_ge(wg_hi, 1)
            dve.tensor_tensor(wgl[:, :, :], wg_sb[:, :, :], f32(wgh[:, :, :]), ALU.subtract).then_inc(wg_lo, 1)
            dve.wait_ge(bias_ready, E)
            dve.tensor_tensor(b1f[:, :], small[:, 0:E], b1_sb[:, :], ALU.add).then_inc(hot_ready, 1)
            tt.dve_lo(dve, 0, 0)
            dve.wait_ge(sel_done, 2 + E)

            def body(b, p, last):
                if not last:
                    dve.wait_ge(y_ready, b)
                    tt.dve_normalise(dve, x, b + 1, 1 - p)
                    tt.dve_lo(dve, b + 1, 1 - p)
                done = 0

                def link(ins):
                    nonlocal done
                    ins.then_inc(gate_step, 1)
                    done += 1
                    dve.wait_ge(gate_step, b * STEPS + done)
                dve.wait_ge(logit_ready, b * 2 + 1)
                link(dve.tensor_copy(logit[:, :, :], small[0:T, 0:TB * E].rearrange("p (t e) -> p t e", t=TB)))
                link(dve.tensor_reduce(top[:, :], logit[:, :, :], AX.X, ALU.max))
                link(dve.tensor_tensor(is_top[:, :, :], logit[:, :, :],
                                       top[:, :].unsqueeze(2).to_broadcast([T, TB, E]), ALU.is_equal))
                link(dve.tensor_tensor(pick[:, :, :], is_top[:, :, :], rank[:, :, :], ALU.mult))
                link(dve.tensor_reduce(best[:, :], pick[:, :, :], AX.X, ALU.max))
                link(dve.tensor_tensor(hot[:, :, :], rank[:, :, :],
                                       best[:, :].unsqueeze(2).to_broadcast([T, TB, E]), ALU.is_equal))
                dve.wait_ge(logit_ready, b * 2 + 2)
                dve.wait_ge(y_ready, b)
                dve.tensor_copy(hot_t[:, :], small[0:E, 64:64 + S]).then_inc(hot_ready, 2)
                for e in range(E):
                    dve.wait_ge(gelu_done, b * E + (e + 1))
                    dve.wait_ge(mask_ready, b * E + (e + 1))
                    dve.tensor_tensor(hm[e % 2][:, :], mask_ps[:, 0:S], hid[e % 2][:, :], ALU.mult).then_inc(h_masked, 1)
                    dve.wait_ge(h_masked, b * E + (e + 1))
                    dve.tensor_copy(hh[p][0][:, e, :], hm[e % 2][:, :]).then_inc(h_hi, 1)
                    dve.wait_ge(h_hi, b * E + (e + 1))
                    dve.tensor_tensor(hh[p][1][:, e, :], hm[e % 2][:, :], f32(hh[p][0][:, e, :]),
                                      ALU.subtract).then_inc(h_lo, 1)
                dve.wait_ge(y_ready, b + 1)
                xb = x[:, bass.ds(b * TB, TB), :]
                dve.tensor_tensor(xb, y_ps[0:T, :, :], xb, ALU.add).then_inc(y_added, 1)
            batch_pairs(dve, body)


QMAX = 32767.0
MAGIC = 1.5 * 2.0 ** 23
MAGIC16 = 1.5 * 2.0 ** 7
WMAX = 7.0
WBLOCK = 32


def quantised_input(nc, x, x_scr, xq_hi, xq_lo, sx):
    with Phase(nc, "fq") as ph:
        ln = LayerNormStats(ph)
        xn = x
        am, am1, rs = ph.sb("am", [P, NT]), ph.sb("am1", [P, 4]), ph.sb("rs", [P, 1])
        qb, qi = ph.sb("qb", [T, 2, D]), ph.sb("qi", [T, 2, D])
        ident = ph.sb("ident", [P, P])
        ps = ph.ps("ps", [P, 2, 512])
        ident_done, norm, amax, scale = ph.sem("ident_done"), ph.sem("norm"), ph.sem("amax"), ph.sem("scale")
        biased, rounded = ph.sem("biased"), ph.sem("rounded")
        turned, hi_done, lo_done, x_stored = ph.sem("turned"), ph.sem("hi_done"), ph.sem("lo_done"), ph.sem("x_stored")
        block = ph.block()

        def view(ap, p):
            return ap[:, p, 0:C * T].rearrange("p (c s) -> p c s", c=C)

        @block.sync
        def _(sp):
            sp.dma_start(x_scr.rearrange("(n p) d -> p n d", p=T), x[:, :, :]).then_inc(x_stored, 16)
            sp.wait_ge(x_stored, 16)

        @block.gpsimd
        def _(pool):
            identity(pool, ident, ident_done)
            ln.on_pool(pool)
            pool.wait_ge(scale, 2)
            pool.partition_all_reduce(am1[:, 1:2], am1[:, 0:1], P, RMAX).then_inc(scale, 1)

        @block.vector
        def _(dve):
            dve.memset(am[:, :], 0.0).then_inc(scale, 1)
            ln.on_vector(dve, x)
            dve.wait_ge(scale, 1)
            dve.wait_ge(x_stored, 16)
            with dve.Fori(0, NT) as n:
                xt = xn[:, bass.ds(n, 1), :].rearrange("p a d -> p (a d)")
                ln.normalise(dve, xt, x, n).then_inc(norm, 1)
                dve.wait_ge(norm, n + 1)
                dve.tensor_reduce(am[0:T, bass.ds(n, 1)], xt, AX.X, ALU.max, apply_absolute_value=True).then_inc(amax, 1)
            dve.wait_ge(amax, NT)
            dve.tensor_reduce(am1[:, 0:1], am[:, :], AX.X, ALU.max).then_inc(scale, 1)
            dve.wait_ge(scale, 3)
            dve.tensor_scalar(sx, am1[:, 1:2], 1.0 / QMAX, 1e-12, ALU.mult, ALU.max).then_inc(scale, 1)
            dve.wait_ge(scale, 4)
            dve.reciprocal(rs[:, :], sx).then_inc(scale, 1)
            dve.wait_ge(scale, 5)
            with dve.Fori(0, NT // 2) as i:
                for p in range(2):
                    n = i * 2 + p
                    dve.tensor_scalar(qb[:, p, :], xn[:, bass.ds(n, 1), :].rearrange("p a d -> p (a d)"),
                                      rs[0:T, :], MAGIC, ALU.mult, ALU.add).then_inc(biased, 1)
                    dve.wait_ge(biased, n + 1)
                    dve.tensor_scalar(qi[:, p, :], qb[:, p, :], -MAGIC, None, ALU.add).then_inc(rounded, 1)
                    dve.wait_ge(hi_done, n + 1)
                    dve.tensor_tensor(xq_lo[:, :, bass.ds(n * T, T)], view(ps, p), f32(xq_hi[:, :, bass.ds(n * T, T)]),
                                      ALU.subtract).then_inc(lo_done, 1)

        @block.tensor
        def _(pe):
            pe.wait_ge(ident_done, 2)
            with pe.Fori(0, NT // 2) as i:
                for p in range(2):
                    n = i * 2 + p
                    pe.wait_ge(rounded, n + 1)
                    for c in range(C):
                        mm = pe.transpose(ps[:, p, c * T:(c + 1) * T], qi[:, p, c * P:(c + 1) * P], ident[0:T, 0:T])
                    mm.then_inc(turned, 1)

        @block.scalar
        def _(act):
            with act.Fori(0, NT // 2) as i:
                for p in range(2):
                    n = i * 2 + p
                    act.wait_ge(turned, n + 1)
                    act.activation(xq_hi[:, :, bass.ds(n * T, T)], view(ps, p), ACT.Identity).then_inc(hi_done, 1)


class WeightTiles:

    def __init__(self, ph):
        NB = D // WBLOCK
        self.raw = ph.sb("w_raw", [P, 2, D])
        self.bmax, self.bs, self.br = ph.sb("w_bmax", [P, NB]), ph.sb("w_bs", [P, NB]), ph.sb("w_br", [P, NB])
        self.q1, self.q2 = ph.sb("w_q1", [P, D]), ph.sb("w_q2", [P, D])
        self.deq = ph.sb("w_deq", [P, D])
        self.hi = [ph.sb(f"w_hi{i}", [P, C, P], F32R) for i in range(2)]
        self.lo = [ph.sb(f"w_lo{i}", [P, C, P], F32R) for i in range(2)]
        self.ps = ph.ps("w_ps", [P, C, P])
        self.loaded = ph.sems("w_loaded", 2)
        self.step = ph.sem("w_step")
        self.turned, self.hi_done, self.lo_done = ph.sem("w_turned"), ph.sem("w_hi_done"), ph.sem("w_lo_done")
    STEPS = 6

    def load(self, sp, src, n, p):
        sp.wait_ge(self.lo_done, n - p)
        sp.dma_start(self.raw[:, p, :], src).then_inc(self.loaded[p], 16)

    def dequantise(self, dve, n, half, p):
        def blocks(ap):
            return ap.rearrange("p (a w) -> p a w", w=WBLOCK)

        done = 0

        def link(ins):
            nonlocal done
            ins.then_inc(self.step, 1)
            done += 1
            dve.wait_ge(self.step, n * self.STEPS + done)

        wide = [P, D // WBLOCK, WBLOCK]
        dve.wait_ge(self.loaded[p], half * 16 + 16)
        link(dve.tensor_reduce(self.bmax[:, :], blocks(self.raw[:, p, :]), AX.X, ALU.max, apply_absolute_value=True))
        link(dve.tensor_scalar(self.bs[:, :], self.bmax[:, :], 1.0 / WMAX, 1e-12, ALU.mult, ALU.max))
        link(dve.reciprocal(self.br[:, :], self.bs[:, :]))
        link(dve.tensor_tensor(blocks(self.q1[:, :]), blocks(self.raw[:, p, :]),
                               self.br[:, :].unsqueeze(2).to_broadcast(wide), ALU.mult))
        link(dve.tensor_scalar(self.q2[:, :], self.q1[:, :], MAGIC, -MAGIC, ALU.add, ALU.add))
        dve.wait_ge(self.turned, n)
        dve.tensor_tensor(blocks(self.deq[:, :]), blocks(self.q2[:, :]),
                          self.bs[:, :].unsqueeze(2).to_broadcast(wide), ALU.mult).then_inc(self.step, 1)

    def transpose(self, pe, n, ident):
        pe.wait_ge(self.step, n * self.STEPS + self.STEPS)
        pe.wait_ge(self.lo_done, n)
        for c in range(C):
            mm = pe.transpose(self.ps[:, c, :], self.deq[:, c * P:(c + 1) * P], ident[:, :])
        mm.then_inc(self.turned, 1)

    def split_hi(self, act, n, p):
        act.wait_ge(self.turned, n + 1)
        act.activation(self.hi[p][:, :, :], self.ps[:, :, :], ACT.Identity).then_inc(self.hi_done, 1)

    def split_lo(self, dve, n, p):
        dve.wait_ge(self.hi_done, n + 1)
        dve.tensor_tensor(self.lo[p][:, :, :], self.ps[:, :, :], f32(self.hi[p][:, :, :]),
                          ALU.subtract).then_inc(self.lo_done, 1)


def up_and_gate(nc, w_up, w_gate, w_down, xq_hi, xq_lo, sx, gate, umax, gmax, up_scr, down_scr):
    NTOK = B * S
    NG, GT = 4, NTOK // 4
    JD = 12
    with Phase(nc, "ug") as ph:
        w = WeightTiles(ph)
        ust = [ph.sb(f"ust{p}", [P, NTOK]) for p in range(2)]
        ident = ph.sb("ident", [P, P])
        ps = ph.ps("ps", [P, 4, 512])
        ident_done, product, kept, amax = ph.sem("ident_done"), ph.sem("product"), ph.sem("kept"), ph.sem("amax")
        u_stored, d_stored = ph.sems("u_stored", 2), ph.sems("d_stored", 2)
        credit = ph.sb("credit", [P, 2])
        block = ph.block()

        def source(ap, n):
            return ap[bass.ds(n * P, P), :]

        def store_down(sp, m):
            o, i = m // 3, m % 3
            sp.wait_ge(w.lo_done, 2 * FI + m + 1)
            for part, t in enumerate((w.hi, w.lo)):
                sp.dma_start(down_scr[part, :, i * C:(i + 1) * C, o * P:(o + 1) * P],
                             f32(t[m % 2][:, :, :])).then_inc(d_stored[m % 2], 16)

        @block.sync
        def _(sp):
            for k, ap in enumerate((w_up, w_gate)):
                with sp.Fori(0, FI // 2) as i:
                    for p in range(2):
                        w.load(sp, source(ap, i * 2 + p), i * 2 + (k * FI + p), p)
            for m in range(JD):
                n = 2 * FI + m
                o, i = m // 3, m % 3
                w.load(sp, w_down[o * P:(o + 1) * P, i * D:(i + 1) * D], n, m % 2)
                if m >= 1:
                    store_down(sp, m - 1)
            store_down(sp, JD - 1)
            for p in range(2):
                sp.wait_ge(u_stored[p], 16 * FI // 2)
                sp.wait_ge(d_stored[p], 32 * JD // 2)

        @block.gpsimd
        def _(pool):
            identity(pool, ident, ident_done)
            with pool.Fori(0, FI // 2) as i:
                for p in range(2):
                    pool.wait_ge(kept, i * (2 * NG) + (p * NG + 2 * NG))
                    pool.dma_start(up_scr[bass.ds(i * 2 + p, 1)].rearrange("a p s -> p (a s)"),
                                   ust[p][:, :]).then_inc(u_stored[p], 16)

        @block.tensor
        def _(pe):
            pe.wait_ge(ident_done, 2)
            w.transpose(pe, 0, ident)
            with pe.Fori(0, FI) as i:
                for p in range(2):
                    n = i * 2 + p
                    pe.wait_ge(w.lo_done, n + 1)
                    for t in range(NG):
                        if t == NG // 2:
                            w.transpose(pe, n + 1, ident)
                        pe.wait_ge(kept, n * NG + (t + 1))
                        tok = slice(t * GT, (t + 1) * GT)
                        three_passes(pe, ps[:, t, 0:GT], lambda a, c: (w.hi, w.lo)[a][p][:, c, :],
                                     lambda a, c: (xq_hi, xq_lo)[a][:, c, tok]).then_inc(product, 1)
            for m in range(1, JD):
                w.transpose(pe, 2 * FI + m, ident)

        @block.scalar
        def _(act):
            w.split_hi(act, 0, 0)
            for k in range(2):
                with act.Fori(0, FI // 2) as i:
                    for p in range(2):
                        j = i * 2 + p
                        n = j + k * FI
                        if k == 0:
                            act.wait_ge(u_stored[p], i * 16)
                            act.wait_ge(amax, n * NG)
                        for t in range(NG):
                            if t == NG // 2:
                                w.split_hi(act, n + 1, 1 - p)
                            act.wait_ge(product, n * NG + (t + 1))
                            out = (ust[p][:, t * GT:(t + 1) * GT] if k == 0 else
                                   gate[:, bass.ds(j, 1), t * GT:(t + 1) * GT].rearrange("p a s -> p (a s)"))
                            act.activation(out, ps[:, t, 0:GT], ACT.Copy, scale=sx).then_inc(kept, 1)
            for m in range(1, JD):
                if m >= 2:
                    act.wait_ge(d_stored[m % 2], 32 * (m // 2))
                else:
                    act.wait_ge(product, 2 * FI * NG)
                w.split_hi(act, 2 * FI + m, m % 2)

        @block.vector
        def _(dve):
            dve.memset(credit[:, 0:1], 0.0).then_inc(kept, NG)
            dve.memset(credit[:, 1:2], 0.0).then_inc(amax, NG)
            w.dequantise(dve, 0, 0, 0)
            w.split_lo(dve, 0, 0)
            for k in range(2):
                with dve.Fori(0, FI // 2) as i:
                    for p in range(2):
                        j = i * 2 + p
                        n = j + k * FI
                        w.dequantise(dve, n + 1, i + (k * FI // 2 + p), 1 - p)
                        for t in range(NG):
                            if t == NG // 2:
                                w.split_lo(dve, n + 1, 1 - p)
                            dve.wait_ge(kept, n * NG + (NG + t + 1))
                            val = (ust[p][:, t * GT:(t + 1) * GT] if k == 0 else
                                   gate[:, bass.ds(j, 1), t * GT:(t + 1) * GT].rearrange("p a s -> p (a s)"))
                            dve.tensor_reduce((umax, gmax)[k][:, bass.ds(j * NG + t, 1)], val, AX.X,
                                              ALU.max, apply_absolute_value=True).then_inc(amax, 1)
            for m in range(1, JD):
                w.dequantise(dve, 2 * FI + m, FI + m // 2, m % 2)
                w.split_lo(dve, 2 * FI + m, m % 2)


def scale_of(link, dve, amax, unit, scale, inverse, tmp):
    if unit is None:
        link(dve.tensor_scalar(scale, amax, 1.0 / QMAX, 1e-12, ALU.mult, ALU.max))
        link(dve.reciprocal(inverse, scale))
    else:
        link(dve.tensor_scalar(tmp, amax, unit, 1.0 / QMAX, ALU.mult, ALU.mult))
        link(dve.tensor_scalar(scale, tmp, 1e-12, None, ALU.max))
        link(dve.reciprocal(tmp, scale))
        link(dve.tensor_tensor(inverse, tmp, unit, ALU.mult))


def activation_and_down(nc, x_scr, up_scr, down_scr, gate, umax, gmax, sx, out):
    NTOK = B * S
    NH, HT = 2, NTOK // 2
    HTT = HT // T
    with Phase(nc, "ad") as ph:
        wd = [ph.sb(f"wd{x_}", [P, FI, D], F32R) for x_ in "hl"]
        ust = [ph.sb(f"ust{p}", [P, NTOK]) for p in range(2)]
        sig = [ph.sb(f"sig{p}", [P, NTOK]) for p in range(2)]
        am = ph.sb("am", [P, 8])
        sc = ph.sb("sc", [P, 16])
        jmax, jmax2 = ph.sb("jmax", [P, FI]), ph.sb("jmax2", [P, FI])
        bias = ph.sb("bias", [P, 2])
        oh = [ph.sb(f"oh{p}", [P, HT], F32R) for p in range(2)]
        ol = [ph.sb(f"ol{p}", [P, HT], F32R) for p in range(2)]
        xt, yt = ph.sb("xt", [T, 2, D]), ph.sb("yt", [T, 2, D])
        ps = ph.ps("ps", [P, HTT, 512])
        wd_loaded, u_loaded = ph.sem("wd_loaded"), ph.sems("u_loaded", 2)
        st, reduced = ph.sem("st"), ph.sem("reduced")
        passed = ph.sem("passed")
        g_biased, g_round, sig_done, sig_round, silu, silu_max = (ph.sem(n) for n in (
            "g_biased", "g_round", "sig_done", "sig_round", "silu", "silu_max"))
        s_biased, u_biased, o_min, prod, prod_max = (ph.sem(n) for n in (
            "s_biased", "u_biased", "o_min", "prod", "prod_max"))
        o_biased, o_round, o_hi, o_lo, mm_done = (ph.sem(n) for n in ("o_biased", "o_round", "o_hi", "o_lo", "mm_done"))
        x_loaded, y_done, y_stored = ph.sems("x_loaded", 2), ph.sem("y_done"), ph.sems("y_stored", 2)
        SILU_ST = 3 + 2 + 2 + 1
        PROD_ST = SILU_ST + 4 + 1 + 1
        credit = ph.sb("credit", [P, 4])
        block = ph.block()
        su, ru, sg, rg, ss, rs, us, so, ro, t0 = (sc[:, i:i + 1] for i in range(10))

        def tile(ap, j):
            return ap[:, bass.ds(j, 1), :].rearrange("p a s -> p (a s)")

        @block.sync
        def _(sp):
            sp.dma_start(f32(wd[0][:, :, :]), down_scr[0]).then_inc(wd_loaded, 16)
            sp.dma_start(f32(wd[1][:, :, :]), down_scr[1]).then_inc(wd_loaded, 16)
            with sp.Fori(0, FI // 2) as i:
                for p in range(2):
                    sp.wait_ge(prod, i * 2 + p)
                    sp.dma_start(ust[p][:, :], up_scr[bass.ds(i * 2 + p, 1)].rearrange(
                        "a p s -> p (a s)")).then_inc(u_loaded[p], 16)
            for n in range(2 * HTT):
                if n >= 2:
                    sp.wait_ge(y_done, n - 1)
                sp.dma_start(xt[:, n % 2, :], x_scr[n * T:(n + 1) * T, :]).then_inc(x_loaded[n % 2], 16)
                if n >= 1:
                    sp.wait_ge(y_done, n)
                    sp.dma_start(out[(n - 1) * T:n * T, :], yt[:, (n - 1) % 2, :]).then_inc(y_stored[(n - 1) % 2], 16)
            n = 2 * HTT
            sp.wait_ge(y_done, n)
            sp.dma_start(out[(n - 1) * T:n * T, :], yt[:, (n - 1) % 2, :]).then_inc(y_stored[(n - 1) % 2], 16)
            for p in range(2):
                sp.wait_ge(y_stored[p], 16 * HTT)

        @block.gpsimd
        def _(pool):
            for k, made in enumerate((2, 3, SILU_ST, PROD_ST)):
                pool.wait_ge(st, made)
                pool.partition_all_reduce(am[:, 4 + k:5 + k], am[:, k:k + 1], P, RMAX).then_inc(reduced, 1)
                if k < 3:
                    pool.wait_ge(reduced, k + 1)

        @block.scalar
        def _(act):
            act.wait_ge(st, SILU_ST - 1)
            with act.Fori(0, FI // 2) as i:
                for p in range(2):
                    j = i * 2 + p
                    act.activation(tile(gate, j), tile(gate, j), ACT.Identity, bias=bias[:, 0:1],
                                   scale=rg).then_inc(g_biased, 1)
                    act.wait_ge(g_round, j + 1)
                    act.wait_ge(silu, j)
                    act.sem_inc(passed, 1)
                    act.activation(sig[p][:, :], tile(gate, j), ACT.Sigmoid, scale=sg).then_inc(sig_done, 1)
            act.wait_ge(st, PROD_ST - 1)
            with act.Fori(0, FI // 2) as i:
                for p in range(2):
                    j = i * 2 + p
                    act.wait_ge(u_loaded[p], i * 16 + 16)
                    act.activation(ust[p][:, :], ust[p][:, :], ACT.Identity, bias=bias[:, 0:1],
                                   scale=ru).then_inc(u_biased, 1)
                    act.activation(tile(gate, j), tile(gate, j), ACT.Identity, bias=bias[:, 0:1],
                                   scale=rs).then_inc(s_biased, 1)
            for h in range(NH):
                with act.Fori(0, FI // 2) as i:
                    for p in range(2):
                        j = i * 2 + p
                        k = j + h * FI
                        act.wait_ge(o_round, k + 1)
                        act.wait_ge(mm_done, k)
                        act.activation(oh[p][:, :], gate[:, bass.ds(j, 1), h * HT:(h + 1) * HT].rearrange(
                            "p a s -> p (a s)"), ACT.Identity).then_inc(o_hi, 1)

        @block.vector
        def _(dve):
            count = [0]

            def link(ins):
                ins.then_inc(st, 1)
                count[0] += 1
                dve.wait_ge(st, count[0])

            dve.memset(credit[:, 0:1], 0.0).then_inc(silu, 1)
            dve.memset(credit[:, 1:2], 0.0).then_inc(prod, 1)
            dve.memset(credit[:, 2:3], 0.0).then_inc(mm_done, 1)
            link(dve.memset(bias[:, :], MAGIC))
            link(dve.tensor_reduce(am[:, 0:1], umax, AX.X, ALU.max))
            link(dve.tensor_reduce(am[:, 1:2], gmax, AX.X, ALU.max))
            dve.wait_ge(reduced, 2)
            scale_of(link, dve, am[:, 4:5], None, su, ru, t0)
            scale_of(link, dve, am[:, 5:6], None, sg, rg, t0)
            assert count[0] == SILU_ST - 1
            with dve.Fori(0, FI // 2) as i:
                for p in range(2):
                    j = i * 2 + p
                    dve.wait_ge(g_biased, j + 1)
                    dve.tensor_scalar(tile(gate, j), tile(gate, j), -MAGIC, None, ALU.add).then_inc(g_round, 1)
                    dve.wait_ge(sig_done, j + 1)
                    dve.tensor_scalar(sig[p][:, :], sig[p][:, :], 65535.0 / 65536.0, MAGIC16,
                                      ALU.min, ALU.add).then_inc(sig_round, 1)
                    dve.wait_ge(sig_round, j + 1)
                    dve.scalar_tensor_tensor(tile(gate, j), sig[p][:, :], MAGIC16, tile(gate, j),
                                             ALU.subtract, ALU.mult).then_inc(silu, 1)
                    dve.wait_ge(silu, j + 2)
                    dve.tensor_reduce(jmax[:, bass.ds(j, 1)], tile(gate, j), AX.X, ALU.max,
                                      apply_absolute_value=True).then_inc(silu_max, 1)
            dve.wait_ge(silu_max, FI)
            link(dve.tensor_reduce(am[:, 2:3], jmax[:, :], AX.X, ALU.max))
            dve.wait_ge(reduced, 3)
            scale_of(link, dve, am[:, 6:7], sg, ss, rs, t0)
            link(dve.tensor_tensor(us, ss, su, ALU.mult))
            assert count[0] == PROD_ST - 1
            with dve.Fori(0, FI // 2) as i:
                for p in range(2):
                    j = i * 2 + p
                    dve.wait_ge(u_biased, j + 1)
                    dve.tensor_scalar(ust[p][:, :], ust[p][:, :], -MAGIC, None, ALU.add).then_inc(o_min, 1)
                    dve.wait_ge(s_biased, j + 1)
                    dve.wait_ge(o_min, j + 1)
                    dve.scalar_tensor_tensor(tile(gate, j), tile(gate, j), MAGIC, ust[p][:, :],
                                             ALU.subtract, ALU.mult).then_inc(prod, 1)
                    dve.wait_ge(prod, j + 2)
                    dve.tensor_reduce(jmax2[:, bass.ds(j, 1)], tile(gate, j), AX.X, ALU.max,
                                      apply_absolute_value=True).then_inc(prod_max, 1)
            dve.wait_ge(prod_max, FI)
            link(dve.tensor_reduce(am[:, 3:4], jmax2[:, :], AX.X, ALU.max))
            dve.wait_ge(reduced, 4)
            scale_of(link, dve, am[:, 7:8], us, so, ro, t0)
            for h in range(NH):
                with dve.Fori(0, FI // 2) as i:
                    for p in range(2):
                        j = i * 2 + p
                        k = j + h * FI
                        o = gate[:, bass.ds(j, 1), h * HT:(h + 1) * HT].rearrange("p a s -> p (a s)")
                        dve.tensor_scalar(o, o, ro, MAGIC, ALU.mult, ALU.add).then_inc(o_biased, 1)
                        dve.wait_ge(o_biased, k + 1)
                        dve.tensor_scalar(o, o, -MAGIC, None, ALU.add).then_inc(o_round, 1)
                        dve.wait_ge(o_hi, k + 1)
                        dve.tensor_tensor(ol[p][:, :], o, f32(oh[p][:, :]), ALU.subtract).then_inc(o_lo, 1)
                dve.wait_ge(mm_done, h * FI + (FI + 1))
                for t in range(HTT):
                    n = h * HTT + t
                    dve.wait_ge(x_loaded[n % 2], 16 * (n // 2 + 1))
                    if n >= 2:
                        dve.wait_ge(y_stored[n % 2], 16 * (n // 2))
                    dve.scalar_tensor_tensor(yt[:, n % 2, :], ps[0:T, t, :], so[0:T, :], xt[:, n % 2, :],
                                             ALU.mult, ALU.add).then_inc(y_done, 1)

        @block.tensor
        def _(pe):
            pe.wait_ge(wd_loaded, 32)
            for h in range(NH):
                if h:
                    pe.wait_ge(y_done, h * HTT)
                def tile_products(j, p, first, last):
                    pe.wait_ge(o_lo, j + (h * FI + 1))
                    for t in range(HTT):
                        tok = slice(t * T, (t + 1) * T)
                        for n, (a, b) in enumerate(((oh, 0), (oh, 1), (ol, 0))):
                            mm = pe.matmul(ps[0:T, t, :], a[p][:, tok], tile(wd[b], j),
                                           start=first and n == 0, stop=last and n == 2)
                    mm.then_inc(mm_done, 1)

                tile_products(0, 0, True, False)
                tile_products(1, 1, False, False)
                with pe.Fori(1, FI // 2 - 1) as i:
                    for p in range(2):
                        tile_products(i * 2 + p, p, False, False)
                tile_products(FI - 2, 0, False, False)
                tile_products(FI - 1, 1, False, True)


def quantised_ffn(nc, x_stack, x, w_up, w_gate, w_down, x_scr, up_scr, down_scr, out):
    NTOK = B * S
    with Phase(nc, "ff") as outer:
        sx = outer.sb("sx", [P, 1])[:, :]
        umax, gmax = outer.sb("umax", [P, FI * 4])[:, :], outer.sb("gmax", [P, FI * 4])[:, :]
        with Phase(nc, "xq") as ph:
            xq_hi, xq_lo = ph.sb("hi", [P, C, NTOK], F32R), ph.sb("lo", [P, C, NTOK], F32R)
            quantised_input(nc, x, x_scr, xq_hi, xq_lo, sx)
            x_stack.close()
            gate = x_stack.enter_context(nc.sbuf_tensor("gate", [P, FI, NTOK], F32, side="right"))
            up_and_gate(nc, w_up, w_gate, w_down, xq_hi, xq_lo, sx, gate, umax, gmax, up_scr, down_scr)
        activation_and_down(nc, x_scr, up_scr, down_scr, gate, umax, gmax, sx, out)
        x_stack.close()


def build(nc, x, ctx_t, mask, mask_t, keypad, keypad_t, wq0, bq0, wk0, wv0, wo0, bo0, wgate, ln_scale, ln_bias,
          w1, b1, w2, b2, wq1, wk1, wv1, bqk1, bv1, wka1, wva1, wo1, bo1, g, bk_ctx, bv_ctx,
          w_gate, w_up, w_down, out):
    def scratch(name, *shape):
        return nc.dram_tensor(name, shape, F32).ap()

    k_ctx, v_ctx = scratch("k_ctx", 2, 2, B, D, S2), scratch("v_ctx", 2, B, S2, H * VW)
    q0, qk1 = scratch("q0", 1, 2, D, B * S), scratch("qk1", 2, 2, D, B * S)
    v_self = scratch("v_self", B * S, H * VW)
    x_scr = scratch("x_scr", B * S, D)
    up_scr, down_scr = scratch("up_scr", FI, P, B * S), scratch("down_scr", 2, P, FI, D)

    def ctx_source(layer):
        return (S2, lambda b, part: k_ctx[layer, part, bass.ds(b, 1)].rearrange("b n k -> (b n) k"),
                lambda b: v_ctx[layer, bass.ds(b, 1)].rearrange("b k n -> (b k) n"))

    self_source = (S, lambda b, part: qk1[1, part][:, bass.ds(b * S, S)],
                   lambda b: v_self[bass.ds(b * S, S), :])

    x_stack = ExitStack()
    xr = x_stack.enter_context(nc.sbuf_tensor("x_res", [T, NT, D], F32, side="right"))
    ctx_projections(nc, ctx_t, [wk0, wv0, wka1, wva1], bk_ctx, bv_ctx, k_ctx, v_ctx)
    token_projections(nc, "q0", xr, x, [wq0], bq0, None, q0, None)
    attention(nc, "a0", xr, q0[0], [ctx_source(0)], wo0, bo0, masks=(mask, mask_t, keypad, keypad_t))
    experts(nc, xr, wgate, ln_scale, ln_bias, w1, b1, w2, b2)
    token_projections(nc, "q1", xr, None, [wq1, wk1, wv1], bqk1, bv1, qk1, v_self)
    attention(nc, "a1", xr, qk1[0], [self_source, ctx_source(1)], wo1, bo1, gates=g)
    quantised_ffn(nc, x_stack, xr, w_up, w_gate, w_down, x_scr, up_scr, down_scr, out)


def kernel(**inputs):
    import numpy as np
    import concourse.bacc as bacc
    from concourse.bass_utils import run_bass_kernel_spmd

    a = {name: np.asarray(value) for name, value in inputs.items()}

    def chunks(w):
        return w.reshape(w.shape[0] // 128, 128, -1).transpose(1, 0, 2)

    def per_partition(b, n):
        return b.reshape(n, 4, 128).transpose(2, 0, 1)

    def spread(b, rows):
        return np.broadcast_to(b, (rows,) + b.shape)

    Bs, Ss, Dm = a["x"].shape
    keys = a["ctx_1024"].shape[1]
    padded = -(-keys // 128) * 128
    mask = a["mask_BxSxS2_bf0"]
    keypad = a["mask_BxS2_bf0"]
    keypad_t = np.zeros((Bs, padded), bool)
    keypad_t[:, :keys] = keypad
    w_self, b_self = a["L1_xattn_Wqkv"], a["L1_xattn_bqkv"]
    w_aux, b_aux = a["L1_xattn_Wqkv_aux"], a["L1_xattn_bqkv_aux"]
    laid = [
        a["x"].reshape(Bs * Ss, Dm),
        a["ctx_1024"].transpose(0, 2, 1).reshape(Bs, Dm // 128, 128, keys).transpose(0, 2, 1, 3),
        mask, mask.transpose(0, 2, 1), keypad, keypad_t.reshape(Bs, padded // 128, 128).transpose(2, 0, 1),
        chunks(a["L0_xattn_Wq"].T), per_partition(a["L0_xattn_bq"], 1),
        chunks(a["L0_xattn_Wk"].T), chunks(a["L0_xattn_Wv"].T),
        chunks(a["L0_xattn_Wo"].T), spread(a["L0_xattn_bo"], 112),
        chunks(a["L0_ffn_Wg"].T), chunks(a["L0_ffn_ln_scale"].T), chunks(a["L0_ffn_ln_bias"].T),
        a["L0_ffn_W1"].reshape(8, 4, 128, 128).transpose(2, 0, 1, 3), a["L0_ffn_b1"].T,
        a["L0_ffn_W2"].transpose(1, 0, 2), a["L0_ffn_b2"],
        chunks(w_self[:, :Dm]), chunks(w_self[:, Dm:2 * Dm]), chunks(w_self[:, 2 * Dm:]),
        per_partition(b_self[:2 * Dm], 2), spread(b_self[2 * Dm:], 128),
        chunks(w_aux[:, Dm:2 * Dm]), chunks(w_aux[:, 2 * Dm:]),
        chunks(a["L1_xattn_Wo"]), spread(a["L1_xattn_bo"], 112), spread(a["L1_xattn_g"], 112),
        per_partition(np.concatenate([a["L0_xattn_bk"], b_aux[Dm:2 * Dm]]), 2),
        spread(np.stack([a["L0_xattn_bv"], b_aux[2 * Dm:]]), 128),
        a["L1_ffn_w_gate"], a["L1_ffn_w_up"], a["L1_ffn_w_down"],
    ]
    nc = bacc.Bacc("TRN2", target_bir_lowering=False, num_devices=1)
    arrays, args = {}, []
    for i, array in enumerate(laid):
        array = np.ascontiguousarray(array)
        arrays[f"in_{i}"] = array
        args.append(nc.dram_tensor(f"in_{i}", array.shape, mybir.dt.from_np(array.dtype),
                                   kind="ExternalInput").ap())
    out = nc.dram_tensor("out", (Bs * Ss, Dm), F32, kind="ExternalOutput").ap()
    build(nc, *args, out)
    result = run_bass_kernel_spmd(nc, [arrays], core_ids=[0])
    return result.results[0]["out"].reshape(Bs, Ss, Dm)
```

```python
from contextlib import ExitStack

import concourse.bass as bass
from concourse import mybir

F32 = mybir.dt.float32
F32R = mybir.dt.float32r
BF16 = mybir.dt.bfloat16
U8 = mybir.dt.uint8
ALU = mybir.AluOpType
ACT = mybir.ActivationFunctionType
AX = mybir.AxisListType
RMAX = bass.bass_isa.ReduceOp.max

P = 128
B, S, D, S2 = 8, 224, 512, 750
H, DH = 16, 32
HG = P // DH
G = H // HG
C = D // P
T = 112
TB = S // T
NT = B * TB
KC = (S2 + P - 1) // P
SP2 = KC * P
VB = 3 * (H // 2)
VW = VB * DH
E, HID = 8, 128
FF = 1536
FI = FF // P
EPS = 1e-5
MASKED = -float(2.0 ** 100)
TINY = 1e-30
SCALE = float(DH) ** -0.5


def f32(ap):
    return ap.bitcast(F32)


class Phase:

    def __init__(self, nc, name):
        self.nc, self.name, self.stack, self.semaphores = nc, name, ExitStack(), []

    def __enter__(self):
        self.stack.__enter__()
        return self

    def __exit__(self, *e):
        self.stack.__exit__(*e)
        if self.semaphores:
            self.nc.clear_and_free_semaphores(self.semaphores)
            self.nc.all_engine_barrier()

    def sb(self, name, shape, dt=F32):
        return self.stack.enter_context(self.nc.sbuf_tensor(f"{self.name}_{name}", shape, dt))

    def ps(self, name, shape, dt=F32):
        return self.stack.enter_context(self.nc.psum_tensor(f"{self.name}_{name}", shape, dt))

    def sem(self, name, start=0):
        self.semaphores.append(self.nc.alloc_semaphore(f"{self.name}_{name}"))
        if start:
            self.nc.gpsimd.sem_inc(self.semaphores[-1], start)
        return self.semaphores[-1]

    def sems(self, name, n, start=0):
        return [self.sem(f"{name}{i}", start) for i in range(n)]

    def block(self):
        return self.stack.enter_context(self.nc.Block())


class SplitWeights:

    def __init__(self, ph, weights, raw_cols=C * D):
        self.src = weights
        self.hi = [ph.sb(f"w{i}h", [P, w.shape[1], w.shape[2]], F32R) for i, w in enumerate(weights)]
        self.lo = [ph.sb(f"w{i}l", [P, w.shape[1], w.shape[2]], F32R) for i, w in enumerate(weights)]
        self.raw = ph.sb("wraw", [P, 2, raw_cols])
        self.loaded = ph.sems("w_loaded", 2)
        self.hi_done = ph.sem("w_hi_done")
        self.lo_done = ph.sem("w_lo_done")

    def raw_of(self, i):
        w = self.src[i]
        return self.raw[:, i % 2, 0:w.shape[1] * w.shape[2]].rearrange("p (c n) -> p c n", c=w.shape[1])

    def load(self, sp):
        for i, w in enumerate(self.src):
            if i >= 2:
                sp.wait_ge(self.lo_done, i - 1)
            sp.dma_start(self.raw_of(i), w).then_inc(self.loaded[i % 2], 16)

    def split_hi(self, act):
        for i in range(len(self.src)):
            act.wait_ge(self.loaded[i % 2], 16 * (i // 2 + 1))
            act.activation(self.hi[i][:, :, :], self.raw_of(i), ACT.Identity).then_inc(self.hi_done, 1)

    def split_lo(self, dve):
        for i in range(len(self.src)):
            dve.wait_ge(self.hi_done, i + 1)
            dve.tensor_tensor(self.lo[i][:, :, :], self.raw_of(i), f32(self.hi[i][:, :, :]),
                              ALU.subtract).then_inc(self.lo_done, 1)

    def wait(self, pe):
        pe.wait_ge(self.lo_done, len(self.src))


def three_passes(pe, out, lhs, rhs, start=True, stop=True):
    for c in range(C):
        for k, (a, b) in enumerate(((0, 0), (0, 1), (1, 0))):
            last = pe.matmul(out, lhs(a, c), rhs(b, c), start=start and c == 0 and k == 0,
                             stop=stop and c == C - 1 and k == 2)
    return last


def value_blocks(ap):
    return ap.rearrange("p (a k) w -> p a k w", k=3)[:, :, 0:3:2, :]


def ctx_projections(nc, ctx_t, weights, bk, bv, k_scr, v_scr):
    HALF = (376, 374)
    PER = 2 * G * 2 + 2 * KC
    BANKS = 8
    with Phase(nc, "cp") as ph:
        w = SplitWeights(ph, weights)
        raw = ph.sb("raw", [P, C, S2])
        ctxs = [[ph.sb(f"ctx{p}{x}", [P, C, S2], F32R) for x in "hl"] for p in range(2)]
        kst = [ph.sb(f"kst{i}", [P, 2, S2], F32R) for i in range(G)]
        vst = ph.sb("vst", [P, 4, VB, DH])
        bk_sb = ph.sb("bk", [P, 2, G])
        bv_sb = ph.sb("bv", [P, 2, D])
        ps = ph.ps("ps", [P, BANKS, 512])
        consts = ph.sem("consts")
        raw_loaded, ctx_split = ph.sem("raw_loaded"), ph.sem("ctx_split", start=1)
        tile_ready, bank_free = ph.sem("tile_ready", start=1), ph.sem("bank_free")
        passed = ph.sem("passed")
        hi_done = ph.sem("hi_done")
        k_stored, v_stored = ph.sems("k_stored", G, start=1), ph.sems("v_stored", 4, start=1)
        split_hi = ph.sem("split_hi")
        credit = ph.sb("credit", [P, 2])
        ones = ph.sem("ones")
        block = ph.block()

        @block.sync
        def _(sp):
            sp.dma_start(bk_sb[:, :, :], bk).then_inc(consts, 16)
            sp.dma_start(bv_sb[:, :, :], bv).then_inc(consts, 16)
            w.load(sp)
            with sp.Fori(0, B // 2) as i:
                for p in range(2):
                    b = i * 2 + p
                    for l in range(2):
                        for g in range(G):
                            sp.wait_ge(bank_free, b * PER + (l * 2 * G + 2 * g + 2 + BANKS))
                            sp.dma_start(k_scr[l, :, bass.ds(b, 1), g * P:(g + 1) * P, :].rearrange(
                                "x b p k -> p (x b) k"), f32(kst[g][:, :, :])).then_inc(k_stored[g], 16)
                    for v in range(2 * KC):
                        m = min(P, S2 - v % KC * P)
                        sp.wait_ge(bank_free, b * PER + (4 * G + v + 1 + BANKS))
                        sp.dma_start(v_scr[v // KC, bass.ds(b, 1), v % KC * P:v % KC * P + m, :].rearrange(
                            "b k n -> (b k) n"), vst[0:m, v % 4, :, :].rearrange("p h w -> p (h w)")).then_inc(
                                v_stored[v % 4], 16)
            for g in range(G):
                sp.wait_ge(k_stored[g], 1 + 16 * 2 * B)
            for s in range(4):
                sp.wait_ge(v_stored[s], 1 + 16 * 2 * KC * B // 4)

        @block.gpsimd
        def _(pool):
            with pool.Fori(0, B // 2) as i:
                for p in range(2):
                    b = i * 2 + p
                    pool.wait_ge(ctx_split, 1 + b)
                    pool.dma_start(raw[:, :, :], ctx_t[bass.ds(b, 1)].rearrange(
                        "b p c k -> p (b c) k")).then_inc(raw_loaded, 16)
                    pool.wait_ge(raw_loaded, b * 16 + 16)
                    pool.wait_ge(tile_ready, 1 + b * PER)
                    pool.sem_inc(passed, 1)
                    pool.tensor_copy(ctxs[p][0][:, :, :], raw[:, :, :]).then_inc(split_hi, 1)
                    pool.wait_ge(split_hi, b + 1)
                    pool.tensor_tensor(ctxs[p][1][:, :, :], raw[:, :, :], f32(ctxs[p][0][:, :, :]),
                                       ALU.subtract).then_inc(ctx_split, 1)

        @block.tensor
        def _(pe):
            w.wait(pe)
            with pe.Fori(0, B // 2) as i:
                for p in range(2):
                    b = i * 2 + p
                    pe.wait_ge(ctx_split, 1 + b + 1)
                    n = 0
                    for l in range(2):
                        wk = (w.hi[2 * l], w.lo[2 * l])
                        for g in range(G):
                            for half in range(2):
                                pe.wait_ge(bank_free, b * PER + (n + 1))
                                lo = half * HALF[0]
                                three_passes(pe, ps[:, (p * PER + n) % BANKS, 0:HALF[half]],
                                             lambda a, c: wk[a][:, c, g * P:(g + 1) * P],
                                             lambda a, c: ctxs[p][a][:, c, lo:lo + HALF[half]]).then_inc(tile_ready, 1)
                                n += 1
                    for l in range(2):
                        wv = (w.hi[2 * l + 1], w.lo[2 * l + 1])
                        for k in range(KC):
                            m = min(P, S2 - k * P)
                            pe.wait_ge(bank_free, b * PER + (n + 1))
                            last = three_passes(pe, ps[0:m, (p * PER + n) % BANKS, :],
                                                lambda a, c: ctxs[p][a][:, c, k * P:k * P + m],
                                                lambda a, c: wv[a][:, c, :])
                            last.then_inc(tile_ready, 1)
                            n += 1

        @block.scalar
        def _(act):
            w.split_hi(act)
            act.wait_ge(consts, 32)
            with act.Fori(0, B // 2) as i:
                for p in range(2):
                    b = i * 2 + p
                    for l in range(2):
                        for g in range(G):
                            act.wait_ge(k_stored[g], 1 + b * 32 + 16 * l)
                            for half in range(2):
                                n = (l * G + g) * 2 + half
                                lo = half * HALF[0]
                                act.wait_ge(tile_ready, 1 + b * PER + (PER + n + 1))
                                act.activation(kst[g][:, 0, lo:lo + HALF[half]],
                                               ps[:, (p * PER + n) % BANKS, 0:HALF[half]], ACT.Identity,
                                               bias=bk_sb[:, l, g:g + 1]).then_inc(hi_done, 1)

        @block.vector
        def _(dve):
            dve.memset(vst[:, :, :, :], 1.0).then_inc(ones, 1)
            dve.memset(credit[:, 0:1], 0.0).then_inc(bank_free, BANKS)
            dve.memset(credit[:, 1:2], 0.0).then_inc(tile_ready, PER)
            w.split_lo(dve)
            dve.wait_ge(consts, 32)
            dve.wait_ge(ones, 1)
            with dve.Fori(0, B // 2) as i:
                for p in range(2):
                    b = i * 2 + p
                    for l in range(2):
                        for g in range(G):
                            for half in range(2):
                                n = (l * G + g) * 2 + half
                                lo = half * HALF[0]
                                dve.wait_ge(hi_done, b * 4 * G + (n + 1))
                                dve.scalar_tensor_tensor(
                                    kst[g][:, 1, lo:lo + HALF[half]], ps[:, (p * PER + n) % BANKS, 0:HALF[half]],
                                    bk_sb[:, l, g:g + 1], f32(kst[g][:, 0, lo:lo + HALF[half]]),
                                    ALU.add, ALU.subtract).then_inc(bank_free, 1)
                    for v in range(2 * KC):
                        m = min(P, S2 - v % KC * P)
                        n = 4 * G + v
                        dve.wait_ge(v_stored[v % 4], 1 + b * (16 * 2 * KC // 4) + 16 * (v // 4))
                        dve.wait_ge(tile_ready, 1 + b * PER + (PER + n + 1))
                        dve.tensor_tensor(
                            value_blocks(vst[0:m, v % 4, :, :]),
                            ps[0:m, (p * PER + n) % BANKS, :].rearrange("p (a k d) -> p a k d", k=2, d=DH),
                            bv_sb[0:m, v // KC, :].rearrange("p (a k d) -> p a k d", k=2, d=DH),
                            ALU.add).then_inc(bank_free, 1)


class LayerNormStats:

    def __init__(self, ph, twice=False):
        self.twice = twice
        self.st = ph.sb("ln_st", [T, NT, 6])
        self.t = [ph.sb(f"ln_t{i}", [T, NT]) for i in range(10)]
        self.mean, self.rstd = ph.sb("ln_mean", [T, NT]), ph.sb("ln_rstd", [T, NT])
        self.power = ph.sb("ln_power", [T, NT])
        self.stat = ph.sem("ln_stat")
        self.pow_ready = ph.sem("ln_pow_ready")
        self.count = NT

    def chain(self, dve, ins):
        ins.then_inc(self.stat, 1)
        self.count += 1
        dve.wait_ge(self.stat, self.count)

    def on_vector(self, dve, x):
        m_even, m_odd, v_even, v_odd = (self.st[:, :, i] for i in (1, 4, 2, 5))
        t = [a[:, :] for a in self.t]
        with dve.Fori(0, NT) as n:
            dve.bn_stats(self.st[:, bass.ds(n, 1), :].rearrange("p a s -> p (a s)"),
                         x[:, bass.ds(n, 1), :].rearrange("p a d -> p (a d)")).then_inc(self.stat, 1)
        dve.wait_ge(self.stat, NT)
        self.chain(dve, dve.tensor_tensor(t[0], m_even, m_odd, ALU.add))
        self.chain(dve, dve.tensor_scalar(self.mean[:, :], t[0], 0.5, None, ALU.mult))
        self.chain(dve, dve.tensor_tensor(t[1], m_even, m_odd, ALU.subtract))
        self.chain(dve, dve.scalar_tensor_tensor(t[2], t[1], 0.25, t[1], ALU.mult, ALU.mult))
        self.chain(dve, dve.tensor_tensor(t[3], v_even, v_odd, ALU.add))
        self.chain(dve, dve.scalar_tensor_tensor(t[4], t[3], 1.0 / D, t[2], ALU.mult, ALU.add))
        self.chain(dve, dve.tensor_scalar(t[5], t[4], EPS, None, ALU.add))
        self.var_done = self.count
        if self.twice:
            dve.wait_ge(self.pow_ready, 2)
            self.chain(dve, dve.tensor_tensor(t[6], t[4], t[9], ALU.mult))
            self.chain(dve, dve.tensor_tensor(t[7], t[6], t[9], ALU.mult))
            self.chain(dve, dve.tensor_scalar(t[8], t[7], EPS, None, ALU.add))
            dve.wait_ge(self.pow_ready, 3)
            self.chain(dve, dve.tensor_tensor(self.rstd[:, :], t[9], self.t[6][:, :], ALU.mult))
        else:
            dve.wait_ge(self.pow_ready, 2)

    def on_pool(self, pool):
        t = [a[:, :] for a in self.t]
        pool.memset(self.power[:, :], -0.5).then_inc(self.pow_ready, 1)
        pool.wait_ge(self.pow_ready, 1)
        pool.wait_ge(self.stat, NT + 7)
        first = t[9] if self.twice else self.rstd[:, :]
        pool.tensor_tensor(first, t[5], self.power[:, :], ALU.pow).then_inc(self.pow_ready, 1)
        if self.twice:
            pool.wait_ge(self.stat, NT + 10)
            pool.tensor_tensor(t[6], t[8], self.power[:, :], ALU.pow).then_inc(self.pow_ready, 1)

    def normalise(self, dve, out, x, n):
        return dve.tensor_scalar(out, x[:, bass.ds(n, 1), :].rearrange("p a d -> p (a d)"),
                                 self.mean[:, bass.ds(n, 1)], self.rstd[:, bass.ds(n, 1)],
                                 ALU.subtract, ALU.mult)


def identity(pool, ident, done):
    pool.memset(ident[:, :], 0.0).then_inc(done, 1)
    pool.wait_ge(done, 1)
    pool.affine_select(out=ident[:, :], in_=ident[:, :], compare_op=ALU.not_equal, fill=1.0, base=0,
                       pattern=[[-1, P]], channel_multiplier=1).then_inc(done, 1)


def batch_pairs(engine, body):
    with engine.Fori(0, B // 2 - 1) as i:
        for p in range(2):
            body(i * 2 + p, p, False)
    for p in range(2):
        body(B - 2 + p, p, p == 1)


class TransposedTokens:

    def __init__(self, ph, ln):
        self.ln = ln
        self.xn = [ph.sb(f"xn{p}", [T, TB, D]) for p in range(2)]
        self.xt = [[ph.sb(f"xt{p}{x}", [P, C, S], F32R) for x in "hl"] for p in range(2)]
        self.ps = ph.ps("xt_ps", [P, 2, 512])
        self.ident = ph.sb("ident", [P, P])
        self.ident_done = ph.sem("ident_done")
        self.xn_ready, self.xt_ready = ph.sem("xn_ready"), ph.sem("xt_ready")
        self.hi, self.lo = ph.sem("xt_hi"), ph.sem("xt_lo", start=1)

    def ps_view(self):
        return self.ps[:, :, 0:2 * S]

    def xt_view(self, p, part):
        return self.xt[p][part][:, :, :].rearrange("p (a c) s -> p a (c s)", a=2)

    def dve_normalise(self, dve, x, b, p):
        for t in range(TB):
            self.ln.normalise(dve, self.xn[p][:, t, :], x, b * TB + t).then_inc(self.xn_ready, 1)

    def pe_transpose(self, pe, b, p):
        pe.wait_ge(self.xn_ready, b * TB + TB)
        pe.wait_ge(self.lo, 1 + b)
        for t in range(TB):
            for c in range(C):
                last = pe.transpose(self.ps[:, c // 2, c % 2 * S + t * T:c % 2 * S + (t + 1) * T],
                                    self.xn[p][:, t, c * P:(c + 1) * P], self.ident[0:T, 0:T])
        last.then_inc(self.xt_ready, 1)

    def act_hi(self, act, b, p):
        act.wait_ge(self.xt_ready, b + 1)
        act.activation(self.xt_view(p, 0), self.ps_view(), ACT.Identity).then_inc(self.hi, 1)

    def dve_lo(self, dve, b, p):
        dve.wait_ge(self.hi, b + 1)
        dve.tensor_tensor(self.xt_view(p, 1), self.ps_view(), f32(self.xt_view(p, 0)),
                          ALU.subtract).then_inc(self.lo, 1)


def token_projections(nc, name, x, x_src, weights, bq, bv, q_scr, v_scr):
    NP = 1 if len(weights) == 1 else 2
    with_v = len(weights) == 3
    PER = NP * G + (TB if with_v else 0)
    BANKS = 4
    with Phase(nc, name) as ph:
        w = SplitWeights(ph, weights)
        ln = LayerNormStats(ph)
        tt = TransposedTokens(ph, ln)
        stage = [ph.sb(f"stage{i}", [P, 2, S], F32R) for i in range(G)]
        vst = ph.sb("vst", [T, TB, VB, DH])
        bq_sb = ph.sb("bq", [P, NP, G])
        bv_sb = ph.sb("bv", [P, D])
        ps = ph.ps("ps", [P, BANKS, 512])
        credit = ph.sb("credit", [P, 2])
        consts, x_loaded, ones = ph.sem("consts"), ph.sem("x_loaded"), ph.sem("ones")
        tile_ready, bank_free, hi_done = ph.sem("tile_ready", start=1), ph.sem("bank_free"), ph.sem("hi_done")
        stored, v_stored = ph.sems("stored", G, start=1), ph.sems("v_stored", TB, start=1)
        block = ph.block()
        n_x = 0

        @block.sync
        def _(sp):
            if x_src is not None:
                sp.dma_start(x[:, :, :], x_src.rearrange("(n p) d -> p n d", p=T)).then_inc(x_loaded, 16)
            w.load(sp)
            sp.dma_start(bq_sb[:, :, :], bq).then_inc(consts, 16)
            if with_v:
                sp.dma_start(bv_sb[:, :], bv).then_inc(consts, 16)

            with sp.Fori(0, B) as b:
                for i in range(NP):
                    for g in range(G):
                        sp.wait_ge(bank_free, b * PER + (i * G + g + 1 + BANKS))
                        sp.dma_start(q_scr[i, :, g * P:(g + 1) * P, bass.ds(b * S, S)].rearrange(
                            "x p s -> p x s"), f32(stage[g][:, :, :])).then_inc(stored[g], 16)
                if with_v:
                    for t in range(TB):
                        sp.wait_ge(bank_free, b * PER + (NP * G + t + 1 + BANKS))
                        sp.dma_start(v_scr[bass.ds(b * S + t * T, T), :],
                                     vst[:, t, :, :].rearrange("p h w -> p (h w)")).then_inc(v_stored[t], 16)
            for g in range(G):
                sp.wait_ge(stored[g], 1 + 16 * B * NP)
            if with_v:
                for t in range(TB):
                    sp.wait_ge(v_stored[t], 1 + 16 * B)

        @block.gpsimd
        def _(pool):
            identity(pool, tt.ident, tt.ident_done)
            ln.on_pool(pool)

        @block.tensor
        def _(pe):
            pe.wait_ge(tt.ident_done, 2)
            tt.pe_transpose(pe, 0, 0)
            w.wait(pe)

            def body(b, p, last):
                if not last:
                    tt.pe_transpose(pe, b + 1, 1 - p)
                pe.wait_ge(tt.lo, 1 + b + 1)
                n = 0
                for i in range(NP):
                    for g in range(G):
                        pe.wait_ge(bank_free, b * PER + (n + 1))
                        three_passes(pe, ps[:, (p * PER + n) % BANKS, 0:S],
                                     lambda a, c: (w.hi[i], w.lo[i])[a][:, c, g * P:(g + 1) * P],
                                     lambda a, c: tt.xt[p][a][:, c, :]).then_inc(tile_ready, 1)
                        n += 1
                for t in range(TB if with_v else 0):
                    pe.wait_ge(bank_free, b * PER + (n + 1))
                    three_passes(pe, ps[0:T, (p * PER + n) % BANKS, :],
                                 lambda a, c: tt.xt[p][a][:, c, t * T:(t + 1) * T],
                                 lambda a, c: (w.hi[2], w.lo[2])[a][:, c, :]).then_inc(tile_ready, 1)
                    n += 1
            batch_pairs(pe, body)

        @block.scalar
        def _(act):
            w.split_hi(act)
            act.wait_ge(consts, 16 * (2 if with_v else 1))
            tt.act_hi(act, 0, 0)

            def body(b, p, last):
                if not last:
                    act.wait_ge(tile_ready, 1 + b * PER)
                    tt.act_hi(act, b + 1, 1 - p)
                for n in range(NP * G):
                    act.wait_ge(stored[n % G], 1 + b * 16 * NP + 16 * (n // G))
                    act.wait_ge(tile_ready, 1 + b * PER + (n + 1))
                    act.activation(stage[n % G][:, 0, :], ps[:, (p * PER + n) % BANKS, 0:S], ACT.Identity,
                                   bias=bq_sb[:, n // G, n % G:n % G + 1]).then_inc(hi_done, 1)
            batch_pairs(act, body)

        @block.vector
        def _(dve):
            dve.memset(vst[:, :, :, :], 1.0).then_inc(ones, 1)
            dve.memset(credit[:, 0:1], 0.0).then_inc(bank_free, BANKS)
            if x_src is not None:
                dve.wait_ge(x_loaded, 16)
            ln.on_vector(dve, x)
            tt.dve_normalise(dve, x, 0, 0)
            w.split_lo(dve)
            tt.dve_lo(dve, 0, 0)
            dve.wait_ge(ones, 1)
            dve.wait_ge(consts, 16 * (2 if with_v else 1))

            def body(b, p, last):
                if not last:
                    dve.wait_ge(tile_ready, 1 + b * PER)
                    tt.dve_normalise(dve, x, b + 1, 1 - p)
                    tt.dve_lo(dve, b + 1, 1 - p)
                for n in range(NP * G):
                    dve.wait_ge(hi_done, b * NP * G + (n + 1))
                    dve.scalar_tensor_tensor(stage[n % G][:, 1, :], ps[:, (p * PER + n) % BANKS, 0:S],
                                             bq_sb[:, n // G, n % G:n % G + 1], f32(stage[n % G][:, 0, :]),
                                             ALU.add, ALU.subtract).then_inc(bank_free, 1)
                for t in range(TB if with_v else 0):
                    n = NP * G + t
                    dve.wait_ge(v_stored[t], 1 + b * 16)
                    dve.wait_ge(tile_ready, 1 + b * PER + (n + 1))
                    dve.tensor_tensor(value_blocks(vst[:, t, :, :]),
                                      ps[0:T, (p * PER + n) % BANKS, :].rearrange("p (a k d) -> p a k d", k=2, d=DH),
                                      bv_sb[0:T, :].rearrange("p (a k d) -> p a k d", k=2, d=DH),
                                      ALU.add).then_inc(bank_free, 1)
            batch_pairs(dve, body)


def attention(nc, name, x, q_scr, sources, wo, bo, masks=None, gates=None):
    NSRC = len(sources)
    units = [(src, g) for g in range(G) for src in range(NSRC)]
    NU = len(units)
    NBUF = 4
    UNIT_SLOTS = 2 * HG + 1
    SLOTS = UNIT_SLOTS * NU + 2
    FIRST = 2 * UNIT_SLOTS - 1
    LOADS = 8
    NM = 2 + TB + KC
    with Phase(nc, name) as ph:
        w = SplitWeights(ph, [wo])
        kst = [ph.sb(f"kst{i}", [97, HG, SP2], F32R) for i in range(NBUF)]
        qst = [ph.sb(f"qst{i}", [97, HG, S], F32R) for i in range(NBUF)]
        vst = [ph.sb(f"vst{i}", [P, KC, VB // G, DH]) for i in range(NBUF)]
        prob = [ph.sb(f"prob{i}", [P, KC, S]) for i in range(2)]
        raw = ph.sb("raw", [P, 2 * S])
        dens, rden = ph.sb("dens", [P, 2 * S]), ph.sb("rden", [P, 2 * S])
        logd, defect = ph.sb("logd", [P, 2 * S]), ph.sb("defect", [P, 2 * S])
        rneg = ph.sb("rneg", [P, 2 * S])
        tiny = ph.sb("tiny", [P, 1])
        OUT_AT, SUM_AT = (slice(0, DH), slice(3 * DH, 4 * DH)), (slice(DH, 2 * DH), slice(2 * DH, 3 * DH))
        osb = ph.sb("osb", [P, G, S])
        part = ph.sb("part", [P, S])
        ot = [ph.sb(f"ot{x}", [P, C, S], F32R) for x in "hl"]
        mx = [ph.sb(f"mx{i}", [T, 2 * HG]) for i in range(2)]
        mrow = [ph.sb(f"mrow{i}", [2 * HG, T], F32R) for i in range(2)]
        ident, ident_b = ph.sb("ident", [P, P]), ph.sb("ident_b", [P, P], BF16)
        bo_sb = ph.sb("bo", [T, D])
        credit = ph.sb("credit", [P, 4])
        slot = ph.ps("slot", [P, 2, 1024])
        st_ps = ph.ps("st_ps", [P, 3, 512])
        o_ps = ph.ps("o_ps", [P, 512])
        ident_done, consts, init = ph.sem("ident_done"), ph.sem("consts"), ph.sem("init")
        loaded = ph.sems("loaded", NBUF)
        slot_ready, slot_free = ph.sem("slot_ready"), ph.sem("slot_free")
        passed = ph.sem("passed")
        m_stored = ph.sems("m_stored", 2)
        st_ready, exp_done, pv_done = ph.sem("st_ready"), ph.sem("exp_done", start=1), ph.sem("pv_done")
        o_free, final, step_done = ph.sem("o_free", start=1), ph.sem("final", start=1), ph.sem("step_done")
        ot_hi, ot_lo, x_biased = ph.sem("ot_hi"), ph.sem("ot_lo"), ph.sem("x_biased")
        sums_copied, logs, inverted, refined = (ph.sem(n) for n in ("sums_copied", "logs", "inverted", "refined"))
        if masks:
            mb = [ph.sb(f"mb{i}", [T, TB, S2], BF16) for i in range(2)]
            mbt = [ph.sb(f"mbt{i}", [P, KC, S], BF16) for i in range(2)]
            m_raw, mt_raw = ph.sb("m_raw", [T, TB, S2], U8), ph.sb("mt_raw", [P, KC, S], U8)
            kp_raw, kpt_raw = ph.sb("kp_raw", [T, S2], U8), ph.sb("kpt_raw", [P, KC], U8)
            kpb, kptb = ph.sb("kpb", [T, S2], BF16), ph.sb("kptb", [P, KC])
            mask_loaded, mask_conv = ph.sem("mask_loaded"), ph.sem("mask_conv", start=1)
        if gates is not None:
            gate_raw, gate = ph.sb("gate_raw", [P, H]), [ph.sb(f"gate{i}", [P, H]) for i in range(3)]
            gate_done = ph.sem("gate_done")
        CREDIT = 4 * HG
        pads = [(keys, -(-keys // P) * P) for keys, _, _ in sources]
        PER_BUF = NU // NBUF

        def slot_of(ui, item, h=0, t=0):
            at = FIRST + ui * UNIT_SLOTS + (2 if ui else 0)
            if item == "T":
                return at
            if item == "B":
                return at + UNIT_SLOTS + t
            return at + 1 + 2 * h + t

        def last_slot(t):
            return slot_of(NU - 2, "T") + 1 + t

        def ahead(b, p, ui, d, last):
            if ui + d < NU:
                return b, p, ui + d
            return None if last else (b + 1, 1 - p, ui + d - NU)

        def steps(engine, step, tail):
            step(0, 0, 0, False, True)

            def body(b, p, last):
                for ui in range(1, NU):
                    step(b, p, ui, last, False)
                if last:
                    tail(b, p)
                else:
                    step(b + 1, 1 - p, 0, False, False)
            batch_pairs(engine, body)

        CONVERT = [(NU - 3, h) for h in range(HG)] + [(NU - 2, 0), (NU - 2, 1)]
        LINKS = [HG if src else 0 for src, g in units]
        INIT = 2 + NBUF * len(pads) + (1 if masks else 0)
        block = ph.block()

        @block.sync
        def _(sp):
            w.load(sp)
            sp.dma_start(bo_sb[:, :], bo).then_inc(consts, 16)
            if gates is not None:
                sp.dma_start(gate_raw[:, :], gates).then_inc(consts, 16)
            sp.wait_ge(init, INIT)
            sp.wait_ge(ident_done, 3 + G)

            def body(b, p, last):
                if masks:
                    sp.wait_ge(mask_conv, 1 + b * NM)
                    sp.sem_inc(passed, 1)
                    attn_mask, attn_mask_t, key_mask, key_mask_t = masks
                    full = KC - 1
                    sp.dma_start(m_raw[:, :, :], attn_mask[bass.ds(b, 1)].rearrange(
                        "b (t p) k -> p (b t) k", p=T)).then_inc(mask_loaded, 16)
                    sp.dma_start(mt_raw[:, 0:full, :], attn_mask_t[bass.ds(b, 1), 0:full * P, :].rearrange(
                        "b (c p) s -> p (b c) s", p=P)).then_inc(mask_loaded, 16)
                    sp.dma_start(mt_raw[0:S2 - full * P, full, :], attn_mask_t[
                        bass.ds(b, 1), full * P:S2, :].rearrange("b p s -> p (b s)")).then_inc(mask_loaded, 16)
                    sp.dma_start(kp_raw[:, :], key_mask[bass.ds(b, 1), :].to_broadcast([T, S2])).then_inc(
                        mask_loaded, 16)
                    sp.dma_start(kpt_raw[:, :], key_mask_t[:, bass.ds(b, 1), :].rearrange(
                        "p b c -> p (b c)")).then_inc(mask_loaded, 16)
                for ui, (src, g) in enumerate(units):
                    keys, k_of, v_of = sources[src]
                    full = (keys - 1) // P
                    sp.wait_ge(pv_done, b * NU * HG + HG * (ui + 1))
                    kh = [k_of(b, part)[g * P:(g + 1) * P, :].rearrange("(h d) k -> d h k", h=HG) for part in (0, 1)]
                    qh = [q_scr[part, g * P:(g + 1) * P, bass.ds(b * S, S)].rearrange("(h d) s -> d h s", h=HG)
                          for part in (0, 1)]
                    buf = ui % NBUF
                    for row, part in enumerate((0, 1, 0)):
                        sp.dma_start(f32(kst[buf][row * DH:(row + 1) * DH, :, 0:keys]), kh[part]).then_inc(loaded[buf], 16)
                    for row, part in enumerate((0, 0, 1)):
                        sp.dma_start(f32(qst[buf][row * DH:(row + 1) * DH, :, :]), qh[part]).then_inc(loaded[buf], 16)
                    v = v_of(b)[:, g * (VW // G):(g + 1) * (VW // G)]
                    sp.dma_start(vst[buf][:, 0:full, :, :].rearrange("p c h w -> p c (h w)"), v[0:full * P, :].rearrange(
                        "(c p) w -> p c w", p=P)).then_inc(loaded[buf], 16)
                    sp.dma_start(vst[buf][0:keys - full * P, full, :, :].rearrange("p h w -> p (h w)"), v[full * P:keys, :]).then_inc(loaded[buf], 16)
            with sp.Fori(0, B) as b:
                body(b, 0, False)

        @block.gpsimd
        def _(pool):
            identity(pool, ident, ident_done)
            pool.wait_ge(ident_done, 2)
            pool.tensor_copy(ident_b[:, :], ident[:, :]).then_inc(ident_done, 1)
            for g in range(NBUF):
                pool.wait_ge(ident_done, 3 + g)
                pool.memset(f32(kst[g][96:97, :, :]), 1.0).then_inc(ident_done, 1)

            def m_rows(b, ui, number):
                pool.wait_ge(slot_free, number + 3)
                pool.sem_inc(passed, 1)
                pool.dma_start(f32(qst[ui % NBUF][96:97, :, :]).rearrange("a h (t s) -> a (h t) s", t=TB),
                               f32(mrow[ui % 2][:, :])).then_inc(m_stored[ui % 2], 16)
            m_rows(0, 0, 2 * HG)

            def step(b, p, ui, last, first):
                if (nxt := ahead(b, p, ui, 1, last)):
                    m_rows(nxt[0], nxt[2], b * SLOTS + slot_of(ui, "T"))
            steps(pool, step, lambda b, p: None)

        @block.tensor
        def _(pe):
            pe.wait_ge(ident_done, 3)

            def score_tiles(b, p, ui, h, n0, more=0):
                keys, k, q = sources[units[ui][0]][0], kst[ui % NBUF], qst[ui % NBUF]
                for t in range(TB):
                    pe.wait_ge(slot_free, n0 + (t + 1))
                    par = (parity0 + t) % 2
                    for lo in range(0, keys, 512):
                        n = min(512, keys - lo)
                        last = pe.matmul(slot[0:T, par, lo:lo + n], q[0:96, h, t * T:(t + 1) * T],
                                         k[0:96, h, lo:lo + n], start=True, stop=not masks)
                        if masks:
                            last = pe.matmul(slot[0:T, par, lo:lo + n], ident_b[0:T, 0:T],
                                             mb[p][:, t, lo:lo + n], start=False, stop=True)
                    last.then_inc(slot_ready, 1 + (more if t == TB - 1 else 0))

            def transpose_maxima(ui, number, par):
                pe.wait_ge(slot_free, number + 2)
                pe.transpose(slot[0:2 * HG, par, 0:T], mx[ui % 2][:, :], ident[0:T, 0:T]).then_inc(slot_ready, 1)

            def unit_loaded(b, ui):
                pe.wait_ge(loaded[ui % NBUF], b * (16 * LOADS * PER_BUF) + 16 * LOADS * (ui // NBUF + 1))

            def transposed_scores(b, p, ui, h):
                keys, k, q = sources[units[ui][0]][0], kst[ui % NBUF], qst[ui % NBUF]
                nch = (keys + P - 1) // P
                at = 0
                if nch > 2 or h == 0:
                    pe.wait_ge(exp_done, b * NU * HG + (1 + ui * HG + h))
                elif h == 3:
                    pe.wait_ge(exp_done, b * NU * HG + (1 + ui * HG + 1))
                if nch <= 2:
                    at = h % 3
                for c in range(nch):
                    out = st_ps[:, at + c // 2, c % 2 * S:c % 2 * S + S]
                    mm = pe.matmul(out, k[:, h, c * P:(c + 1) * P], q[:, h, :], start=True, stop=not masks)
                    if masks:
                        mm = pe.matmul(out, ident_b[:, :], mbt[p][:, c, :], start=False, stop=True)
                mm.then_inc(st_ready, 1)

            def probabilities_times_v(n, ui, h):
                keys, v = sources[units[ui][0]][0], vst[ui % NBUF]
                nch = (keys + P - 1) // P
                pe.wait_ge(exp_done, n + 1)
                at, first = h % 2 * 2 * DH, h // 2 * 3 + h % 2
                for c in range(nch):
                    m = min(P, keys - c * P)
                    mm = pe.matmul(o_ps[at:at + 2 * DH, h // 2 * S:(h // 2 + 1) * S],
                                   v[0:m, c, first:first + 2, :].rearrange("p h w -> p (h w)"), prob[h % 2][0:m, c, :],
                                   start=c == 0, stop=c == nch - 1)
                mm.then_inc(pv_done, 1)

            def outputs_times_wo(number, b, t, par):
                if t == 0:
                    pe.wait_ge(ot_lo, b + 1)
                pe.wait_ge(slot_free, number + 1)
                three_passes(pe, slot[0:T, par, 0:D], lambda a, c: ot[a][:, c, t * T:(t + 1) * T],
                             lambda a, c: (w.hi[0], w.lo[0])[a][:, c, :]).then_inc(slot_ready, 1)

            unit_loaded(0, 0)
            if masks:
                pe.wait_ge(mask_conv, 1 + NM)
            parity0 = 0
            for h in range(HG):
                score_tiles(0, 0, 0, h, 2 * h)
            transpose_maxima(0, 2 * HG, 0)
            unit_loaded(0, 1)
            parity0 = 1
            for h in range(HG):
                score_tiles(0, 0, 1, h, 2 * HG + 1 + 2 * h)
            w.wait(pe)

            def step(b, p, ui, last, first):
                nonlocal parity0
                nxt, nxt2 = ahead(b, p, ui, 1, last), ahead(b, p, ui, 2, last)
                if nxt2:
                    unit_loaded(nxt2[0], nxt2[2])
                    if masks and nxt2[2] == 0:
                        pe.wait_ge(mask_conv, nxt2[0] * NM + (1 + 2 + TB))
                if masks and ui == 0:
                    pe.wait_ge(mask_conv, b * NM + (1 + NM))
                pe.wait_ge(m_stored[ui % 2], b * (8 * NU) + 16 * (ui // 2 + 1))
                for h in range(HG):
                    k = b * NU * HG + (ui * HG + h)
                    transposed_scores(b, p, ui, h)
                    if h == 0 and nxt:
                        n = slot_of(ui, "T")
                        transpose_maxima(nxt[2], b * SLOTS + n, n % 2)
                    if not (first and h == 0):
                        if h == 1 and not first:
                            pe.wait_ge(o_free, b * NU + (ui + 1))
                        probabilities_times_v(k, (ui - (h == 0)) % NU, (h - 1) % HG)
                    if nxt2:
                        n = slot_of(ui, "tile", h)
                        parity0 = n % 2
                        score_tiles(*nxt2, h, b * SLOTS + n, 2 if first and h == HG - 1 else 0)
                    if ui == 0 and h == HG - 1 and not first:
                        for t in range(TB):
                            n = slot_of(0, "B", t=t)
                            outputs_times_wo(b * SLOTS + n, b - 1, t, n % 2)

            def tail(b, p):
                probabilities_times_v(B * NU * HG, NU - 1, HG - 1)
                for t in range(TB):
                    n = last_slot(t)
                    outputs_times_wo(b * SLOTS + n, b, t, n % 2)
            steps(pe, step, tail)

        @block.scalar
        def _(act):
            if gates is not None:
                act.wait_ge(consts, 32)
                act.activation(gate[0][:, :], gate_raw[:, :], ACT.Exp, scale=-1.0).then_inc(gate_done, 1)
            w.split_hi(act)
            act.wait_ge(init, 2)

            def outputs_from_psum(b, ui):
                act.wait_ge(pv_done, b * NU * HG + (CREDIT + HG * (ui + 1)))
                act.wait_ge(final, b * NU + (1 + ui))
                for at, sums in zip(OUT_AT, SUM_AT):
                    act.activation(dens[at, :], o_ps[sums, 0:2 * S], ACT.Identity,
                                   bias=tiny[sums, :]).then_inc(sums_copied, 1)
                act.activation(raw[:, :], o_ps[:, 0:2 * S], ACT.Identity).then_inc(o_free, 1)
                act.wait_ge(sums_copied, b * (2 * NU) + (2 * ui + 2))
                act.activation(logd[:, :], dens[:, :], ACT.Ln).then_inc(logs, 1)
                act.wait_ge(logs, b * NU + (ui + 1))
                act.activation(rden[:, :], logd[:, :], ACT.Exp, scale=-1.0).then_inc(inverted, 1)

            def outputs_hi(b):
                act.wait_ge(final, b * NU + (1 + NU))
                act.activation(ot[0][:, :, :], osb[:, :, :], ACT.Identity).then_inc(ot_hi, 1)

            def step(b, p, ui, last, first):
                nch = (sources[units[ui][0]][0] + P - 1) // P
                for h in range(HG):
                    k = ui * HG + h
                    at = h % 3 if nch <= 2 else 0
                    act.wait_ge(st_ready, b * NU * HG + (k + 1))
                    act.wait_ge(pv_done, b * NU * HG + (k + CREDIT - 1))
                    act.activation(prob[h % 2][:, 0:nch, :].rearrange("p (a c) s -> p a (c s)", c=2),
                                   st_ps[:, at:at + nch // 2, 0:2 * S], ACT.Exp, scale=SCALE).then_inc(exp_done, 1)
                    if h == 0 and ui:
                        outputs_from_psum(b, ui - 1)
                    elif h == 0 and not first:
                        outputs_from_psum(b - 1, NU - 1)
                    if ui == 0 and h == HG - 1 and not first:
                        outputs_hi(b - 1)

            def tail(b, p):
                outputs_from_psum(b, NU - 1)
                outputs_hi(b)
            steps(act, step, tail)

        @block.vector
        def _(dve):
            dve.memset(credit[:, 0:1], 0.0).then_inc(slot_free, 2)
            dve.memset(credit[:, 1:2], 0.0).then_inc(pv_done, CREDIT)
            dve.memset(tiny[:, :], TINY).then_inc(init, 1)
            dve.memset(dens[:, :], 1.0).then_inc(init, 1)
            for i in range(NBUF):
                for lo, hi in pads:
                    dve.memset(f32(kst[i][0:96, :, lo:hi]), 0.0).then_inc(init, 1)
            if masks:
                dve.memset(mt_raw[:, :, :].rearrange("p c s -> p (c s)"), 1).then_inc(init, 1)
            if gates is not None:
                dve.wait_ge(gate_done, 1)
                dve.tensor_scalar(gate[1][:, :], gate[0][:, :], 1.0, None, ALU.add).then_inc(gate_done, 1)
                dve.wait_ge(gate_done, 2)
                dve.reciprocal(gate[0][:, :], gate[1][:, :]).then_inc(gate_done, 1)
                dve.wait_ge(gate_done, 3)
                dve.tensor_scalar(gate[2][:, :], gate[0][:, :], -1.0, None, ALU.add).then_inc(gate_done, 1)
                dve.tensor_scalar(gate[1][:, :], gate[0][:, :], -1.0, None, ALU.mult).then_inc(gate_done, 1)
                dve.wait_ge(gate_done, 5)
            w.split_lo(dve)
            dve.wait_ge(consts, 16 * (2 if gates is not None else 1))
            with dve.Fori(0, NT) as n:
                xt = x[:, bass.ds(n, 1), :].rearrange("p a d -> p (a d)")
                dve.tensor_tensor(xt, xt, bo_sb[:, :], ALU.add).then_inc(x_biased, 1)

            def convert_masks(b, p, part):
                if part == 0:
                    dve.wait_ge(mask_loaded, b * 80 + 80)
                    dve.tensor_scalar(kpb[:, :], kp_raw[:, :], MASKED, None, ALU.mult).then_inc(mask_conv, 1)
                    dve.tensor_scalar(kptb[:, :], kpt_raw[:, :], MASKED, None, ALU.mult).then_inc(mask_conv, 1)
                elif part <= TB:
                    if part == 1:
                        dve.wait_ge(mask_conv, b * NM + 3)
                    dve.scalar_tensor_tensor(mb[p][:, part - 1, :], m_raw[:, part - 1, :], MASKED, kpb[:, :],
                                             ALU.mult, ALU.add).then_inc(mask_conv, 1)
                else:
                    for c in range((part - 1 - TB) * 2, (part - TB) * 2):
                        dve.tensor_scalar(mbt[p][:, c, :], mt_raw[:, c, :], MASKED, kptb[:, c:c + 1],
                                          ALU.mult, ALU.add).then_inc(mask_conv, 1)

            def maxima(ui, h, n0, par0, more=0):
                keys = sources[units[ui][0]][0]
                for t in range(TB):
                    dve.wait_ge(slot_ready, n0 + (t + 1))
                    dve.tensor_reduce(mx[ui % 2][:, h * TB + t:h * TB + t + 1], slot[0:T, (par0 + t) % 2, 0:keys],
                                      AX.X, ALU.max, negate=True).then_inc(slot_free, 1 + (more if t == TB - 1 else 0))

            def maxima_to_row(ui, number, par):
                dve.wait_ge(slot_ready, number + 1)
                if masks:
                    dve.tensor_scalar(mrow[ui % 2][:, :], slot[0:2 * HG, par, 0:T], -MASKED / 2, None,
                                      ALU.min).then_inc(slot_free, 1)
                else:
                    dve.tensor_copy(mrow[ui % 2][:, :], slot[0:2 * HG, par, 0:T]).then_inc(slot_free, 1)

            def finalise(b, ui):
                src, g = units[ui]
                done = sum(LINKS[:ui])

                def link(ins):
                    nonlocal done
                    ins.then_inc(step_done, 1)
                    done += 1

                dve.wait_ge(inverted, b * NU + (ui + 1))
                dve.tensor_tensor(defect[:, :], dens[:, :], rden[:, :], ALU.mult).then_inc(refined, 1)
                dve.wait_ge(refined, b * (2 * NU) + (2 * ui + 1))
                dve.scalar_tensor_tensor(rneg[:, :], defect[:, :], 2.0, rden[:, :],
                                         ALU.subtract, ALU.mult).then_inc(refined, 1)
                dve.wait_ge(refined, b * (2 * NU) + (2 * ui + 2))
                for h in range(HG):
                    at, cols = OUT_AT[h % 2], slice(h // 2 * S, (h // 2 + 1) * S)
                    rows = slice(h * DH, (h + 1) * DH)
                    dst = part[rows, :] if src else osb[rows, g, :]
                    if gates is not None:
                        n = g * HG + h
                        ins = dve.scalar_tensor_tensor(dst, raw[at, cols], gate[1 if src else 2][at, n:n + 1],
                                                       rneg[at, cols], ALU.mult, ALU.mult)
                    else:
                        ins = dve.scalar_tensor_tensor(dst, raw[at, cols], -1.0, rneg[at, cols], ALU.mult, ALU.mult)
                    if src:
                        link(ins)
                    elif h == HG - 1:
                        ins.then_inc(final, 1)
                if src:
                    dve.wait_ge(step_done, b * sum(LINKS) + done)
                    dve.tensor_tensor(osb[:, g, :], osb[:, g, :], part[:, :], ALU.add).then_inc(final, 1)

            def outputs_lo(batches):
                dve.wait_ge(ot_hi, batches)
                dve.tensor_tensor(ot[1][:, :, :], osb[:, :, :], f32(ot[0][:, :, :]), ALU.subtract).then_inc(ot_lo, 1)

            def add_outputs(number, par, b, t):
                dve.wait_ge(slot_ready, number + 1)
                xb = x[:, bass.ds(b * TB + t, 1), :].rearrange("p a d -> p (a d)")
                dve.tensor_tensor(xb, slot[0:T, par, 0:D], xb, ALU.add).then_inc(slot_free, 1)

            if masks:
                for part_ in range(6):
                    convert_masks(0, 0, part_)
            for h in range(HG):
                maxima(0, h, 2 * h, 0)
            maxima_to_row(0, 2 * HG, 0)
            for h in range(HG):
                maxima(1, h, 2 * HG + 1 + 2 * h, 1)

            def step(b, p, ui, last, first):
                nxt, nxt2 = ahead(b, p, ui, 1, last), ahead(b, p, ui, 2, last)
                if nxt:
                    n = slot_of(ui, "T")
                    maxima_to_row(nxt[2], b * SLOTS + n, n % 2)
                for h in range(HG):
                    if nxt2:
                        n = slot_of(ui, "tile", h)
                        maxima(nxt2[2], h, b * SLOTS + n, n % 2, 2 if first and h == HG - 1 else 0)
                    if h == 2 and ui:
                        finalise(b, ui - 1)
                    elif h == 2 and not first:
                        finalise(b - 1, NU - 1)
                    if masks and not last and (ui, h) in CONVERT:
                        convert_masks(b + 1, 1 - p, CONVERT.index((ui, h)))
                    if ui == 0 and h == HG - 1 and not first:
                        outputs_lo(b)
                    if ui == 0 and h == HG - 1 and not first:
                        for t in range(TB):
                            n = slot_of(0, "B", t=t)
                            add_outputs(b * SLOTS + n, n % 2, b - 1, t)

            def tail(b, p):
                finalise(b, NU - 1)
                outputs_lo(B)
                for t in range(TB):
                    n = last_slot(t)
                    add_outputs(b * SLOTS + n, n % 2, b, t)
            steps(dve, step, tail)


def experts(nc, x, wg, ln_scale, ln_bias, w1, b1, w2, b2):
    with Phase(nc, "ex") as ph:
        ln = LayerNormStats(ph, twice=True)
        tt = TransposedTokens(ph, ln)
        w1_raw = ph.sb("w1_raw", [P, 2, C, HID])
        w1_sc = ph.sb("w1_sc", [P, 2, C, HID])
        w1h, w1l = [ph.sb(f"w1{x_}", [P, E, C, HID], F32R) for x_ in "hl"]
        w2_raw = ph.sb("w2_raw", [P, 2, D])
        w2h, w2l = [ph.sb(f"w2{x_}", [P, E, D], F32R) for x_ in "hl"]
        wg_sb, sc_sb, bi_sb = ph.sb("wg", [P, C, E]), ph.sb("sc", [P, C, E]), ph.sb("bi", [P, C, E])
        wgh, wgl = [ph.sb(f"wg{x_}", [P, C, E], F32R) for x_ in "hl"]
        b1_sb, b1f = ph.sb("b1", [P, E]), ph.sb("b1f", [P, E])
        b2_sb = ph.sb("b2", [E, D])
        rank = ph.sb("rank", [T, TB, E])
        sel = ph.sb("sel", [E, E, P])
        logit = ph.sb("logit", [T, TB, E])
        top, pick, best = ph.sb("top", [T, TB]), ph.sb("pick", [T, TB, E]), ph.sb("best", [T, TB])
        is_top, hot = ph.sb("is_top", [T, TB, E]), ph.sb("hot", [T, TB, E])
        hot_t = ph.sb("hot_t", [E, S])
        hid = [ph.sb(f"hid{i}", [P, S]) for i in range(2)]
        hm = [ph.sb(f"hm{i}", [P, S]) for i in range(2)]
        hh = [[ph.sb(f"h{x_}{p}", [P, E, S], F32R) for x_ in "hl"] for p in range(2)]
        small = ph.ps("small", [P, 512])
        hid_ps = [ph.ps(f"hid_ps{i}", [P, 512]) for i in range(2)]
        y_ps = ph.ps("y_ps", [P, 2, 512])
        mask_ps = ph.ps("mask_ps", [P, 512])
        consts = ph.sem("consts")
        w1_loaded, w2_loaded = ph.sems("w1_loaded", 2), ph.sems("w2_loaded", 2)
        w1_scaled, w1_hi, w1_lo = ph.sem("w1_scaled"), ph.sem("w1_hi"), ph.sem("w1_lo")
        w2_hi, w2_lo = ph.sem("w2_hi"), ph.sem("w2_lo")
        bias_ready, bias_done, wg_hi, wg_lo = ph.sem("bias_ready"), ph.sem("bias_done"), ph.sem("wg_hi"), ph.sem("wg_lo")
        sel_done = ph.sem("sel_done")
        logit_ready, gate_step, hot_ready = ph.sem("logit_ready"), ph.sem("gate_step"), ph.sem("hot_ready")
        mask_ready, hid_ready, gelu_done = ph.sem("mask_ready"), ph.sem("hid_ready"), ph.sem("gelu_done", start=1)
        h_masked, h_hi, h_lo = ph.sem("h_masked", start=1), ph.sem("h_hi"), ph.sem("h_lo")
        y_ready, y_added = ph.sem("y_ready", start=1), ph.sem("y_added", start=1)
        block = ph.block()
        STEPS = 6

        @block.sync
        def _(sp):
            for dst, src in ((wg_sb[:, :, :], wg), (sc_sb[:, :, :], ln_scale), (bi_sb[:, :, :], ln_bias),
                             (b1_sb[:, :], b1), (b2_sb[:, :], b2)):
                sp.dma_start(dst, src).then_inc(consts, 16)
            for e in range(E):
                if e >= 2:
                    sp.wait_ge(w1_scaled, C * (e - 1))
                    sp.wait_ge(bias_ready, e - 1)
                    sp.wait_ge(w2_lo, e - 1)
                sp.dma_start(w1_raw[:, e % 2, :, :], w1[:, e, :, :]).then_inc(w1_loaded[e % 2], 16)
                sp.dma_start(w2_raw[:, e % 2, :], w2[:, e, :]).then_inc(w2_loaded[e % 2], 16)

        @block.gpsimd
        def _(pool):
            identity(pool, tt.ident, tt.ident_done)
            ln.on_pool(pool)
            pool.memset(sel[:, :, :], 0.0).then_inc(sel_done, 1)
            pool.wait_ge(sel_done, 1)
            pool.affine_select(out=sel[:, :, :], in_=sel[:, :, :], compare_op=ALU.not_equal, fill=1.0, base=0,
                               pattern=[[-1, E], [0, P]], channel_multiplier=1).then_inc(sel_done, 1)
            for e in range(E):
                pool.memset(rank[:, :, e:e + 1], float(E - e)).then_inc(sel_done, 1)
                pool.wait_ge(sel_done, 3 + e)

        @block.tensor
        def _(pe):
            pe.wait_ge(tt.ident_done, 2)
            pe.wait_ge(consts, 80)
            for e in range(E):
                pe.wait_ge(w1_loaded[e % 2], 16 * (e // 2 + 1))
                for c in range(C):
                    mm = pe.matmul(small[:, e:e + 1], w1_raw[:, e % 2, c, :], bi_sb[:, c, e:e + 1],
                                   start=c == 0, stop=c == C - 1)
                mm.then_inc(bias_ready, 1)
            tt.pe_transpose(pe, 0, 0)

            def body(b, p, last):
                if not last:
                    tt.pe_transpose(pe, b + 1, 1 - p)
                pe.wait_ge(tt.lo, 1 + b + 1)
                pe.wait_ge(hot_ready, b * 2 + 1)
                if isinstance(b, int) or True:
                    pe.wait_ge(wg_lo, 1)
                for t in range(TB):
                    mm = three_passes(pe, small[0:T, t * E:(t + 1) * E],
                                      lambda a, c: tt.xt[p][a][:, c, t * T:(t + 1) * T],
                                      lambda a, c: (wgh, wgl)[a][:, c, :])
                mm.then_inc(logit_ready, 1)

                def first_product(e):
                    k = e
                    pe.wait_ge(gelu_done, 1 + b * E + k - 1) if k >= 1 else pe.wait_ge(gelu_done, 1 + b * E)
                    three_passes(pe, hid_ps[e % 2][:, 0:S], lambda a, c: (w1h, w1l)[a][:, e, c, :],
                                 lambda a, c: tt.xt[p][a][:, c, :]).then_inc(hid_ready, 1)
                pe.wait_ge(w1_lo, E * C)
                first_product(0)
                first_product(1)
                pe.wait_ge(gate_step, b * STEPS + STEPS)
                for t in range(TB):
                    mm = pe.transpose(small[0:E, 64 + t * T:64 + (t + 1) * T], hot[:, t, :], tt.ident[0:T, 0:T])
                mm.then_inc(logit_ready, 1)
                for e in range(E):
                    if e >= 2:
                        first_product(e)
                    pe.wait_ge(hot_ready, b * 2 + 3)
                    pe.wait_ge(h_masked, 1 + b * E + e)
                    pe.matmul(mask_ps[:, 0:S], sel[:, e, :], hot_t[:, :], start=True, stop=True).then_inc(mask_ready, 1)
                pe.wait_ge(w2_lo, E)
                pe.wait_ge(y_added, 1 + b)
                for t in range(TB):
                    pe.matmul(y_ps[0:T, t, :], hot_t[:, t * T:(t + 1) * T], b2_sb[:, :], start=True, stop=False)
                for e in range(E):
                    pe.wait_ge(h_lo, b * E + (e + 1))
                    for t in range(TB):
                        for a, w in ((0, w2h), (0, w2l), (1, w2h)):
                            mm = pe.matmul(y_ps[0:T, t, :], hh[p][a][:, e, t * T:(t + 1) * T], w[:, e, :],
                                           start=False, stop=e == E - 1 and a == 1)
                mm.then_inc(y_ready, 1)
            batch_pairs(pe, body)

        @block.scalar
        def _(act):
            for e in range(E):
                for c in range(C):
                    act.wait_ge(w1_scaled, e * C + c + 1)
                act.activation(w1h[:, e, :, :], w1_sc[:, e % 2, :, :], ACT.Identity).then_inc(w1_hi, 1)
                act.wait_ge(w2_loaded[e % 2], 16 * (e // 2 + 1))
                act.activation(w2h[:, e, :], w2_raw[:, e % 2, :], ACT.Identity).then_inc(w2_hi, 1)
            act.wait_ge(consts, 80)
            act.activation(wgh[:, :, :], wg_sb[:, :, :], ACT.Identity).then_inc(wg_hi, 1)
            tt.act_hi(act, 0, 0)
            act.wait_ge(hot_ready, 1)

            def body(b, p, last):
                if not last:
                    act.wait_ge(y_ready, 1 + b)
                    tt.act_hi(act, b + 1, 1 - p)
                for e in range(E):
                    act.wait_ge(hid_ready, b * E + (e + 1))
                    if e >= 2:
                        act.wait_ge(h_masked, 1 + b * E + (e - 1))
                    else:
                        act.wait_ge(h_masked, 1 + b * E)
                    act.activation(hid[e % 2][:, :], hid_ps[e % 2][:, 0:S], ACT.Gelu,
                                   bias=b1f[:, e:e + 1]).then_inc(gelu_done, 1)
            batch_pairs(act, body)

        @block.vector
        def _(dve):
            ln.on_vector(dve, x)
            tt.dve_normalise(dve, x, 0, 0)
            dve.wait_ge(consts, 80)
            for e in range(E):
                dve.wait_ge(w1_loaded[e % 2], 16 * (e // 2 + 1))
                if e >= 2:
                    dve.wait_ge(w1_lo, C * (e - 1))
                for c in range(C):
                    dve.tensor_scalar(w1_sc[:, e % 2, c, :], w1_raw[:, e % 2, c, :], sc_sb[:, c, e:e + 1], None,
                                      ALU.mult).then_inc(w1_scaled, 1)
                dve.wait_ge(w1_hi, e + 1)
                dve.tensor_tensor(w1l[:, e, :, :], w1_sc[:, e % 2, :, :], f32(w1h[:, e, :, :]),
                                  ALU.subtract).then_inc(w1_lo, C)
                dve.wait_ge(w2_hi, e + 1)
                dve.tensor_tensor(w2l[:, e, :], w2_raw[:, e % 2, :], f32(w2h[:, e, :]), ALU.subtract).then_inc(w2_lo, 1)
            dve.wait_ge(wg_hi, 1)
            dve.tensor_tensor(wgl[:, :, :], wg_sb[:, :, :], f32(wgh[:, :, :]), ALU.subtract).then_inc(wg_lo, 1)
            dve.wait_ge(bias_ready, E)
            dve.tensor_tensor(b1f[:, :], small[:, 0:E], b1_sb[:, :], ALU.add).then_inc(hot_ready, 1)
            tt.dve_lo(dve, 0, 0)
            dve.wait_ge(sel_done, 2 + E)

            def body(b, p, last):
                if not last:
                    dve.wait_ge(y_ready, 1 + b)
                    tt.dve_normalise(dve, x, b + 1, 1 - p)
                    tt.dve_lo(dve, b + 1, 1 - p)
                done = 0

                def link(ins):
                    nonlocal done
                    ins.then_inc(gate_step, 1)
                    done += 1
                    dve.wait_ge(gate_step, b * STEPS + done)
                dve.wait_ge(logit_ready, b * 2 + 1)
                link(dve.tensor_copy(logit[:, :, :], small[0:T, 0:TB * E].rearrange("p (t e) -> p t e", t=TB)))
                link(dve.tensor_reduce(top[:, :], logit[:, :, :], AX.X, ALU.max))
                link(dve.tensor_tensor(is_top[:, :, :], logit[:, :, :],
                                       top[:, :].unsqueeze(2).to_broadcast([T, TB, E]), ALU.is_equal))
                link(dve.tensor_tensor(pick[:, :, :], is_top[:, :, :], rank[:, :, :], ALU.mult))
                link(dve.tensor_reduce(best[:, :], pick[:, :, :], AX.X, ALU.max))
                link(dve.tensor_tensor(hot[:, :, :], rank[:, :, :],
                                       best[:, :].unsqueeze(2).to_broadcast([T, TB, E]), ALU.is_equal))
                dve.wait_ge(logit_ready, b * 2 + 2)
                dve.wait_ge(y_ready, 1 + b)
                dve.tensor_copy(hot_t[:, :], small[0:E, 64:64 + S]).then_inc(hot_ready, 2)
                for e in range(E):
                    dve.wait_ge(gelu_done, 1 + b * E + (e + 1))
                    dve.wait_ge(mask_ready, b * E + (e + 1))
                    dve.tensor_tensor(hm[e % 2][:, :], mask_ps[:, 0:S], hid[e % 2][:, :], ALU.mult).then_inc(h_masked, 1)
                    dve.wait_ge(h_masked, 1 + b * E + (e + 1))
                    dve.tensor_copy(hh[p][0][:, e, :], hm[e % 2][:, :]).then_inc(h_hi, 1)
                    dve.wait_ge(h_hi, b * E + (e + 1))
                    dve.tensor_tensor(hh[p][1][:, e, :], hm[e % 2][:, :], f32(hh[p][0][:, e, :]),
                                      ALU.subtract).then_inc(h_lo, 1)
                dve.wait_ge(y_ready, 1 + b + 1)
                xb = x[:, bass.ds(b * TB, TB), :]
                dve.tensor_tensor(xb, y_ps[0:T, :, :], xb, ALU.add).then_inc(y_added, 1)
            batch_pairs(dve, body)


QMAX = 32767.0
MAGIC = 1.5 * 2.0 ** 23
MAGIC16 = 1.5 * 2.0 ** 7
WMAX = 7.0
WBLOCK = 32


def quantised_input(nc, x, x_scr, xq_hi, xq_lo, sx):
    with Phase(nc, "fq") as ph:
        ln = LayerNormStats(ph)
        xn = x
        am, am1, rs = ph.sb("am", [P, NT]), ph.sb("am1", [P, 4]), ph.sb("rs", [P, 1])
        qb, qi = ph.sb("qb", [T, 2, D]), ph.sb("qi", [T, 2, D])
        ident = ph.sb("ident", [P, P])
        ps = ph.ps("ps", [P, 2, 512])
        ident_done, norm, amax, scale = ph.sem("ident_done"), ph.sem("norm"), ph.sem("amax"), ph.sem("scale")
        biased, rounded = ph.sem("biased"), ph.sem("rounded")
        turned, hi_done, lo_done, x_stored = ph.sem("turned"), ph.sem("hi_done"), ph.sem("lo_done"), ph.sem("x_stored")
        block = ph.block()

        def view(ap, p):
            return ap[:, p, 0:C * T].rearrange("p (c s) -> p c s", c=C)

        @block.sync
        def _(sp):
            sp.dma_start(x_scr.rearrange("(n p) d -> p n d", p=T), x[:, :, :]).then_inc(x_stored, 16)
            sp.wait_ge(x_stored, 16)

        @block.gpsimd
        def _(pool):
            identity(pool, ident, ident_done)
            ln.on_pool(pool)
            pool.wait_ge(scale, 2)
            pool.partition_all_reduce(am1[:, 1:2], am1[:, 0:1], P, RMAX).then_inc(scale, 1)

        @block.vector
        def _(dve):
            dve.memset(am[:, :], 0.0).then_inc(scale, 1)
            ln.on_vector(dve, x)
            dve.wait_ge(scale, 1)
            dve.wait_ge(x_stored, 16)
            with dve.Fori(0, NT) as n:
                xt = xn[:, bass.ds(n, 1), :].rearrange("p a d -> p (a d)")
                ln.normalise(dve, xt, x, n).then_inc(norm, 1)
                dve.wait_ge(norm, n + 1)
                dve.tensor_reduce(am[0:T, bass.ds(n, 1)], xt, AX.X, ALU.max, apply_absolute_value=True).then_inc(amax, 1)
            dve.wait_ge(amax, NT)
            dve.tensor_reduce(am1[:, 0:1], am[:, :], AX.X, ALU.max).then_inc(scale, 1)
            dve.wait_ge(scale, 3)
            dve.tensor_scalar(sx, am1[:, 1:2], 1.0 / QMAX, 1e-12, ALU.mult, ALU.max).then_inc(scale, 1)
            dve.wait_ge(scale, 4)
            dve.reciprocal(rs[:, :], sx).then_inc(scale, 1)
            dve.wait_ge(scale, 5)
            with dve.Fori(0, NT // 2) as i:
                for p in range(2):
                    n = i * 2 + p
                    dve.tensor_scalar(qb[:, p, :], xn[:, bass.ds(n, 1), :].rearrange("p a d -> p (a d)"),
                                      rs[0:T, :], MAGIC, ALU.mult, ALU.add).then_inc(biased, 1)
                    dve.wait_ge(biased, n + 1)
                    dve.tensor_scalar(qi[:, p, :], qb[:, p, :], -MAGIC, None, ALU.add).then_inc(rounded, 1)
                    dve.wait_ge(hi_done, n + 1)
                    dve.tensor_tensor(xq_lo[:, :, bass.ds(n * T, T)], view(ps, p), f32(xq_hi[:, :, bass.ds(n * T, T)]),
                                      ALU.subtract).then_inc(lo_done, 1)

        @block.tensor
        def _(pe):
            pe.wait_ge(ident_done, 2)
            with pe.Fori(0, NT // 2) as i:
                for p in range(2):
                    n = i * 2 + p
                    pe.wait_ge(rounded, n + 1)
                    for c in range(C):
                        mm = pe.transpose(ps[:, p, c * T:(c + 1) * T], qi[:, p, c * P:(c + 1) * P], ident[0:T, 0:T])
                    mm.then_inc(turned, 1)

        @block.scalar
        def _(act):
            with act.Fori(0, NT // 2) as i:
                for p in range(2):
                    n = i * 2 + p
                    act.wait_ge(turned, n + 1)
                    act.activation(xq_hi[:, :, bass.ds(n * T, T)], view(ps, p), ACT.Identity).then_inc(hi_done, 1)


class WeightTiles:

    def __init__(self, ph):
        NB = D // WBLOCK
        self.raw = ph.sb("w_raw", [P, 2, D])
        self.bmax, self.bs, self.br = ph.sb("w_bmax", [P, NB]), ph.sb("w_bs", [P, NB]), ph.sb("w_br", [P, NB])
        self.q1, self.q2 = ph.sb("w_q1", [P, D]), ph.sb("w_q2", [P, D])
        self.deq = ph.sb("w_deq", [P, D])
        self.hi = [ph.sb(f"w_hi{i}", [P, C, P], F32R) for i in range(2)]
        self.lo = [ph.sb(f"w_lo{i}", [P, C, P], F32R) for i in range(2)]
        self.ps = ph.ps("w_ps", [P, C, P])
        self.loaded = ph.sems("w_loaded", 2)
        self.step = ph.sem("w_step")
        self.turned, self.hi_done = ph.sem("w_turned", start=1), ph.sem("w_hi_done")
        self.lo_done = ph.sem("w_lo_done", start=1)
    STEPS = 6

    def load(self, sp, src, n, p):
        sp.wait_ge(self.lo_done, 1 + n - p)
        sp.dma_start(self.raw[:, p, :], src).then_inc(self.loaded[p], 16)

    def dequantise(self, dve, n, half, p):
        def blocks(ap):
            return ap.rearrange("p (a w) -> p a w", w=WBLOCK)

        done = 0

        def link(ins):
            nonlocal done
            ins.then_inc(self.step, 1)
            done += 1
            dve.wait_ge(self.step, n * self.STEPS + done)

        wide = [P, D // WBLOCK, WBLOCK]
        dve.wait_ge(self.loaded[p], half * 16 + 16)
        link(dve.tensor_reduce(self.bmax[:, :], blocks(self.raw[:, p, :]), AX.X, ALU.max, apply_absolute_value=True))
        link(dve.tensor_scalar(self.bs[:, :], self.bmax[:, :], 1.0 / WMAX, 1e-12, ALU.mult, ALU.max))
        link(dve.reciprocal(self.br[:, :], self.bs[:, :]))
        link(dve.tensor_tensor(blocks(self.q1[:, :]), blocks(self.raw[:, p, :]),
                               self.br[:, :].unsqueeze(2).to_broadcast(wide), ALU.mult))
        link(dve.tensor_scalar(self.q2[:, :], self.q1[:, :], MAGIC, -MAGIC, ALU.add, ALU.add))
        dve.wait_ge(self.turned, 1 + n)
        dve.tensor_tensor(blocks(self.deq[:, :]), blocks(self.q2[:, :]),
                          self.bs[:, :].unsqueeze(2).to_broadcast(wide), ALU.mult).then_inc(self.step, 1)

    def transpose(self, pe, n, ident):
        pe.wait_ge(self.step, n * self.STEPS + self.STEPS)
        pe.wait_ge(self.lo_done, 1 + n)
        for c in range(C):
            mm = pe.transpose(self.ps[:, c, :], self.deq[:, c * P:(c + 1) * P], ident[:, :])
        mm.then_inc(self.turned, 1)

    def split_hi(self, act, n, p):
        act.wait_ge(self.turned, 1 + n + 1)
        act.activation(self.hi[p][:, :, :], self.ps[:, :, :], ACT.Identity).then_inc(self.hi_done, 1)

    def split_lo(self, dve, n, p):
        dve.wait_ge(self.hi_done, n + 1)
        dve.tensor_tensor(self.lo[p][:, :, :], self.ps[:, :, :], f32(self.hi[p][:, :, :]),
                          ALU.subtract).then_inc(self.lo_done, 1)


def up_and_gate(nc, w_up, w_gate, w_down, xq_hi, xq_lo, sx, gate, umax, gmax, up_scr, down_scr):
    NTOK = B * S
    NG, GT = 4, NTOK // 4
    JD = 12
    with Phase(nc, "ug") as ph:
        w = WeightTiles(ph)
        ust = [ph.sb(f"ust{p}", [P, NTOK]) for p in range(2)]
        ident = ph.sb("ident", [P, P])
        ps = ph.ps("ps", [P, 4, 512])
        ident_done, product, kept, amax = ph.sem("ident_done"), ph.sem("product"), ph.sem("kept"), ph.sem("amax", start=1)
        u_stored, d_stored = ph.sems("u_stored", 2, start=1), ph.sems("d_stored", 2)
        credit = ph.sb("credit", [P, 2])
        block = ph.block()

        def source(ap, n):
            return ap[bass.ds(n * P, P), :]

        def store_down(sp, m):
            o, i = m // 3, m % 3
            sp.wait_ge(w.lo_done, 1 + 2 * FI + m + 1)
            for part, t in enumerate((w.hi, w.lo)):
                sp.dma_start(down_scr[part, :, i * C:(i + 1) * C, o * P:(o + 1) * P],
                             f32(t[m % 2][:, :, :])).then_inc(d_stored[m % 2], 16)

        @block.sync
        def _(sp):
            for k, ap in enumerate((w_up, w_gate)):
                with sp.Fori(0, FI // 2) as i:
                    for p in range(2):
                        w.load(sp, source(ap, i * 2 + p), i * 2 + (k * FI + p), p)
            for m in range(JD):
                n = 2 * FI + m
                o, i = m // 3, m % 3
                w.load(sp, w_down[o * P:(o + 1) * P, i * D:(i + 1) * D], n, m % 2)
                if m >= 1:
                    store_down(sp, m - 1)
            store_down(sp, JD - 1)
            for p in range(2):
                sp.wait_ge(u_stored[p], 1 + 16 * FI // 2)
                sp.wait_ge(d_stored[p], 32 * JD // 2)

        @block.gpsimd
        def _(pool):
            identity(pool, ident, ident_done)

        @block.tensor
        def _(pe):
            pe.wait_ge(ident_done, 2)
            w.transpose(pe, 0, ident)
            with pe.Fori(0, FI) as i:
                for p in range(2):
                    n = i * 2 + p
                    pe.wait_ge(w.lo_done, 1 + n + 1)
                    for t in range(NG):
                        if t == NG // 2:
                            w.transpose(pe, n + 1, ident)
                        pe.wait_ge(kept, n * NG + (t + 1))
                        tok = slice(t * GT, (t + 1) * GT)
                        three_passes(pe, ps[:, t, 0:GT], lambda a, c: (w.hi, w.lo)[a][p][:, c, :],
                                     lambda a, c: (xq_hi, xq_lo)[a][:, c, tok]).then_inc(product, 1)
            for m in range(1, JD):
                w.transpose(pe, 2 * FI + m, ident)

        @block.scalar
        def _(act):
            w.split_hi(act, 0, 0)
            for k in range(2):
                with act.Fori(0, FI // 2) as i:
                    for p in range(2):
                        j = i * 2 + p
                        n = j + k * FI
                        if k == 0:
                            act.wait_ge(u_stored[p], 1 + i * 16)
                            act.wait_ge(amax, 1 + n * NG)
                        for t in range(NG):
                            if t == NG // 2:
                                w.split_hi(act, n + 1, 1 - p)
                            act.wait_ge(product, n * NG + (t + 1))
                            out = (ust[p][:, t * GT:(t + 1) * GT] if k == 0 else
                                   gate[:, bass.ds(j, 1), t * GT:(t + 1) * GT].rearrange("p a s -> p (a s)"))
                            act.activation(out, ps[:, t, 0:GT], ACT.Copy, scale=sx).then_inc(kept, 1)
                        if k == 0:
                            act.wait_ge(kept, n * NG + 2 * NG)
                            act.dma_start(up_scr[bass.ds(j, 1)].rearrange("a p s -> p (a s)"),
                                          ust[p][:, :]).then_inc(u_stored[p], 16)
            for m in range(1, JD):
                if m >= 2:
                    act.wait_ge(d_stored[m % 2], 32 * (m // 2))
                else:
                    act.wait_ge(product, 2 * FI * NG)
                w.split_hi(act, 2 * FI + m, m % 2)

        @block.vector
        def _(dve):
            dve.memset(credit[:, 0:1], 0.0).then_inc(kept, NG)
            dve.memset(credit[:, 1:2], 0.0).then_inc(amax, NG)
            w.dequantise(dve, 0, 0, 0)
            w.split_lo(dve, 0, 0)
            for k in range(2):
                with dve.Fori(0, FI // 2) as i:
                    for p in range(2):
                        j = i * 2 + p
                        n = j + k * FI
                        w.dequantise(dve, n + 1, i + (k * FI // 2 + p), 1 - p)
                        for t in range(NG):
                            if t == NG // 2:
                                w.split_lo(dve, n + 1, 1 - p)
                            dve.wait_ge(kept, n * NG + (NG + t + 1))
                            val = (ust[p][:, t * GT:(t + 1) * GT] if k == 0 else
                                   gate[:, bass.ds(j, 1), t * GT:(t + 1) * GT].rearrange("p a s -> p (a s)"))
                            dve.tensor_reduce((umax, gmax)[k][:, bass.ds(j * NG + t, 1)], val, AX.X,
                                              ALU.max, apply_absolute_value=True).then_inc(amax, 1)
            for m in range(1, JD):
                w.dequantise(dve, 2 * FI + m, FI + m // 2, m % 2)
                w.split_lo(dve, 2 * FI + m, m % 2)


def scale_of(link, dve, amax, unit, scale, inverse, tmp):
    if unit is None:
        link(dve.tensor_scalar(scale, amax, 1.0 / QMAX, 1e-12, ALU.mult, ALU.max))
        link(dve.reciprocal(inverse, scale))
    else:
        link(dve.tensor_scalar(tmp, amax, unit, 1.0 / QMAX, ALU.mult, ALU.mult))
        link(dve.tensor_scalar(scale, tmp, 1e-12, None, ALU.max))
        link(dve.reciprocal(tmp, scale))
        link(dve.tensor_tensor(inverse, tmp, unit, ALU.mult))


def activation_and_down(nc, x_scr, up_scr, down_scr, gate, umax, gmax, sx, out):
    NTOK = B * S
    NH, HT = 2, NTOK // 2
    HTT = HT // T
    with Phase(nc, "ad") as ph:
        wd = [ph.sb(f"wd{x_}", [P, FI, D], F32R) for x_ in "hl"]
        ust = [ph.sb(f"ust{p}", [P, NTOK]) for p in range(2)]
        sig = [ph.sb(f"sig{p}", [P, NTOK]) for p in range(2)]
        am = ph.sb("am", [P, 8])
        sc = ph.sb("sc", [P, 16])
        jmax, jmax2 = ph.sb("jmax", [P, FI]), ph.sb("jmax2", [P, FI])
        bias = ph.sb("bias", [P, 2])
        oh = [ph.sb(f"oh{p}", [P, HT], F32R) for p in range(2)]
        ol = [ph.sb(f"ol{p}", [P, HT], F32R) for p in range(2)]
        xt, yt = ph.sb("xt", [T, 2, D]), ph.sb("yt", [T, 2, D])
        ps = ph.ps("ps", [P, HTT, 512])
        wd_loaded, u_loaded = ph.sem("wd_loaded"), ph.sems("u_loaded", 2)
        st, reduced = ph.sem("st"), ph.sem("reduced")
        passed = ph.sem("passed")
        g_biased, g_round, sig_done, sig_round, silu, silu_max = (ph.sem(n) for n in (
            "g_biased", "g_round", "sig_done", "sig_round", "silu", "silu_max"))
        s_biased, u_biased, o_min, prod, prod_max = (ph.sem(n) for n in (
            "s_biased", "u_biased", "o_min", "prod", "prod_max"))
        o_biased, o_round, o_hi, o_lo, mm_done = (ph.sem(n) for n in ("o_biased", "o_round", "o_hi", "o_lo", "mm_done"))
        x_loaded, y_done, y_stored = ph.sems("x_loaded", 2), ph.sem("y_done"), ph.sems("y_stored", 2)
        SILU_ST = 3 + 2 + 2 + 1
        PROD_ST = SILU_ST + 4 + 1 + 1
        credit = ph.sb("credit", [P, 4])
        block = ph.block()
        su, ru, sg, rg, ss, rs, us, so, ro, t0 = (sc[:, i:i + 1] for i in range(10))

        def tile(ap, j):
            return ap[:, bass.ds(j, 1), :].rearrange("p a s -> p (a s)")

        @block.sync
        def _(sp):
            sp.dma_start(f32(wd[0][:, :, :]), down_scr[0]).then_inc(wd_loaded, 16)
            sp.dma_start(f32(wd[1][:, :, :]), down_scr[1]).then_inc(wd_loaded, 16)
            with sp.Fori(0, FI // 2) as i:
                for p in range(2):
                    sp.wait_ge(prod, 1 + i * 2 + p)
                    sp.dma_start(ust[p][:, :], up_scr[bass.ds(i * 2 + p, 1)].rearrange(
                        "a p s -> p (a s)")).then_inc(u_loaded[p], 16)
            for n in range(2 * HTT):
                if n >= 2:
                    sp.wait_ge(y_done, n - 1)
                sp.dma_start(xt[:, n % 2, :], x_scr[n * T:(n + 1) * T, :]).then_inc(x_loaded[n % 2], 16)
                if n >= 1:
                    sp.wait_ge(y_done, n)
                    sp.dma_start(out[(n - 1) * T:n * T, :], yt[:, (n - 1) % 2, :]).then_inc(y_stored[(n - 1) % 2], 16)
            n = 2 * HTT
            sp.wait_ge(y_done, n)
            sp.dma_start(out[(n - 1) * T:n * T, :], yt[:, (n - 1) % 2, :]).then_inc(y_stored[(n - 1) % 2], 16)
            for p in range(2):
                sp.wait_ge(y_stored[p], 16 * HTT)

        @block.gpsimd
        def _(pool):
            for k, made in enumerate((2, 3, SILU_ST, PROD_ST)):
                pool.wait_ge(st, made)
                pool.partition_all_reduce(am[:, 4 + k:5 + k], am[:, k:k + 1], P, RMAX).then_inc(reduced, 1)
                if k < 3:
                    pool.wait_ge(reduced, k + 1)

        @block.scalar
        def _(act):
            act.wait_ge(st, SILU_ST - 1)
            with act.Fori(0, FI // 2) as i:
                for p in range(2):
                    j = i * 2 + p
                    act.activation(tile(gate, j), tile(gate, j), ACT.Identity, bias=bias[:, 0:1],
                                   scale=rg).then_inc(g_biased, 1)
                    act.wait_ge(g_round, j + 1)
                    act.wait_ge(silu, 1 + j)
                    act.sem_inc(passed, 1)
                    act.activation(sig[p][:, :], tile(gate, j), ACT.Sigmoid, scale=sg).then_inc(sig_done, 1)
            act.wait_ge(st, PROD_ST - 1)
            with act.Fori(0, FI // 2) as i:
                for p in range(2):
                    j = i * 2 + p
                    act.wait_ge(u_loaded[p], i * 16 + 16)
                    act.activation(ust[p][:, :], ust[p][:, :], ACT.Identity, bias=bias[:, 0:1],
                                   scale=ru).then_inc(u_biased, 1)
                    act.activation(tile(gate, j), tile(gate, j), ACT.Identity, bias=bias[:, 0:1],
                                   scale=rs).then_inc(s_biased, 1)
            for h in range(NH):
                with act.Fori(0, FI // 2) as i:
                    for p in range(2):
                        j = i * 2 + p
                        k = j + h * FI
                        act.wait_ge(o_round, k + 1)
                        act.wait_ge(mm_done, 1 + k)
                        act.activation(oh[p][:, :], gate[:, bass.ds(j, 1), h * HT:(h + 1) * HT].rearrange(
                            "p a s -> p (a s)"), ACT.Identity).then_inc(o_hi, 1)

        @block.vector
        def _(dve):
            count = [0]

            def link(ins):
                ins.then_inc(st, 1)
                count[0] += 1
                dve.wait_ge(st, count[0])

            dve.memset(credit[:, 0:1], 0.0).then_inc(silu, 2)
            dve.memset(credit[:, 1:2], 0.0).then_inc(prod, 2)
            dve.memset(credit[:, 2:3], 0.0).then_inc(mm_done, 2)
            link(dve.memset(bias[:, :], MAGIC))
            link(dve.tensor_reduce(am[:, 0:1], umax, AX.X, ALU.max))
            link(dve.tensor_reduce(am[:, 1:2], gmax, AX.X, ALU.max))
            dve.wait_ge(reduced, 2)
            scale_of(link, dve, am[:, 4:5], None, su, ru, t0)
            scale_of(link, dve, am[:, 5:6], None, sg, rg, t0)
            assert count[0] == SILU_ST - 1
            with dve.Fori(0, FI // 2) as i:
                for p in range(2):
                    j = i * 2 + p
                    dve.wait_ge(g_biased, j + 1)
                    dve.tensor_scalar(tile(gate, j), tile(gate, j), -MAGIC, None, ALU.add).then_inc(g_round, 1)
                    dve.wait_ge(sig_done, j + 1)
                    dve.tensor_scalar(sig[p][:, :], sig[p][:, :], 65535.0 / 65536.0, MAGIC16,
                                      ALU.min, ALU.add).then_inc(sig_round, 1)
                    dve.wait_ge(sig_round, j + 1)
                    dve.scalar_tensor_tensor(tile(gate, j), sig[p][:, :], MAGIC16, tile(gate, j),
                                             ALU.subtract, ALU.mult).then_inc(silu, 1)
                    dve.wait_ge(silu, 1 + j + 2)
                    dve.tensor_reduce(jmax[:, bass.ds(j, 1)], tile(gate, j), AX.X, ALU.max,
                                      apply_absolute_value=True).then_inc(silu_max, 1)
            dve.wait_ge(silu_max, FI)
            link(dve.tensor_reduce(am[:, 2:3], jmax[:, :], AX.X, ALU.max))
            dve.wait_ge(reduced, 3)
            scale_of(link, dve, am[:, 6:7], sg, ss, rs, t0)
            link(dve.tensor_tensor(us, ss, su, ALU.mult))
            assert count[0] == PROD_ST - 1
            with dve.Fori(0, FI // 2) as i:
                for p in range(2):
                    j = i * 2 + p
                    dve.wait_ge(u_biased, j + 1)
                    dve.tensor_scalar(ust[p][:, :], ust[p][:, :], -MAGIC, None, ALU.add).then_inc(o_min, 1)
                    dve.wait_ge(s_biased, j + 1)
                    dve.wait_ge(o_min, j + 1)
                    dve.scalar_tensor_tensor(tile(gate, j), tile(gate, j), MAGIC, ust[p][:, :],
                                             ALU.subtract, ALU.mult).then_inc(prod, 1)
                    dve.wait_ge(prod, 1 + j + 2)
                    dve.tensor_reduce(jmax2[:, bass.ds(j, 1)], tile(gate, j), AX.X, ALU.max,
                                      apply_absolute_value=True).then_inc(prod_max, 1)
            dve.wait_ge(prod_max, FI)
            link(dve.tensor_reduce(am[:, 3:4], jmax2[:, :], AX.X, ALU.max))
            dve.wait_ge(reduced, 4)
            scale_of(link, dve, am[:, 7:8], us, so, ro, t0)
            for h in range(NH):
                with dve.Fori(0, FI // 2) as i:
                    for p in range(2):
                        j = i * 2 + p
                        k = j + h * FI
                        o = gate[:, bass.ds(j, 1), h * HT:(h + 1) * HT].rearrange("p a s -> p (a s)")
                        dve.tensor_scalar(o, o, ro, MAGIC, ALU.mult, ALU.add).then_inc(o_biased, 1)
                        dve.wait_ge(o_biased, k + 1)
                        dve.tensor_scalar(o, o, -MAGIC, None, ALU.add).then_inc(o_round, 1)
                        dve.wait_ge(o_hi, k + 1)
                        dve.tensor_tensor(ol[p][:, :], o, f32(oh[p][:, :]), ALU.subtract).then_inc(o_lo, 1)
                dve.wait_ge(mm_done, 1 + h * FI + (FI + 1))
                for t in range(HTT):
                    n = h * HTT + t
                    dve.wait_ge(x_loaded[n % 2], 16 * (n // 2 + 1))
                    if n >= 2:
                        dve.wait_ge(y_stored[n % 2], 16 * (n // 2))
                    dve.scalar_tensor_tensor(yt[:, n % 2, :], ps[0:T, t, :], so[0:T, :], xt[:, n % 2, :],
                                             ALU.mult, ALU.add).then_inc(y_done, 1)

        @block.tensor
        def _(pe):
            pe.wait_ge(wd_loaded, 32)
            for h in range(NH):
                if h:
                    pe.wait_ge(y_done, h * HTT)
                def tile_products(j, p, first, last):
                    pe.wait_ge(o_lo, j + (h * FI + 1))
                    for t in range(HTT):
                        tok = slice(t * T, (t + 1) * T)
                        for n, (a, b) in enumerate(((oh, 0), (oh, 1), (ol, 0))):
                            mm = pe.matmul(ps[0:T, t, :], a[p][:, tok], tile(wd[b], j),
                                           start=first and n == 0, stop=last and n == 2)
                    mm.then_inc(mm_done, 1)

                tile_products(0, 0, True, False)
                tile_products(1, 1, False, False)
                with pe.Fori(1, FI // 2 - 1) as i:
                    for p in range(2):
                        tile_products(i * 2 + p, p, False, False)
                tile_products(FI - 2, 0, False, False)
                tile_products(FI - 1, 1, False, True)


def quantised_ffn(nc, x_stack, x, w_up, w_gate, w_down, x_scr, up_scr, down_scr, out):
    NTOK = B * S
    with Phase(nc, "ff") as outer:
        sx = outer.sb("sx", [P, 1])[:, :]
        umax, gmax = outer.sb("umax", [P, FI * 4])[:, :], outer.sb("gmax", [P, FI * 4])[:, :]
        with Phase(nc, "xq") as ph:
            xq_hi, xq_lo = ph.sb("hi", [P, C, NTOK], F32R), ph.sb("lo", [P, C, NTOK], F32R)
            quantised_input(nc, x, x_scr, xq_hi, xq_lo, sx)
            x_stack.close()
            gate = x_stack.enter_context(nc.sbuf_tensor("gate", [P, FI, NTOK], F32, side="right"))
            up_and_gate(nc, w_up, w_gate, w_down, xq_hi, xq_lo, sx, gate, umax, gmax, up_scr, down_scr)
        activation_and_down(nc, x_scr, up_scr, down_scr, gate, umax, gmax, sx, out)
        x_stack.close()


def build(nc, x, ctx_t, mask, mask_t, keypad, keypad_t, wq0, bq0, wk0, wv0, wo0, bo0, wgate, ln_scale, ln_bias,
          w1, b1, w2, b2, wq1, wk1, wv1, bqk1, bv1, wka1, wva1, wo1, bo1, g, bk_ctx, bv_ctx,
          w_gate, w_up, w_down, out):
    def scratch(name, *shape):
        return nc.dram_tensor(name, shape, F32).ap()

    k_ctx, v_ctx = scratch("k_ctx", 2, 2, B, D, S2), scratch("v_ctx", 2, B, S2, VW)
    q0, qk1 = scratch("q0", 1, 2, D, B * S), scratch("qk1", 2, 2, D, B * S)
    v_self = scratch("v_self", B * S, VW)
    x_scr = scratch("x_scr", B * S, D)
    up_scr, down_scr = scratch("up_scr", FI, P, B * S), scratch("down_scr", 2, P, FI, D)

    def ctx_source(layer):
        return (S2, lambda b, part: k_ctx[layer, part, bass.ds(b, 1)].rearrange("b n k -> (b n) k"),
                lambda b: v_ctx[layer, bass.ds(b, 1)].rearrange("b k n -> (b k) n"))

    self_source = (S, lambda b, part: qk1[1, part][:, bass.ds(b * S, S)],
                   lambda b: v_self[bass.ds(b * S, S), :])

    ctx_projections(nc, ctx_t, [wk0, wv0, wka1, wva1], bk_ctx, bv_ctx, k_ctx, v_ctx)
    x_stack = ExitStack()
    xr = x_stack.enter_context(nc.sbuf_tensor("x_res", [T, NT, D], F32, side="right"))
    token_projections(nc, "q0", xr, x, [wq0], bq0, None, q0, None)
    attention(nc, "a0", xr, q0[0], [ctx_source(0)], wo0, bo0, masks=(mask, mask_t, keypad, keypad_t))
    experts(nc, xr, wgate, ln_scale, ln_bias, w1, b1, w2, b2)
    token_projections(nc, "q1", xr, None, [wq1, wk1, wv1], bqk1, bv1, qk1, v_self)
    attention(nc, "a1", xr, qk1[0], [self_source, ctx_source(1)], wo1, bo1, gates=g)
    quantised_ffn(nc, x_stack, xr, w_up, w_gate, w_down, x_scr, up_scr, down_scr, out)


def kernel(**inputs):
    import numpy as np
    import concourse.bacc as bacc
    from concourse.bass_utils import run_bass_kernel_spmd

    a = {name: np.asarray(value) for name, value in inputs.items()}

    def chunks(w):
        return w.reshape(w.shape[0] // 128, 128, -1).transpose(1, 0, 2)

    def per_partition(b, n):
        return b.reshape(n, 4, 128).transpose(2, 0, 1)

    def spread(b, rows):
        return np.broadcast_to(b, (rows,) + b.shape)

    Bs, Ss, Dm = a["x"].shape
    keys = a["ctx_1024"].shape[1]
    padded = -(-keys // 128) * 128
    mask = a["mask_BxSxS2_bf0"]
    keypad = a["mask_BxS2_bf0"]
    keypad_t = np.zeros((Bs, padded), bool)
    keypad_t[:, :keys] = keypad
    w_self, b_self = a["L1_xattn_Wqkv"], a["L1_xattn_bqkv"]
    w_aux, b_aux = a["L1_xattn_Wqkv_aux"], a["L1_xattn_bqkv_aux"]
    laid = [
        a["x"].reshape(Bs * Ss, Dm),
        a["ctx_1024"].transpose(0, 2, 1).reshape(Bs, Dm // 128, 128, keys).transpose(0, 2, 1, 3),
        mask, mask.transpose(0, 2, 1), keypad, keypad_t.reshape(Bs, padded // 128, 128).transpose(2, 0, 1),
        chunks(a["L0_xattn_Wq"].T), per_partition(a["L0_xattn_bq"], 1),
        chunks(a["L0_xattn_Wk"].T), chunks(a["L0_xattn_Wv"].T),
        chunks(a["L0_xattn_Wo"].T), spread(a["L0_xattn_bo"], 112),
        chunks(a["L0_ffn_Wg"].T), chunks(a["L0_ffn_ln_scale"].T), chunks(a["L0_ffn_ln_bias"].T),
        a["L0_ffn_W1"].reshape(8, 4, 128, 128).transpose(2, 0, 1, 3), a["L0_ffn_b1"].T,
        a["L0_ffn_W2"].transpose(1, 0, 2), a["L0_ffn_b2"],
        chunks(w_self[:, :Dm]), chunks(w_self[:, Dm:2 * Dm]), chunks(w_self[:, 2 * Dm:]),
        per_partition(b_self[:2 * Dm], 2), spread(b_self[2 * Dm:], 128),
        chunks(w_aux[:, Dm:2 * Dm]), chunks(w_aux[:, 2 * Dm:]),
        chunks(a["L1_xattn_Wo"]), spread(a["L1_xattn_bo"], 112), spread(a["L1_xattn_g"], 128),
        per_partition(np.concatenate([a["L0_xattn_bk"], b_aux[Dm:2 * Dm]]), 2),
        spread(np.stack([a["L0_xattn_bv"], b_aux[2 * Dm:]]), 128),
        a["L1_ffn_w_gate"], a["L1_ffn_w_up"], a["L1_ffn_w_down"],
    ]
    nc = bacc.Bacc("TRN2", target_bir_lowering=False, num_devices=1)
    arrays, args = {}, []
    for i, array in enumerate(laid):
        array = np.ascontiguousarray(array)
        arrays[f"in_{i}"] = array
        args.append(nc.dram_tensor(f"in_{i}", array.shape, mybir.dt.from_np(array.dtype),
                                   kind="ExternalInput").ap())
    out = nc.dram_tensor("out", (Bs * Ss, Dm), F32, kind="ExternalOutput").ap()
    build(nc, *args, out)
    result = run_bass_kernel_spmd(nc, [arrays], core_ids=[0])
    return result.results[0]["out"].reshape(Bs, Ss, Dm)
```
